# Optimizing a Trainium2 kernel written in Bass

```python
import numpy as np
import jax
import jax.numpy as jnp

def _softmax(x, axis=-1):
    return jax.nn.softmax(x, axis=axis)

def _gelu(x):
    return jax.nn.gelu(x, approximate=True)

def _silu(x):
    return jax.nn.silu(x)

def _sigmoid(x):
    return jax.nn.sigmoid(x)

def _layernorm(x, axis=-1, eps=1e-05):
    m = jnp.mean(x, axis=axis, keepdims=True)
    v = jnp.var(x, axis=axis, keepdims=True)
    return (x - m) / jnp.sqrt(v + eps)

def _scatter_add(tgt, idx, src, axis=0):
    return tgt.at[idx].add(src)

def _segment_sum(src, seg, n):
    return jax.ops.segment_sum(src, seg, n)
kernel_name = 'mk_gnn_resnorm_d2_gnn_r64_d1cb81'

def setup_inputs(seed: int=0):
    np.random.seed(seed)
    _w = jnp.asarray

    def _rec_inputs():
        import jax
        import jax.numpy as jnp
        _gk = jax.random.key(seed)
        x = -0.0005121 + 1.001 * jax.random.normal(jax.random.fold_in(_gk, 1), (100000, 32), jnp.float32)
        src = jax.random.randint(jax.random.fold_in(_gk, 2), (25000,), 0, 100000, jnp.int32)
        dst = jax.random.randint(jax.random.fold_in(_gk, 3), (25000,), 0, 100000, jnp.int32)
        _o = jnp.argsort(dst, stable=True)
        src = src[_o]
        dst = dst[_o]
        edge_attr_16 = 0.000312547 + 1.00004 * jax.random.normal(jax.random.fold_in(_gk, 11), (25000, 16), jnp.float32)
        return (x, src, dst, edge_attr_16)
    x, src, dst, edge_attr_16 = _rec_inputs()

    def _L0_gnn_setup():
        import jax, jax.numpy as jnp
        import numpy as np
        N_NODES = 100000
        N_EDGES = 15625
        IN_CH = 32
        EDGE_CH = 16
        OUT_CH = 32
        D_CAT = 2 * IN_CH + EDGE_CH
        D_MID = 56
        key = jax.random.key(seed)
        ks = jax.random.split(key, 8)
        x = jax.random.normal(ks[0], (N_NODES, IN_CH), dtype=jnp.float32)
        edge_index = jax.random.randint(ks[1], (2, N_EDGES), 0, N_NODES, dtype=jnp.int64)
        edge_attr = jax.random.normal(ks[2], (N_EDGES, EDGE_CH), dtype=jnp.float32)
        W1 = jax.random.normal(ks[3], (D_CAT, D_MID), dtype=jnp.float32) / np.sqrt(D_CAT).astype(np.float32)
        b1 = jnp.zeros((D_MID,), dtype=jnp.float32)
        W2 = jax.random.normal(ks[4], (D_MID, OUT_CH), dtype=jnp.float32) / np.sqrt(D_MID).astype(np.float32)
        b2 = jnp.zeros((OUT_CH,), dtype=jnp.float32)
        return {'x': x, 'edge_index': edge_index, 'edge_attr': edge_attr, 'W1': W1, 'b1': b1, 'W2': W2, 'b2': b2}
    _L0_gnn_all = _L0_gnn_setup()
    _L0_gnn_in = {k: v for k, v in _L0_gnn_all.items() if k in ('W1', 'b1', 'W2', 'b2')}
    del _L0_gnn_all

    def _L1_gnn_setup():
        import jax, jax.numpy as jnp
        import numpy as np
        N_ATOMS = 100000
        N_EDGES = 300000
        ATOM_DIM = 32
        BOND_DIM = 16
        STEPS = 4

        def _gru_cell(x, h, W_ih, W_hh, b_ih, b_hh):
            gi = x @ W_ih.T + b_ih
            gh = h @ W_hh.T + b_hh
            i_r, i_z, i_n = jnp.split(gi, 3, axis=-1)
            h_r, h_z, h_n = jnp.split(gh, 3, axis=-1)
            r = jax.nn.sigmoid(i_r + h_r)
            z = jax.nn.sigmoid(i_z + h_z)
            n = jnp.tanh(i_n + r * h_n)
            return (1.0 - z) * n + z * h
        key = jax.random.key(seed)
        ks = jax.random.split(key, 8)
        atom_features = jax.random.normal(ks[0], (N_ATOMS, ATOM_DIM), dtype=jnp.float32)
        bond_features = jax.random.normal(ks[1], (N_EDGES, BOND_DIM), dtype=jnp.float32)
        pair_indices = jax.random.randint(ks[2], (N_EDGES, 2), 0, N_ATOMS, dtype=jnp.int64 if jax.config.jax_enable_x64 else jnp.int32)
        W_bond = jax.random.normal(ks[3], (BOND_DIM, ATOM_DIM * ATOM_DIM), dtype=jnp.float32) * 0.05
        b_bond = jnp.zeros((ATOM_DIM * ATOM_DIM,), dtype=jnp.float32)
        W_ih = jax.random.normal(ks[4], (3 * ATOM_DIM, ATOM_DIM), dtype=jnp.float32) * 0.1
        W_hh = jax.random.normal(ks[5], (3 * ATOM_DIM, ATOM_DIM), dtype=jnp.float32) * 0.1
        b_ih = jnp.zeros((3 * ATOM_DIM,), dtype=jnp.float32)
        b_hh = jnp.zeros((3 * ATOM_DIM,), dtype=jnp.float32)
        return {'atom_features': atom_features, 'bond_features': bond_features, 'pair_indices': pair_indices, 'W_bond': W_bond, 'b_bond': b_bond, 'W_ih': W_ih, 'W_hh': W_hh, 'b_ih': b_ih, 'b_hh': b_hh}
    _L1_gnn_all = _L1_gnn_setup()
    _L1_gnn_in = {k: v for k, v in _L1_gnn_all.items() if k in ('W_bond', 'b_bond', 'W_ih', 'W_hh', 'b_ih', 'b_hh')}
    del _L1_gnn_all
    return {'x': x, 'src': src, 'dst': dst, 'edge_attr_16': edge_attr_16, 'L0_gnn_W1': _L0_gnn_in['W1'], 'L0_gnn_b1': _L0_gnn_in['b1'], 'L0_gnn_W2': _L0_gnn_in['W2'], 'L0_gnn_b2': _L0_gnn_in['b2'], 'L1_gnn_W_bond': _L1_gnn_in['W_bond'], 'L1_gnn_b_bond': _L1_gnn_in['b_bond'], 'L1_gnn_W_ih': _L1_gnn_in['W_ih'], 'L1_gnn_W_hh': _L1_gnn_in['W_hh'], 'L1_gnn_b_ih': _L1_gnn_in['b_ih'], 'L1_gnn_b_hh': _L1_gnn_in['b_hh']}

def reference(x, src, dst, edge_attr_16, L0_gnn_W1, L0_gnn_b1, L0_gnn_W2, L0_gnn_b2, L1_gnn_W_bond, L1_gnn_b_bond, L1_gnn_W_ih, L1_gnn_W_hh, L1_gnn_b_ih, L1_gnn_b_hh):
    import jax
    import jax.numpy as jnp

    def _L0_gnn_ref(x, edge_index, edge_attr, W1, b1, W2, b2):
        import jax, jax.numpy as jnp
        import numpy as np
        N_NODES = 100000
        N_EDGES = 15625
        IN_CH = 32
        EDGE_CH = 16
        OUT_CH = 32
        D_CAT = 2 * IN_CH + EDGE_CH
        D_MID = 56
        num_nodes = x.shape[0]
        rol, col = (edge_index[0], edge_index[1])
        e = jnp.concatenate([x[rol], x[col], edge_attr], axis=-1)
        h = jax.nn.leaky_relu(e @ W1 + b1)
        v = jax.nn.leaky_relu(h @ W2 + b2)
        agg = jax.ops.segment_max(v, col, num_segments=num_nodes)
        agg = jnp.where(jnp.isneginf(agg), jnp.zeros((), dtype=agg.dtype), agg)
        out = jnp.maximum(agg, x[:, -v.shape[-1]:])
        return out

    def _L1_gnn_ref(atom_features, bond_features, pair_indices, W_bond, b_bond, W_ih, W_hh, b_ih, b_hh):
        import jax, jax.numpy as jnp
        import numpy as np
        N_ATOMS = 100000
        N_EDGES = 300000
        ATOM_DIM = 32
        BOND_DIM = 16
        STEPS = 4

        def _gru_cell(x, h, W_ih, W_hh, b_ih, b_hh):
            gi = x @ W_ih.T + b_ih
            gh = h @ W_hh.T + b_hh
            i_r, i_z, i_n = jnp.split(gi, 3, axis=-1)
            h_r, h_z, h_n = jnp.split(gh, 3, axis=-1)
            r = jax.nn.sigmoid(i_r + h_r)
            z = jax.nn.sigmoid(i_z + h_z)
            n = jnp.tanh(i_n + r * h_n)
            return (1.0 - z) * n + z * h
        n_atoms, d = atom_features.shape
        edge_mats = (bond_features @ W_bond + b_bond).reshape(-1, d, d)
        dst = pair_indices[:, 0]
        nbr = pair_indices[:, 1]
        h = atom_features
        for _ in range(STEPS):
            msg = jnp.einsum('eij,ej->ei', edge_mats, h[nbr])
            agg = jax.ops.segment_sum(msg, dst, num_segments=n_atoms)
            h = _gru_cell(agg, h, W_ih, W_hh, b_ih, b_hh)
        return h
    edge_index = jnp.stack([src, dst])
    edge_index_t = jnp.stack([src, dst], axis=1)
    x = _layernorm(x + _L0_gnn_ref(x, edge_index, edge_attr_16, L0_gnn_W1, L0_gnn_b1, L0_gnn_W2, L0_gnn_b2), axis=-1)
    x = _layernorm(x + _L1_gnn_ref(x, edge_attr_16, edge_index_t, L1_gnn_W_bond, L1_gnn_b_bond, L1_gnn_W_ih, L1_gnn_W_hh, L1_gnn_b_ih, L1_gnn_b_hh), axis=-1)
    return x

_drawn_inputs = setup_inputs


def setup_inputs(seed=0):
    import zlib

    import numpy as np

    out = dict(_drawn_inputs(seed))
    spreads = {'L0_gnn_b1': (0.0, 0.567),
     'L0_gnn_b2': (0.0, 0.383),
     'L1_gnn_b_bond': (0.0, 0.1),
     'L1_gnn_b_ih': (0.0, 0.1),
     'L1_gnn_b_hh': (0.0, 0.1)}
    factors = {}
    for name, (base, spread) in spreads.items():
        noise = np.random.default_rng([zlib.crc32(name.encode()), seed]).standard_normal(out[name].shape)
        drawn = base * np.exp(spread * noise) if base else spread * noise
        out[name] = jnp.asarray(drawn.astype(out[name].dtype))
    for name, factor in factors.items():
        out[name] = (out[name] * factor).astype(out[name].dtype)
    return out
```

```python
from contextlib import ExitStack

import numpy as np
import concourse.bass as bass
from concourse import mybir

F32 = mybir.dt.float32
BF16 = mybir.dt.bfloat16
I32 = mybir.dt.int32
ALU = mybir.AluOpType
ACT = mybir.ActivationFunctionType

N, D, E, EC, DM = 100000, 32, 25000, 16, 56
P = 128
Q = 4
J = -(-E // (P * Q))
T = Q * J
QE = J * P
EP = T * P
JC = 7
EI = J // JC
CW = JC * P
UC = JC * Q
NP = 125
NR = N // NP
NG = 8
NI = NR // (NG * Q)
NH = NG // 2 * NP
NC = NG * Q
TW = 36
RW = 20
HT = 14
PI = T // (2 * HT)
LOW, HIGH = 256, 392
BT = 14
STEPS = 4
FAR = 1.0e6
BIG = 1.5e38
EPS = 1e-5

IH, HH, WB = 0, 3, 6
L0S, L0D, L0E, L0V = WB + EC + 1, WB + EC + 3, WB + EC + 5, WB + EC + 7
IDENT, CENTRE, MEAN, ONES = range(WB + EC + 9, WB + EC + 13)
NW = ONES + 1
B_R, B_Z, B_IN, B_HN, B_RH, B_ZH, B_1A, B_1B, B_2, B_EPS = range(10)
NB = 10


class Signal:

    def __init__(self, sem, base):
        self.sem, self.base = sem, base

    def at(self, n):
        return n + self.base


def bass_gnn_resnorm(nc, x, src_pu, dst_pu, ea_pu, ea_t, weights, biases, sel_h, triu_h, iota_h, slot_h, out):
    ctx = ExitStack()
    with ctx:
        def sb(name, shape, dt=F32):
            return ctx.enter_context(nc.sbuf_tensor(name, shape, dt))

        def dram(name, shape, dt=F32):
            return nc.dram_tensor(name, shape, dt, kind="Internal").ap()

        signals = {}

        def sig(name):
            if name not in signals:
                signals[name] = Signal(ctx.enter_context(nc.semaphore(name)), 0 if name.startswith("d_") else 2)
            return signals[name]

        l0_src_rows = dram("l0_src_rows", (P, T, D))
        l0_dst_rows = dram("l0_dst_rows", (P, T, D))
        edges0 = dram("edges0", (P, T, RW))
        edges1 = dram("edges1", (EP, RW))
        edges2 = dram("edges2", (EP, RW))
        x1_rows = dram("x1_rows", (P, T, TW))
        table = dram("table", (N, TW))
        table_words = table.rearrange("n (w o) -> (n w) o", o=1)
        src_rows = dram("src_rows", (P, T, D))
        dst_rows = dram("dst_rows", (P, T, D))
        nbr_rows = dram("nbr_rows", (P, T, D))
        state = dram("state", (EP, D))
        state_rows = state.rearrange("(p u) d -> p u d", p=P)
        final_rows = dram("final_rows", (P, T, D))

        w = sb("w", [P, NW * P])
        bias = sb("bias", [P, NB])
        sel = sb("sel", [P, EC * P], BF16)
        triu = sb("triu", [P, P], BF16)
        iota = sb("iota", [P, HIGH])
        slots = sb("slots", [P, T])

        def W(n, k=P):
            return w[0:k, n * P:(n + 1) * P]

        def B(n):
            return bias[:, n:n + 1]

        arr_s = sb("arr_s", [P, QE])
        arr_d = sb("arr_d", [P, QE])
        arr_m = sb("arr_m", [P, QE + 1])
        same = sb("same", [P, QE], BF16)
        prefix = sb("prefix", [P, QE], BF16)
        ea_hm = sb("ea_hm", [P, QE], BF16)
        ea_lo = sb("ea_lo", [Q * EC, QE], BF16)

        src_i = sb("src_i", [P, T], I32)
        dst_i = sb("dst_i", [P, T], I32)
        key_f = sb("key_f", [P, T])
        src_f = sb("src_f", [P, T])
        dst_f = sb("dst_f", [P, T])
        digit = sb("digit", [P, T])
        rank = sb("rank", [P, T])
        rank_t = sb("rank_t", [P, BT])
        tmp_i = sb("tmp_i", [P, T], I32)
        tmp_f = sb("tmp_f", [P, T])
        idx_a = sb("idx_a", [P, T], I32)
        idx_b = sb("idx_b", [P, T], I32)
        idx_c = sb("idx_c", [P, T], I32)
        slot_f = sb("slot_f", [P, T])
        last_f = sb("last_f", [P, T])

        ring = sb("ring", [P, 2, HT * TW])
        ring_i = sb("ring_i", [P, 2, HT], I32)

        rows = sb("rows", [P, NC * TW])
        rows_b = sb("rows_b", [P, CW])
        rows_o = sb("rows_o", [P, NC * TW])
        ca = sb("ca", [P, NC * D])
        cb = sb("cb", [P, NC * D])
        cc = sb("cc", [P, NC * D])
        cd = sb("cd", [P, NC * D])
        ce = sb("ce", [P, NC * D])
        cf = sb("cf", [P, NC * D])
        cg = sb("cg", [P, NC * D])
        col = sb("col", [P, 8])
        oh = sb("oh", [P, 2, HIGH], BF16)
        cum = sb("cum", [P, 2, HIGH])

        PA, PB, PC, PD = (ctx.enter_context(nc.psum_tensor(f"p{n}", [P, 1024], F32)) for n in "abcd")

        def halves(ps, buf, dense):
            if dense:
                return [(ps[:, 512 * h:512 * h + NH], buf[:, NH * h:NH * h + NH]) for h in range(2)]
            return [(ps[:, 0:512], buf[:, 0:512]), (ps[:, 512:CW], buf[:, 512:CW])]

        def pv(ps, dense):
            return ps[:, :].rearrange("p (h c) -> p h c", h=2)[:, :, 0:NH] if dense else ps[:, 0:CW]

        def bv(buf, dense):
            return buf[:, 0:2 * NH].rearrange("p (h c) -> p h c", h=2) if dense else buf[:, 0:CW]

        def advance(name, n):
            sig(name).base += n

        class RingPass:

            def __init__(self, idx, table_ap, width, last, scatter=False, load_from=None, store=None, stored=0):
                self.idx, self.table_ap, self.width, self.last, self.scatter = idx, table_ap, width, last, scatter
                self.load_from, self.store, self.n_stored = load_from, store, stored
                self.n_loaded = 16 if load_from is None else 32
                self.base = {n: sig(n).base for h in range(2) for n in (f"d_loaded{h}", f"d_done{h}", f"d_stored{h}")}
                for h in range(2):
                    advance(f"d_loaded{h}", PI * self.n_loaded)
                    advance(f"d_done{h}", PI * 16 * HT)
                    advance(f"d_stored{h}", PI * 16 * stored)

            def pool(self, pool):
                width = self.width
                with pool.Fori(0, PI) as i:
                    for h in range(2):
                        pool.wait_ge(sig(f"d_loaded{h}").sem, (i + 1) * self.n_loaded + self.base[f"d_loaded{h}"])
                        pool.sem_inc(sig("turns").sem, 1)
                        for k in range(HT):
                            view = ring[:, h, k * width:(k + 1) * width]
                            at = bass.IndirectOffsetOnAxis(ap=ring_i[:, h, k:k + 1], axis=0)
                            ends = (self.table_ap, at, view, None) if self.scatter else (view, None, self.table_ap, at)
                            pool.indirect_dma_start(*ends, bounds_check=self.last, oob_is_err=False)\
                                .then_inc(sig(f"d_done{h}").sem, 16)

            def sp(self, sp):
                def fill(h, u):
                    sp.dma_start(ring_i[:, h, :], self.idx[:, bass.ds(u, HT)]).then_inc(sig(f"d_loaded{h}").sem, 16)
                    if self.load_from is not None:
                        sp.dma_start(ring[:, h, 0:HT * self.width].rearrange("p (t w) -> p t w", w=self.width),
                                     self.load_from[:, bass.ds(u, HT), :]).then_inc(sig(f"d_loaded{h}").sem, 16)

                def turn(i, h):
                    sp.wait_ge(sig(f"d_done{h}").sem, (i + 1) * (16 * HT) + self.base[f"d_done{h}"])
                    if self.store is not None:
                        self.store(sp, h, (i * 2 + h) * HT, sig(f"d_stored{h}").sem)
                        sp.wait_ge(sig(f"d_stored{h}").sem, (i + 1) * (16 * self.n_stored) + self.base[f"d_stored{h}"])

                for h in range(2):
                    fill(h, h * HT)
                with sp.Fori(0, PI - 1) as i:
                    for h in range(2):
                        turn(i, h)
                        fill(h, (i * 2 + 2 + h) * HT)
                for h in range(2):
                    turn(PI - 1, h)

        def back(store_ap, width=D):
            def store(sp, h, u, sem):
                sp.dma_start(store_ap[:, bass.ds(u, HT), :],
                             ring[:, h, 0:HT * width].rearrange("p (t w) -> p t w", w=width)[:, :, 0:D]).then_inc(sem, 16)
            return store

        def back_with_slot(store_ap):
            def store(sp, h, u, sem):
                g = ring[:, h, :].rearrange("p (t w) -> p t w", w=TW)
                sp.dma_start(store_ap[:, bass.ds(u, HT), :], g[:, :, 0:D]).then_inc(sem, 16)
                sp.dma_start(slot_f[:, bass.ds(u, HT)], g[:, :, D]).then_inc(sem, 16)
            return store

        def ln_pe(pe, n, xin, dense):
            for ps, b in halves(PA, xin, dense):
                ins = pe.matmul(ps, W(CENTRE), b, start=True, stop=True)
            ins.then_inc(sig("ln_centred").sem, 1)
            pe.wait_ge(sig("ln_squared").sem, sig("ln_squared").at(n + 1))
            for ps, b in halves(PB, cc, dense):
                ins = pe.matmul(ps, W(MEAN), b, start=True, stop=True)
            ins.then_inc(sig("ln_var").sem, 1)

        def ln_act(act, n, dense):
            act.wait_ge(sig("ln_centred").sem, sig("ln_centred").at(n + 1))
            act.activation(bv(cc, dense), pv(PA, dense), ACT.Square).then_inc(sig("ln_squared").sem, 1)
            act.wait_ge(sig("ln_var").sem, sig("ln_var").at(n + 1))
            act.activation(bv(cd, dense), pv(PB, dense), ACT.Sqrt, bias=B(B_EPS)).then_inc(sig("ln_dev").sem, 1)

        def ln_dve(dve, n, xout, dense):
            dve.wait_ge(sig("ln_dev").sem, sig("ln_dev").at(n + 1))
            dve.reciprocal(bv(ce, dense), bv(cd, dense)).then_inc(sig("ln_inv").sem, 1)
            dve.wait_ge(sig("ln_inv").sem, sig("ln_inv").at(n + 1))
            dve.tensor_tensor(bv(xout, dense), pv(PA, dense), bv(ce, dense), ALU.mult).then_inc(sig("ln_out").sem, 1)

        def ln_advance(n):
            for name in ("ln_centred", "ln_squared", "ln_var", "ln_dev", "ln_inv", "ln_out"):
                advance(name, n)

        def to_columns(pe, ps, buf, dense, width=D):
            if dense:
                v = buf[0:NP, 0:NC * width].rearrange("p (g r w) -> p g r w", r=Q, w=width)
                for g in range(NG):
                    o = 512 * (g // (NG // 2)) + NP * (g % (NG // 2))
                    ins = pe.transpose(ps[:, o:o + NP], v[:, g, :, 0:D], W(IDENT)[0:NP, 0:NP])
            else:
                for j in range(JC):
                    ins = pe.transpose(ps[:, j * P:(j + 1) * P], buf[:, j * P:(j + 1) * P], W(IDENT))
            return ins

        def to_rows(pe, ps, buf, dense):
            if dense:
                for g in range(NG):
                    ins = pe.transpose(ps[0:NP, g * P:(g + 1) * P], buf[:, g * NP:(g + 1) * NP], W(IDENT))
            else:
                for j in range(JC):
                    ins = pe.transpose(ps[:, j * P:(j + 1) * P], buf[:, j * P:(j + 1) * P], W(IDENT))
            return ins

        def gru_pe(pe, n, h, agg, dense):
            gates = [(PA, IH, HH), (PB, IH + 1, HH + 1), (PC, None, HH + 2), (PD, IH + 2, None)]
            for ps, wi, wh in gates:
                if wh is None and agg is None:
                    continue
                for half in range(2):
                    o = halves(ps, h, dense)[half][0]
                    parts = [(W(wh), halves(ps, h, dense)[half][1])] if wh is not None else []
                    if wi is not None and agg is not None:
                        parts.append((W(wi), halves(ps, agg, dense)[half][1]))
                    for m, (l, r) in enumerate(parts):
                        ins = pe.matmul(o, l, r, start=(m == 0), stop=(m == len(parts) - 1))
            ins.then_inc(sig("gates").sem, 1)

        def gru_act(act, n, dense):
            act.wait_ge(sig("gates").sem, sig("gates").at(n + 1))
            act.activation(bv(ca, dense), pv(PA, dense), ACT.Sigmoid, bias=B(B_R)).then_inc(sig("gate_r").sem, 1)
            act.activation(bv(cb, dense), pv(PB, dense), ACT.Sigmoid, bias=B(B_Z)).then_inc(sig("gate_z").sem, 1)
            act.wait_ge(sig("cand").sem, sig("cand").at(n + 1))
            act.activation(bv(cd, dense), bv(cc, dense), ACT.Tanh, bias=B(B_IN)).then_inc(sig("gate_n").sem, 1)

        def gru_dve(dve, n, h, has_agg, dense):
            dve.wait_ge(sig("gate_r").sem, sig("gate_r").at(n + 1))
            t = cc if not has_agg else ce
            ins = dve.scalar_tensor_tensor(bv(t, dense), pv(PC, dense), B(B_HN), bv(ca, dense), ALU.add, ALU.mult)
            if has_agg:
                ins.then_inc(sig("cand_h").sem, 1)
                dve.wait_ge(sig("cand_h").sem, sig("cand_h").at(n + 1))
                ins = dve.tensor_tensor(bv(cc, dense), bv(ce, dense), pv(PD, dense), ALU.add)
            ins.then_inc(sig("cand").sem, 1)
            dve.wait_ge(sig("gate_n").sem, sig("gate_n").at(n + 1))
            dve.wait_ge(sig("gate_z").sem, sig("gate_z").at(n + 1))
            dve.tensor_tensor(bv(ca, dense), h, bv(cd, dense), ALU.subtract).then_inc(sig("h_minus_n").sem, 1)
            dve.wait_ge(sig("h_minus_n").sem, sig("h_minus_n").at(n + 1))
            dve.tensor_tensor(bv(cb, dense), bv(cb, dense), bv(ca, dense), ALU.mult).then_inc(sig("z_part").sem, 1)
            dve.wait_ge(sig("z_part").sem, sig("z_part").at(n + 1))
            dve.tensor_tensor(bv(cf, dense), bv(cd, dense), bv(cb, dense), ALU.add).then_inc(sig("h_new").sem, 1)

        def gru_advance(n, has_agg):
            for name in ("gates", "gate_r", "gate_z", "cand", "gate_n", "h_minus_n", "z_part", "h_new"):
                advance(name, n)
            if has_agg:
                advance("cand_h", n)

        def waited(eng):
            eng.sem_inc(sig("turns").sem, 1)

        link_count = [0]

        def link(eng, ins):
            ins.then_inc(sig("dve_link").sem, 1)
            link_count[0] += 1
            eng.wait_ge(sig("dve_link").sem, sig("dve_link").base + link_count[0])

        def by_tile(a):
            return a[:, :].rearrange("p (j c) -> p c j", c=Q)

        def rank_pe(pe, buckets):
            with pe.Fori(0, T // 2) as i:
                for k in range(2):
                    pe.wait_ge(sig("hot").sem, sig("hot").at(i * 2 + k + 1))
                    pe.matmul(PD[:, 0:buckets], ones_b[:, :], oh[:, k, 0:buckets], start=False, stop=False,
                              skip_group_check=True).then_inc(sig("counted").sem, 1)
            with pe.Fori(0, T // BT) as i:
                for k in range(BT):
                    ps = (PA, PB)[k % 2][:, 0:buckets]
                    pe.wait_ge(sig("hot").sem, sig("hot").at(i * BT + k + 1 + T))
                    pe.wait_ge(sig("cum").sem, sig("cum").at(i * BT + k + 1))
                    pe.wait_ge(sig("placed").sem, sig("placed").at(i * BT + (k - 1 if k else 0)))
                    pe.matmul(ps, triu[:, :], oh[:, k % 2, 0:buckets], start=True, stop=False)
                    pe.matmul(ps, W(ONES), cum[:, k % 2, 0:buckets], start=False, stop=True).then_inc(sig("before").sem, 1)

        def rank_dve(dve, buckets):
            link(dve, dve.memset(PD[:, 0:buckets], 0.0))
            link(dve, dve.memset(cum[:, 0, 0:buckets], 0.0))
            with dve.Fori(0, T // 2) as i:
                for k in range(2):
                    t = i * 2 + k
                    dve.wait_ge(sig("counted").sem, sig("counted").at(i * 2 + (k - 1)))
                    dve.tensor_scalar(oh[:, k, 0:buckets], iota[:, 0:buckets], digit[:, bass.ds(t, 1)], None,
                                      ALU.is_equal).then_inc(sig("hot").sem, 1)
            dve.wait_ge(sig("counted").sem, sig("counted").at(T))
            link(dve, dve.tensor_copy(ca[:, 0:buckets], PD[:, 0:buckets]))
            link(dve, dve.memset(cb[:, 0:buckets], 0.0))
            link(dve, dve.tensor_tensor_scan(cc[:, 0:buckets], ca[:, 0:buckets], cb[:, 0:buckets], 0.0, ALU.add, ALU.add))
            dve.tensor_tensor(cum[0:1, 0, 0:buckets], cc[0:1, 0:buckets], ca[0:1, 0:buckets],
                              ALU.subtract).then_inc(sig("cum").sem, 1)
            with dve.Fori(0, T // BT) as i:
                for k in range(BT + 1):
                    t = i * BT + k
                    if 2 <= k < BT:
                        dve.wait_ge(sig("placed").sem, sig("placed").at(t - 1))
                    if k < BT:
                        dve.tensor_scalar(oh[:, k % 2, 0:buckets], iota[:, 0:buckets], digit[:, bass.ds(t, 1)], None,
                                          ALU.is_equal).then_inc(sig("hot").sem, 1)
                    if k:
                        ps = (PA, PB)[(k - 1) % 2][:, 0:buckets]
                        dve.wait_ge(sig("before").sem, sig("before").at(t))
                        dve.tensor_tensor_reduce(ps, ps, oh[:, (k - 1) % 2, 0:buckets], 1.0, 0.0, ALU.mult, ALU.add,
                                                 rank_t[:, k - 1:k]).then_inc(sig("placed").sem, 1)
                    if k < BT:
                        dve.wait_ge(sig("hot").sem, sig("hot").at(t + 1 + T))
                        dve.wait_ge(sig("cum").sem, sig("cum").at(t + 1))
                        dve.tensor_tensor(cum[:, (k + 1) % 2, 0:buckets], cum[:, k % 2, 0:buckets],
                                          oh[:, k % 2, 0:buckets], ALU.add).then_inc(sig("cum").sem, 1)
                dve.wait_ge(sig("placed").sem, sig("placed").at((i + 1) * BT))
                waited(dve)
                dve.tensor_copy(rank[:, bass.ds(i * BT, BT)], rank_t[:, :]).then_inc(sig("ranked").sem, 1)
                dve.wait_ge(sig("ranked").sem, sig("ranked").at(i + 1))

        def rank_advance():
            advance("hot", 2 * T)
            advance("counted", T)
            advance("cum", T + 1)
            advance("before", T)
            advance("placed", T)
            advance("ranked", T // BT)

        def rank_to_row(dve, idx):
            link(dve, dve.tensor_copy(tmp_i[:, :], rank[:, :]))
            link(dve, dve.tensor_scalar(src_i[:, :], tmp_i[:, :], 7, None, ALU.arith_shift_right))
            link(dve, dve.tensor_copy(tmp_f[:, :], src_i[:, :]))
            link(dve, dve.scalar_tensor_tensor(key_f[:, :], tmp_f[:, :], -128.0, rank[:, :], ALU.mult, ALU.add))
            link(dve, dve.tensor_scalar(key_f[:, :], key_f[:, :], float(T), None, ALU.mult))
            link(dve, dve.scalar_tensor_tensor(key_f[:, :], tmp_f[:, :], float(Q), key_f[:, :], ALU.mult, ALU.add))
            for c in range(1, Q):
                link(dve, dve.tensor_scalar(rank[:, :], tmp_f[:, :], float(c * J), -float(Q * J - 1), ALU.is_ge, ALU.mult))
                link(dve, dve.tensor_tensor(key_f[:, :], key_f[:, :], rank[:, :], ALU.add))
            link(dve, dve.tensor_copy(idx[:, :].rearrange("p (j c) -> p c j", c=Q),
                                      key_f[:, :].rearrange("p (c j) -> p c j", c=Q)))

        ones_b = ctx.enter_context(nc.sbuf_tensor("ones_b", [P, P], BF16))

        def masks_pe(pe):
            with pe.Fori(0, EI) as i:
                pe.wait_ge(sig("m_rows").sem, sig("m_rows").at(i + 1))
                to_columns(pe, PA, cf, False).then_inc(sig("m_cols").sem, 1)
            with pe.Fori(0, EI) as i:
                pe.wait_ge(sig("m_last").sem, sig("m_last").at(i + 1))
                to_rows(pe, PA, ce, False).then_inc(sig("m_back").sem, 1)

        def masks_dve(dve):
            kt = arr_m
            with dve.Fori(0, EI) as i:
                dve.wait_ge(sig("m_cols").sem, sig("m_cols").at(i))
                dve.tensor_copy(ca[:, 0:UC], key_f[:, bass.ds(i * UC, UC)]).then_inc(sig("m_keys").sem, 1)
                dve.wait_ge(sig("m_keys").sem, sig("m_keys").at(i + 1))
                dve.tensor_copy(cf[:, 0:CW].rearrange("p (u f) -> p u f", f=D),
                                ca[:, 0:UC].unsqueeze(2).to_broadcast([P, UC, D])).then_inc(sig("m_rows").sem, 1)
                dve.wait_ge(sig("m_cols").sem, sig("m_cols").at(i + 1))
                waited(dve)
                dve.tensor_copy(kt[:, bass.ds(i * CW, CW)], PA[:, 0:CW]).then_inc(sig("m_kt").sem, 1)
            dve.wait_ge(sig("m_kt").sem, sig("m_kt").at(EI))
            link(dve, dve.memset(col[:, :], -1.0))
            for c in range(1, Q):
                link(dve, dve.tensor_copy(col[D * c:D * c + D, 0:1], kt[D * (c - 1):D * c, QE - 1:QE]))
            link(dve, dve.tensor_tensor(same[:, 1:QE], kt[:, 1:QE], kt[:, 0:QE - 1], ALU.is_equal))
            link(dve, dve.tensor_tensor(same[:, 0:1], kt[:, 0:1], col[:, 0:1], ALU.is_equal))
            link(dve, dve.tensor_tensor_scan(prefix[:, :], same[:, :], same[:, :], 1.0, ALU.mult, ALU.mult))
            link(dve, dve.memset(col[:, 1:2], 0.0))
            for c in range(1, Q):
                link(dve, dve.tensor_copy(col[D * (c - 1):D * c, 1:2], same[D * c:D * c + D, 0:1]))
            link(dve, dve.scalar_tensor_tensor(kt[:, 0:QE - 1], same[:, 1:QE], FAR, kt[:, 0:QE - 1], ALU.mult, ALU.add))
            link(dve, dve.scalar_tensor_tensor(kt[:, QE - 1:QE], col[:, 1:2], FAR, kt[:, QE - 1:QE], ALU.mult, ALU.add))
            link(dve, dve.memset(same[:, 0:1], 0.0))
            with dve.Fori(0, EI) as i:
                dve.wait_ge(sig("m_back").sem, sig("m_back").at(i))
                waited(dve)
                dve.tensor_copy(ce[:, 0:CW], kt[:, bass.ds(i * CW, CW)]).then_inc(sig("m_last").sem, 1)
                dve.wait_ge(sig("m_back").sem, sig("m_back").at(i + 1))
                waited(dve)
                dve.tensor_copy(last_f[:, bass.ds(i * UC, UC)],
                                PA[:, 0:CW].rearrange("p (u f) -> p u f", f=D)[:, :, 0]).then_inc(sig("m_lf").sem, 1)
            dve.wait_ge(sig("m_lf").sem, sig("m_lf").at(EI))

        def masks_advance():
            for name in ("m_rows", "m_cols", "m_last", "m_back", "m_keys", "m_kt", "m_lf"):
                advance(name, EI)

        def carry_over(dve, a, op_fix, neutral, mask):
            last = slice(QE - 1, QE)
            link(dve, dve.memset(col[:, 2:3], neutral))
            link(dve, dve.tensor_copy(col[:, 3:4], a[:, last]))
            link(dve, dve.tensor_copy(col[:, 4:5], mask[:, last]))
            for c in range(1, Q):
                q, b = slice(D * c, D * c + D), slice(D * (c - 1), D * c)
                link(dve, dve.tensor_copy(col[q, 2:3], col[b, 3:4]))
                link(dve, dve.scalar_tensor_tensor(col[q, 3:4], col[q, 4:5], col[q, 2:3], a[q, last], op_fix[0], op_fix[1]))
            link(dve, dve.scalar_tensor_tensor(a[:, 0:QE], mask[:, 0:QE], col[:, 2:3], a[:, 0:QE], op_fix[0], op_fix[1]))

        COMPUTE = """turns ln_centred ln_squared ln_var ln_dev ln_inv ln_out gates gate_r gate_z cand_h cand gate_n
            h_minus_n z_part h_new dve_link hot cum counted before placed m_rows m_cols m_last m_back m_keys m_kt m_lf
            edge_rows in_cols y_ready out_rows rows_ready stored x_cols x1_max l0_cols l0_s l0_d l0_h l0_y l0_hl l0_v
            l0_yv l0_done ea_rows ea_cols split hd_ready sel_cols z_ready z_used msg_saved h_in agg_in
            h_saved packed ranked""".split()

        for name in COMPUTE:
            sig(name)
        with nc.Block() as block:
            @block.sync
            def _(sp):
                for name in COMPUTE:
                    sp.sem_inc(signals[name].sem, 2)

        with nc.Block() as block:
            @block.sync
            def _(sp):
                for dst, source in ((w, weights), (bias, biases), (sel, sel_h), (triu, triu_h), (iota, iota_h),
                                    (slots, slot_h), (src_i, src_pu), (dst_i, dst_pu)):
                    sp.dma_start(dst[:, :], source).then_inc(sig("d_const").sem, 16)
                sp.dma_start(arr_s[:, 0:T * EC], ea_pu.rearrange("p t k -> p (t k)")).then_inc(sig("d_const").sem, 16)
                sp.wait_ge(sig("edge_rows").sem, sig("edge_rows").at(1))
                sp.dma_start(edges0, arr_d[:, 0:T * RW].rearrange("p (t w) -> p t w", w=RW)).then_inc(sig("d_rows0").sem, 16)
                sp.wait_ge(sig("d_rows0").sem, 16)

            @block.vector
            def _(dve):
                dve.wait_ge(sig("d_const").sem, 9 * 16)
                er = arr_d[:, 0:T * RW].rearrange("p (t w) -> p t w", w=RW)
                link(dve, dve.memset(arr_d[:, 0:T * RW], 0.0))
                link(dve, dve.memset(ones_b[:, :], 1.0))
                link(dve, dve.tensor_copy(src_f[:, :], src_i[:, :]))
                link(dve, dve.tensor_copy(dst_f[:, :], dst_i[:, :]))
                link(dve, dve.tensor_copy(er[:, :, 0], src_f[:, :]))
                link(dve, dve.tensor_copy(er[:, :, 1], dst_f[:, :]))
                link(dve, dve.tensor_copy(er[:, :, 2:2 + EC], arr_s[:, 0:T * EC].rearrange("p (t k) -> p t k", k=EC)))
                dve.sem_inc(sig("edge_rows").sem, 1)
                link(dve, dve.tensor_scalar(tmp_f[:, :], src_f[:, :], float(N - 1), None, ALU.min))
                link(dve, dve.tensor_copy(idx_a[:, :], tmp_f[:, :]))
                link(dve, dve.tensor_scalar(tmp_f[:, :], dst_f[:, :], float(N - 1), None, ALU.min))
                link(dve, dve.tensor_copy(idx_b[:, :], tmp_f[:, :]))
                link(dve, dve.tensor_scalar(tmp_i[:, :], src_i[:, :], LOW - 1, None, ALU.bitwise_and))
                link(dve, dve.tensor_copy(digit[:, :].rearrange("p (c j) -> p c j", c=Q), by_tile(tmp_i)))
                link(dve, dve.tensor_tensor(bias[:, B_R:B_R + 2], bias[:, B_R:B_R + 2], bias[:, B_RH:B_RH + 2], ALU.add))
                link(dve, dve.memset(rows_o[:, :], FAR))

        advance("d_const", 9 * 16)
        advance("d_rows0", 16)
        advance("edge_rows", 1)

        def cols(a, i, width=CW):
            return a[:, bass.ds(i * width, width)]

        def stream_sp(sp, n, load, store, n_out=1):
            def put(i):
                sp.wait_ge(sig("rows_ready").sem, sig("rows_ready").at(i + 1))
                store(sp, i).then_inc(sig("d_out").sem, 16)
                sp.wait_ge(sig("d_out").sem, sig("d_out").at((i + 1) * 16))
                sp.sem_inc(sig("stored").sem, 1)

            if load is not None:
                load(sp, 0).then_inc(sig("d_in").sem, 16)
            with sp.Fori(0, n - 1) as i:
                if load is not None:
                    sp.wait_ge(sig("in_cols").sem, sig("in_cols").at(i + 1))
                    load(sp, i + 1).then_inc(sig("d_in").sem, 16)
                if store is not None:
                    put(i)
            if store is not None:
                put(n - 1)

        def stream_advance(n, load, store):
            if load:
                advance("d_in", 16 * n)
                advance("in_cols", n)
            if store:
                advance("d_out", 16 * n)
                advance("stored", n)
                advance("rows_ready", n)
                advance("out_rows", n)

        def x_nodes(ap, i):
            return ap.rearrange("(p n) d -> p n d", p=NP)[:, bass.ds(i * NC, NC), :]

        def rows_view(buf, width, dense):
            return buf[0:NP, 0:NC * width].rearrange("p (n w) -> p n w", w=width) if dense \
                else buf[:, 0:UC * width].rearrange("p (n w) -> p n w", w=width)

        def rows_out(act, i, width, dense):
            act.wait_ge(sig("out_rows").sem, sig("out_rows").at(i + 1))
            act.wait_ge(sig("stored").sem, sig("stored").at(i))
            source = PC[0:NP, 0:NG * P] if dense else PC[:, 0:CW]
            act.activation(rows_view(rows_o, width, dense)[:, :, 0:D], source.rearrange("p (n w) -> p n w", w=D),
                           ACT.Copy).then_inc(sig("rows_ready").sem, 1)

        def act_store(act, i, rows_ap, width):
            act.wait_ge(sig("rows_ready").sem, sig("rows_ready").at(i + 1))
            act.dma_start(rows_ap[:, bass.ds(i * UC, UC), :], rows_view(rows_o, width, False))\
               .then_inc(sig("d_out").sem, 16)
            act.wait_ge(sig("d_out").sem, sig("d_out").at((i + 1) * 16))
            act.sem_inc(sig("stored").sem, 1)

        g_src = RingPass(idx_a, x, D, N - 1, store=back(l0_src_rows), stored=1)
        g_dst = RingPass(idx_b, x, D, N - 1, store=back(l0_dst_rows), stored=1)
        with nc.Block() as block:
            @block.gpsimd
            def _(pool):
                g_src.pool(pool)
                g_dst.pool(pool)

            @block.sync
            def _(sp):
                g_src.sp(sp)
                g_dst.sp(sp)

            @block.tensor
            def _(pe):
                rank_pe(pe, LOW)
                masks_pe(pe)

            @block.vector
            def _(dve):
                rank_dve(dve, LOW)
                rank_to_row(dve, idx_c)
                link(dve, dve.tensor_copy(key_f[:, :], dst_f[:, :]))
                masks_dve(dve)
                link(dve, dve.tensor_scalar(same[:, :], same[:, :], -1.0, BIG, ALU.add, ALU.mult))
                link(dve, dve.tensor_scalar(prefix[:, :], prefix[:, :], -1.0, BIG, ALU.add, ALU.mult))
        rank_advance()
        masks_advance()

        def base_sp(sp):
            stream_sp(sp, NI, lambda sp, i: sp.dma_start(rows_view(rows, D, True), x_nodes(x, i)),
                      lambda sp, i: sp.dma_start(x_nodes(table, i), rows_view(rows_o, TW, True)))

        with nc.Block() as block:
            @block.sync
            def _(sp):
                base_sp(sp)

            @block.tensor
            def _(pe):
                with pe.Fori(0, NI) as i:
                    pe.wait_ge(sig("d_in").sem, sig("d_in").at((i + 1) * 16))
                    to_columns(pe, PA, rows, True).then_inc(sig("in_cols").sem, 1)
                    pe.wait_ge(sig("y_ready").sem, sig("y_ready").at(i + 1))
                    ln_pe(pe, i, cf, True)
                    pe.wait_ge(sig("ln_out").sem, sig("ln_out").at(i + 1))
                    pe.wait_ge(sig("rows_ready").sem, sig("rows_ready").at(i))
                    to_rows(pe, PC, ca, True).then_inc(sig("out_rows").sem, 1)

            @block.scalar
            def _(act):
                with act.Fori(0, NI) as i:
                    act.wait_ge(sig("in_cols").sem, sig("in_cols").at(i + 1))
                    act.activation(bv(cg, True), pv(PA, True), ACT.Copy).then_inc(sig("x_cols").sem, 1)
                    ln_act(act, i, True)
                    rows_out(act, i, TW, True)

            @block.vector
            def _(dve):
                with dve.Fori(0, NI) as i:
                    dve.wait_ge(sig("x_cols").sem, sig("x_cols").at(i + 1))
                    dve.scalar_tensor_tensor(bv(cf, True), bv(cg, True), 0.0, bv(cg, True), ALU.max, ALU.add)\
                       .then_inc(sig("y_ready").sem, 1)
                    ln_dve(dve, i, ca, True)
        stream_advance(NI, True, True)
        advance("x_cols", NI)
        advance("y_ready", NI)
        ln_advance(NI)

        sort_low = RingPass(idx_c, edges1, RW, EP - 1, scatter=True, load_from=edges0)

        def maximum_x1(dve):
            link(dve, dve.tensor_tensor_scan(arr_m[:, 0:QE], same[:, :], arr_m[:, 0:QE], -BIG, ALU.add, ALU.max))
            carry_over(dve, arr_m, (ALU.add, ALU.max), -BIG, prefix)

        with nc.Block() as block:
            @block.gpsimd
            def _(pool):
                sort_low.pool(pool)

            @block.sync
            def _(sp):
                sort_low.sp(sp)

            @block.scalar
            def _(act):
                def load(i):
                    act.dma_start(rows[:, 0:CW].rearrange("p (u d) -> p u d", d=D),
                                  l0_src_rows[:, bass.ds(i * UC, UC), :]).then_inc(sig("d_l0").sem, 16)
                    act.dma_start(rows_b[:, 0:CW].rearrange("p (u d) -> p u d", d=D),
                                  l0_dst_rows[:, bass.ds(i * UC, UC), :]).then_inc(sig("d_l0").sem, 16)
                    act.dma_start(ce[0:Q * EC, 0:CW], ea_t[:, bass.ds(i * CW, CW)]).then_inc(sig("d_l0").sem, 16)
                with act.Fori(0, EI) as i:
                    act.wait_ge(sig("l0_h").sem, sig("l0_h").at(i))
                    load(i)
                    act.wait_ge(sig("l0_cols").sem, sig("l0_cols").at(i + 1))
                    act.activation(ca[:, 0:CW], PA[:, 0:CW], ACT.Copy).then_inc(sig("l0_s").sem, 1)
                    act.wait_ge(sig("l0_h").sem, sig("l0_h").at(i + 1))
                    act.activation(cc[:, 0:CW], PC[:, 0:CW], ACT.Identity, bias=B(B_1A))
                    act.activation(cd[:, 0:CW], PD[:, 0:CW], ACT.Identity, bias=B(B_1B)).then_inc(sig("l0_y").sem, 1)
                    act.wait_ge(sig("l0_v").sem, sig("l0_v").at(i + 1))
                    act.activation(cg[:, 0:CW], PA[:, 0:CW], ACT.Identity, bias=B(B_2)).then_inc(sig("l0_yv").sem, 1)
                with act.Fori(0, EI) as i:
                    ln_act(act, i, False)
                    rows_out(act, i, TW, False)
                    act_store(act, i, x1_rows, TW)

            @block.tensor
            def _(pe):
                with pe.Fori(0, EI) as i:
                    pe.wait_ge(sig("d_l0").sem, sig("d_l0").at((i + 1) * 48))
                    to_columns(pe, PA, rows, False)
                    to_columns(pe, PB, rows_b, False).then_inc(sig("l0_cols").sem, 1)
                    pe.wait_ge(sig("l0_s").sem, sig("l0_s").at(i + 1))
                    pe.wait_ge(sig("l0_d").sem, sig("l0_d").at(i + 1))
                    for pair, ps in enumerate((PC, PD)):
                        for half in range(2):
                            o, xs = halves(ps, ca, False)[half]
                            xd, ea = halves(ps, cb, False)[half][1], halves(ps, ce, False)[half][1]
                            pe.matmul(o, W(L0S + pair), xs, start=True, stop=False)
                            pe.matmul(o, W(L0D + pair), xd, start=False, stop=False)
                            ins = pe.matmul(o, W(L0E + pair, Q * EC), ea[0:Q * EC, :], start=False, stop=True)
                    ins.then_inc(sig("l0_h").sem, 1)
                    pe.wait_ge(sig("l0_hl").sem, sig("l0_hl").at(i + 1))
                    for half in range(2):
                        o, ha = halves(PA, rows_o, False)[half]
                        pe.matmul(o, W(L0V), ha, start=True, stop=False)
                        ins = pe.matmul(o, W(L0V + 1), halves(PA, cf, False)[half][1], start=False, stop=True)
                    ins.then_inc(sig("l0_v").sem, 1)
                    pe.wait_ge(sig("l0_yv").sem, sig("l0_yv").at(i + 1))
                with pe.Fori(0, EI) as i:
                    pe.wait_ge(sig("y_ready").sem, sig("y_ready").at(i + 1))
                    ln_pe(pe, i, cf, False)
                    pe.wait_ge(sig("ln_out").sem, sig("ln_out").at(i + 1))
                    pe.wait_ge(sig("rows_ready").sem, sig("rows_ready").at(i))
                    to_rows(pe, PC, ca, False).then_inc(sig("out_rows").sem, 1)

            @block.vector
            def _(dve):
                with dve.Fori(0, EI) as i:
                    dve.wait_ge(sig("l0_cols").sem, sig("l0_cols").at(i + 1))
                    dve.tensor_copy(cb[:, 0:CW], PB[:, 0:CW]).then_inc(sig("l0_d").sem, 1)
                    dve.tensor_copy(cols(arr_d, i), PB[:, 0:CW])
                    dve.wait_ge(sig("l0_y").sem, sig("l0_y").at(i + 1))
                    dve.scalar_tensor_tensor(rows_o[:, 0:CW], cc[:, 0:CW], 0.01, cc[:, 0:CW], ALU.mult, ALU.max)
                    dve.scalar_tensor_tensor(cf[:, 0:CW], cd[:, 0:CW], 0.01, cd[:, 0:CW], ALU.mult, ALU.max)\
                       .then_inc(sig("l0_hl").sem, 1)
                    dve.wait_ge(sig("l0_yv").sem, sig("l0_yv").at(i + 1))
                    dve.scalar_tensor_tensor(cols(arr_m, i), cg[:, 0:CW], 0.01, cg[:, 0:CW], ALU.mult, ALU.max)\
                       .then_inc(sig("l0_done").sem, 1)
                dve.wait_ge(sig("l0_done").sem, sig("l0_done").at(EI))
                link(dve, dve.memset(rows_o[:, :], FAR))
                maximum_x1(dve)
                with dve.Fori(0, EI) as i:
                    dve.wait_ge(sig("ln_out").sem, sig("ln_out").at(i))
                    dve.tensor_tensor(cb[:, 0:CW], cols(arr_m, i), cols(arr_d, i), ALU.max).then_inc(sig("x1_max").sem, 1)
                    dve.wait_ge(sig("x1_max").sem, sig("x1_max").at(i + 1))
                    dve.tensor_tensor(cf[:, 0:CW], cb[:, 0:CW], cols(arr_d, i), ALU.add).then_inc(sig("y_ready").sem, 1)
                    ln_dve(dve, i, ca, False)
                link(dve, dve.tensor_copy(idx_a[:, :], last_f[:, :]))
        advance("d_l0", 48 * EI)
        for name in ("l0_cols", "l0_s", "l0_d", "l0_h", "l0_y", "l0_hl", "l0_v", "l0_yv", "l0_done", "x1_max", "y_ready"):
            advance(name, EI)
        stream_advance(EI, False, True)
        ln_advance(EI)

        put_x1 = RingPass(idx_a, table, TW, N - 1, scatter=True, load_from=x1_rows)
        with nc.Block() as block:
            @block.gpsimd
            def _(pool):
                put_x1.pool(pool)

            @block.sync
            def _(sp):
                put_x1.sp(sp)

            @block.scalar
            def _(act):
                act.dma_start(arr_s[:, 0:T * RW], edges1.rearrange("(p u) w -> p (u w)", p=P)).then_inc(sig("d_const").sem, 16)

            @block.tensor
            def _(pe):
                rank_pe(pe, HIGH)

            @block.vector
            def _(dve):
                dve.wait_ge(sig("d_const").sem, sig("d_const").at(16))
                link(dve, dve.tensor_copy(src_i[:, :], arr_s[:, 0:T * RW].rearrange("p (t w) -> p t w", w=RW)[:, :, 0]))
                link(dve, dve.tensor_scalar(tmp_i[:, :], src_i[:, :], LOW.bit_length() - 1, None, ALU.arith_shift_right))
                link(dve, dve.tensor_copy(digit[:, :].rearrange("p (c j) -> p c j", c=Q), by_tile(tmp_i)))
                rank_dve(dve, HIGH)
                rank_to_row(dve, idx_c)
        advance("d_const", 16)
        rank_advance()

        sort_high = RingPass(idx_c, edges2, RW, EP - 1, scatter=True, load_from=edges1.rearrange("(p u) w -> p u w", p=P))
        with nc.Block() as block:
            @block.gpsimd
            def _(pool):
                sort_high.pool(pool)

            @block.sync
            def _(sp):
                sort_high.sp(sp)
        with nc.Block() as block:
            @block.sync
            def _(sp):
                stream_sp(sp, NI, lambda sp, i: sp.dma_start(rows_view(rows, TW, True), x_nodes(table, i)),
                          lambda sp, i: sp.dma_start(x_nodes(out, i), rows_view(rows_o, D, True)))

            @block.tensor
            def _(pe):
                with pe.Fori(0, NI) as i:
                    pe.wait_ge(sig("packed").sem, sig("packed").at(i + 1))
                    to_columns(pe, PA, cf, True).then_inc(sig("in_cols").sem, 1)
                    pe.wait_ge(sig("x_cols").sem, sig("x_cols").at(i + 1))
                    for t in range(STEPS):
                        if t:
                            pe.wait_ge(sig("h_new").sem, sig("h_new").at(i * STEPS + t))
                        gru_pe(pe, i * STEPS + t, cf if t else cg, None, True)
                    pe.wait_ge(sig("y_ready").sem, sig("y_ready").at(i + 1))
                    ln_pe(pe, i, cb, True)
                    pe.wait_ge(sig("ln_out").sem, sig("ln_out").at(i + 1))
                    pe.wait_ge(sig("rows_ready").sem, sig("rows_ready").at(i))
                    to_rows(pe, PC, ca, True).then_inc(sig("out_rows").sem, 1)

            @block.scalar
            def _(act):
                with act.Fori(0, NI) as i:
                    act.wait_ge(sig("d_in").sem, sig("d_in").at((i + 1) * 16))
                    act.activation(rows_view(cf, D, True), rows_view(rows, TW, True)[:, :, 0:D], ACT.Copy)\
                       .then_inc(sig("packed").sem, 1)
                    act.wait_ge(sig("in_cols").sem, sig("in_cols").at(i + 1))
                    act.activation(bv(cg, True), pv(PA, True), ACT.Copy).then_inc(sig("x_cols").sem, 1)
                    for t in range(STEPS):
                        gru_act(act, i * STEPS + t, True)
                    ln_act(act, i, True)
                    rows_out(act, i, D, True)

            @block.vector
            def _(dve):
                with dve.Fori(0, NI) as i:
                    for t in range(STEPS):
                        gru_dve(dve, i * STEPS + t, bv(cf if t else cg, True), False, True)
                    dve.wait_ge(sig("h_new").sem, sig("h_new").at(i * STEPS + STEPS))
                    dve.tensor_tensor(bv(cb, True), bv(cf, True), bv(cg, True), ALU.add).then_inc(sig("y_ready").sem, 1)
                    ln_dve(dve, i, ca, True)
        stream_advance(NI, True, True)
        advance("x_cols", NI)
        advance("packed", NI)
        advance("y_ready", NI)
        gru_advance(NI * STEPS, False)
        ln_advance(NI)

        sorted_rows = arr_s[:, 0:T * RW].rearrange("p (t w) -> p t w", w=RW)
        with nc.Block() as block:
            @block.sync
            def _(sp):
                sp.dma_start(arr_s[:, 0:T * RW], edges2.rearrange("(p u) w -> p (u w)", p=P)).then_inc(sig("d_const").sem, 16)

            @block.tensor
            def _(pe):
                masks_pe(pe)
                with pe.Fori(0, EI) as i:
                    pe.wait_ge(sig("ea_rows").sem, sig("ea_rows").at(i + 1))
                    waited(pe)
                    for j in range(JC):
                        ins = pe.transpose(PA[0:Q * EC, j * P:(j + 1) * P], ca[:, j * Q * EC:(j + 1) * Q * EC], W(IDENT))
                    ins.then_inc(sig("ea_cols").sem, 1)

            @block.vector
            def _(dve):
                dve.wait_ge(sig("d_const").sem, sig("d_const").at(16))
                link(dve, dve.tensor_copy(key_f[:, :], sorted_rows[:, :, 0]))
                link(dve, dve.tensor_copy(dst_f[:, :], sorted_rows[:, :, 1]))
                link(dve, dve.tensor_scalar(tmp_f[:, :], key_f[:, :], float(N - 1), None, ALU.min))
                link(dve, dve.tensor_copy(idx_a[:, :], tmp_f[:, :]))
                link(dve, dve.tensor_scalar(tmp_f[:, :], dst_f[:, :], float(N - 1), None, ALU.min))
                link(dve, dve.tensor_copy(idx_b[:, :], tmp_f[:, :]))
                masks_dve(dve)
                half = slice(0, Q * EC)
                with dve.Fori(0, EI) as i:
                    dve.wait_ge(sig("ea_cols").sem, sig("ea_cols").at(i))
                    waited(dve)
                    dve.tensor_copy(ca[:, 0:UC * EC].rearrange("p (u k) -> p u k", k=EC),
                                    sorted_rows[:, bass.ds(i * UC, UC), 2:2 + EC]).then_inc(sig("ea_rows").sem, 1)
                    dve.wait_ge(sig("ea_cols").sem, sig("ea_cols").at(i + 1))
                    n = 6
                    dve.tensor_copy(ea_hm[half, bass.ds(i * CW, CW)], PA[half, 0:CW]).then_inc(sig("split").sem, 1)
                    dve.wait_ge(sig("split").sem, sig("split").at(i * n + 1))
                    dve.tensor_tensor(cb[half, 0:CW], PA[half, 0:CW], ea_hm[half, bass.ds(i * CW, CW)],
                                      ALU.subtract).then_inc(sig("split").sem, 1)
                    dve.wait_ge(sig("split").sem, sig("split").at(i * n + 2))
                    waited(dve)
                    dve.tensor_copy(ea_lo[:, bass.ds(i * CW, CW)], cb[half, 0:CW]).then_inc(sig("split").sem, 1)
                    dve.wait_ge(sig("split").sem, sig("split").at(i * n + 3))
                    dve.tensor_tensor(cc[half, 0:CW], cb[half, 0:CW], ea_lo[:, bass.ds(i * CW, CW)],
                                      ALU.subtract).then_inc(sig("split").sem, 1)
                    dve.tensor_copy(ea_hm[Q * EC:P, bass.ds(i * CW, CW)], ea_lo[:, bass.ds(i * CW, CW)])\
                       .then_inc(sig("split").sem, 1)
                    dve.wait_ge(sig("split").sem, sig("split").at(i * n + 5))
                    waited(dve)
                    dve.tensor_copy(ea_lo[:, bass.ds(i * CW, CW)], cc[half, 0:CW]).then_inc(sig("split").sem, 1)
                link(dve, dve.tensor_copy(idx_c[:, :], last_f[:, :]))
                link(dve, dve.tensor_scalar(tmp_f[:, :], last_f[:, :], float(TW), float(D), ALU.mult, ALU.add))
                link(dve, dve.tensor_copy(tmp_i[:, :], tmp_f[:, :]))
        advance("d_const", 16)
        masks_advance()
        advance("ea_rows", EI)
        advance("ea_cols", EI)
        advance("split", 6 * EI)

        put_slots = RingPass(tmp_i, table_words, 1, N * TW - 1, scatter=True, load_from=slots[:, :].unsqueeze(2))
        with nc.Block() as block:
            @block.gpsimd
            def _(pool):
                put_slots.pool(pool)

            @block.sync
            def _(sp):
                put_slots.sp(sp)
        g_own = RingPass(idx_a, table, TW, N - 1, store=back(src_rows, TW), stored=1)
        g_nbr = RingPass(idx_b, table, TW, N - 1, store=back_with_slot(dst_rows), stored=2)
        with nc.Block() as block:
            @block.gpsimd
            def _(pool):
                g_own.pool(pool)
                g_nbr.pool(pool)

            @block.sync
            def _(sp):
                g_own.sp(sp)
                g_nbr.sp(sp)

        for source, array in ((src_rows, arr_s), (dst_rows, arr_d)):
            with nc.Block() as block:
                @block.sync
                def _(sp):
                    stream_sp(sp, EI, lambda sp, i: sp.dma_start(rows_view(rows, D, False), source[:, bass.ds(i * UC, UC), :]),
                              None)

                @block.tensor
                def _(pe):
                    with pe.Fori(0, EI) as i:
                        pe.wait_ge(sig("d_in").sem, sig("d_in").at((i + 1) * 16))
                        pe.wait_ge(sig("x_cols").sem, sig("x_cols").at(i))
                        to_columns(pe, PA, rows, False).then_inc(sig("in_cols").sem, 1)

                @block.vector
                def _(dve):
                    if array is arr_s:
                        link(dve, dve.tensor_copy(idx_b[:, :], slot_f[:, :]))
                    with dve.Fori(0, EI) as i:
                        dve.wait_ge(sig("in_cols").sem, sig("in_cols").at(i + 1))
                        waited(dve)
                        dve.tensor_copy(cols(array, i), PA[:, 0:CW]).then_inc(sig("x_cols").sem, 1)
            stream_advance(EI, True, False)
            advance("x_cols", EI)

        for step in range(STEPS):
            final = step == STEPS - 1
            neighbours = nbr_rows if step else dst_rows
            if step:
                g_state = RingPass(idx_b, state, D, EP - 1, load_from=dst_rows, store=back(nbr_rows), stored=1)
                with nc.Block() as block:
                    @block.gpsimd
                    def _(pool):
                        g_state.pool(pool)

                    @block.sync
                    def _(sp):
                        g_state.sp(sp)

            with nc.Block() as block:
                @block.sync
                def _(sp):
                    stream_sp(sp, EI, lambda sp, i: sp.dma_start(rows_view(rows, D, False),
                                                                 neighbours[:, bass.ds(i * UC, UC), :]), None)

                @block.scalar
                def _(act):
                    with act.Fori(0, EI) as i:
                        act.wait_ge(sig("in_cols").sem, sig("in_cols").at(i + 1))
                        act.activation(cg[:, 0:CW], PA[:, 0:CW], ACT.Copy).then_inc(sig("hd_ready").sem, 1)

                @block.tensor
                def _(pe):
                    def attributes(i, k):
                        ps = (PB, PC)[k % 2]
                        for a, b in ((0, 512), (512, CW)):
                            pe.matmul(ps[:, a:b], sel[:, k * P:(k + 1) * P], ea_hm[:, bass.ds(i * CW + a, b - a)],
                                      start=True, stop=False)
                            ins = pe.matmul(ps[:, a:b], sel[0:Q * EC, k * P:(k + 1) * P],
                                            ea_lo[:, bass.ds(i * CW + a, b - a)], start=False, stop=True)
                        ins.then_inc(sig("sel_cols").sem, 1)

                    with pe.Fori(0, EI) as i:
                        pe.wait_ge(sig("d_in").sem, sig("d_in").at((i + 1) * 16))
                        to_columns(pe, PA, rows, False).then_inc(sig("in_cols").sem, 1)
                        attributes(i, 0)
                        attributes(i, 1)
                        pe.wait_ge(sig("hd_ready").sem, sig("hd_ready").at(i + 1))
                        pe.wait_ge(sig("msg_saved").sem, sig("msg_saved").at(i))
                        for o, h in halves(PD, cg, False):
                            pe.matmul(o, W(WB + EC), h, start=True, stop=False)
                        for k in range(EC):
                            pe.wait_ge(sig("z_ready").sem, sig("z_ready").at(i * EC + k + 1))
                            for o, z in halves(PD, (ca, cb)[k % 2], False):
                                ins = pe.matmul(o, W(WB + k), z, start=False, stop=(k == EC - 1))
                            ins.then_inc(sig("z_used").sem, 1)
                            if k + 2 < EC:
                                attributes(i, k + 2)

                @block.vector
                def _(dve):
                    with dve.Fori(0, EI) as i:
                        dve.wait_ge(sig("hd_ready").sem, sig("hd_ready").at(i + 1))
                        for k in range(EC):
                            dve.wait_ge(sig("sel_cols").sem, sig("sel_cols").at(i * EC + k + 1))
                            dve.wait_ge(sig("z_used").sem, sig("z_used").at(i * EC + k - 1))
                            dve.tensor_tensor((ca, cb)[k % 2][:, 0:CW], (PB, PC)[k % 2][:, 0:CW], cg[:, 0:CW],
                                              ALU.mult).then_inc(sig("z_ready").sem, 1)
                        dve.wait_ge(sig("z_used").sem, sig("z_used").at((i + 1) * EC))
                        waited(dve)
                        dve.tensor_copy(cols(arr_m, i), PD[:, 0:CW]).then_inc(sig("msg_saved").sem, 1)
                    dve.wait_ge(sig("msg_saved").sem, sig("msg_saved").at(EI))
                    link(dve, dve.tensor_tensor_scan(arr_m[:, 0:QE], same[:, :], arr_m[:, 0:QE], 0.0, ALU.mult, ALU.add))
                    carry_over(dve, arr_m, (ALU.mult, ALU.add), 0.0, prefix)
            stream_advance(EI, True, False)
            for name, n in (("hd_ready", 1), ("sel_cols", EC), ("z_ready", EC), ("z_used", EC), ("msg_saved", 1)):
                advance(name, n * EI)

            for array, has_agg, target in ((arr_s, True, final_rows if final else state_rows), (arr_d, False, dst_rows)):
                if final and not has_agg:
                    continue
                with nc.Block() as block:
                    @block.sync
                    def _(sp):
                        stream_sp(sp, EI, (lambda sp, i: sp.dma_start(rows_view(rows, D, False),
                                                                      src_rows[:, bass.ds(i * UC, UC), :])) if final else None,
                                  lambda sp, i: sp.dma_start(target[:, bass.ds(i * UC, UC), :], rows_view(rows_o, D, False)))

                    @block.scalar
                    def _(act):
                        with act.Fori(0, EI) as i:
                            act.wait_ge(sig("h_new").sem, sig("h_new").at(i))
                            waited(act)
                            act.activation(cg[:, 0:CW], cols(array, i), ACT.Copy).then_inc(sig("h_in").sem, 1)
                            gru_act(act, i, False)
                            if final:
                                ln_act(act, i, False)
                            else:
                                act.wait_ge(sig("h_new").sem, sig("h_new").at(i + 1))
                                waited(act)
                                act.activation(cols(array, i), cf[:, 0:CW], ACT.Copy).then_inc(sig("h_saved").sem, 1)
                            rows_out(act, i, D, False)

                    @block.tensor
                    def _(pe):
                        with pe.Fori(0, EI) as i:
                            pe.wait_ge(sig("h_in").sem, sig("h_in").at(i + 1))
                            if has_agg:
                                pe.wait_ge(sig("agg_in").sem, sig("agg_in").at(i + 1))
                            pe.wait_ge(sig("rows_ready").sem, sig("rows_ready").at(i))
                            gru_pe(pe, i, cg, rows_b if has_agg else None, False)
                            pe.wait_ge(sig("h_new").sem, sig("h_new").at(i + 1))
                            if final:
                                pe.wait_ge(sig("d_in").sem, sig("d_in").at((i + 1) * 16))
                                to_columns(pe, PB, rows, False).then_inc(sig("in_cols").sem, 1)
                                pe.wait_ge(sig("y_ready").sem, sig("y_ready").at(i + 1))
                                ln_pe(pe, i, cb, False)
                                pe.wait_ge(sig("ln_out").sem, sig("ln_out").at(i + 1))
                            to_rows(pe, PC, ca if final else cf, False).then_inc(sig("out_rows").sem, 1)

                    @block.vector
                    def _(dve):
                        with dve.Fori(0, EI) as i:
                            if has_agg:
                                dve.wait_ge(sig("gates").sem, sig("gates").at(i))
                                waited(dve)
                                dve.tensor_copy(rows_b[:, 0:CW], cols(arr_m, i)).then_inc(sig("agg_in").sem, 1)
                            gru_dve(dve, i, cg[:, 0:CW], has_agg, False)
                            if final:
                                dve.wait_ge(sig("h_new").sem, sig("h_new").at(i + 1))
                                dve.wait_ge(sig("in_cols").sem, sig("in_cols").at(i + 1))
                                dve.tensor_tensor(cb[:, 0:CW], cf[:, 0:CW], PB[:, 0:CW], ALU.add).then_inc(sig("y_ready").sem, 1)
                                ln_dve(dve, i, ca, False)
                stream_advance(EI, final, True)
                gru_advance(EI, has_agg)
                advance("h_in", EI)
                if has_agg:
                    advance("agg_in", EI)
                if final:
                    advance("y_ready", EI)
                    ln_advance(EI)
                else:
                    advance("h_saved", EI)

        put_out = RingPass(idx_c, out, D, N - 1, scatter=True, load_from=final_rows)
        with nc.Block() as block:
            @block.gpsimd
            def _(pool):
                put_out.pool(pool)

            @block.sync
            def _(sp):
                put_out.sp(sp)


def kernel(**inputs):
    import concourse.bacc as _bacc
    import ml_dtypes
    from concourse.bass_utils import run_bass_kernel_spmd as _run

    def get(name):
        return np.asarray(inputs[name])

    def by_slot(a, fill):
        full = np.full((EP,) + a.shape[1:], fill, a.dtype)
        full[:E] = a
        full = full.reshape((Q, J, P) + a.shape[1:])
        return np.ascontiguousarray(np.moveaxis(full, 2, 0).swapaxes(1, 2)).reshape((P, T) + a.shape[1:])

    ea = get("edge_attr_16")
    ea_t = np.zeros((EP, EC), np.float32)
    ea_t[:E] = ea
    ea_t = np.ascontiguousarray(ea_t.reshape(Q, QE, EC).transpose(0, 2, 1)).reshape(Q * EC, QE)

    w = np.zeros((P, NW, P), np.float32)
    w_ih, w_hh = get("L1_gnn_W_ih"), get("L1_gnn_W_hh")
    w_bond, b_bond = get("L1_gnn_W_bond").reshape(EC, D, D), get("L1_gnn_b_bond").reshape(D, D)
    w1, w2 = get("L0_gnn_W1"), get("L0_gnn_W2")
    for c in range(Q):
        q = slice(c * D, c * D + D)
        for g in range(3):
            w[q, IH + g, q] = w_ih[g * D:(g + 1) * D].T
            w[q, HH + g, q] = w_hh[g * D:(g + 1) * D].T
        for k in range(EC):
            w[q, WB + k, q] = w_bond[k].T
        w[q, WB + EC, q] = b_bond.T
        pair, m = c // 2, slice((c % 2) * DM, (c % 2) * DM + DM)
        w[q, L0S + pair, m] = w1[0:D]
        w[q, L0D + pair, m] = w1[D:2 * D]
        w[c * EC:(c + 1) * EC, L0E + pair, m] = w1[2 * D:]
        w[m, L0V + pair, q] = w2
    w[:, IDENT] = np.eye(P)
    block_mean = np.kron(np.eye(Q), np.ones((D, D))) / D
    w[:, CENTRE] = np.eye(P) - block_mean
    w[:, MEAN] = block_mean
    w[:, ONES] = 1.0

    bias = np.zeros((P, NB), np.float32)
    b_ih, b_hh = get("L1_gnn_b_ih"), get("L1_gnn_b_hh")
    b1, b2 = get("L0_gnn_b1"), get("L0_gnn_b2")
    for c in range(Q):
        q = slice(c * D, c * D + D)
        bias[q, B_R], bias[q, B_Z], bias[q, B_IN] = b_ih[:D], b_ih[D:2 * D], b_ih[2 * D:]
        bias[q, B_RH], bias[q, B_ZH], bias[q, B_HN] = b_hh[:D], b_hh[D:2 * D], b_hh[2 * D:]
        bias[q, B_2] = b2
    for m in range(2):
        bias[m * DM:(m + 1) * DM, B_1A] = b1
        bias[m * DM:(m + 1) * DM, B_1B] = b1
    bias[:, B_EPS] = EPS

    sel = np.zeros((2, Q, EC, EC, Q, D), np.float32)
    for k in range(EC):
        for c in range(Q):
            sel[:, c, k, k, c, :] = 1.0
    arrays = {
        "x": np.ascontiguousarray(get("x")),
        "src_pu": by_slot(get("src"), N),
        "dst_pu": by_slot(get("dst"), N),
        "ea_pu": by_slot(ea, 0),
        "ea_t": ea_t,
        "weights": w.reshape(P, NW * P),
        "biases": bias,
        "sel_h": sel.reshape(P, EC * P).astype(ml_dtypes.bfloat16),
        "triu_h": np.triu(np.ones((P, P), np.float32), 1).astype(ml_dtypes.bfloat16),
        "iota_h": np.tile(np.arange(HIGH, dtype=np.float32), (P, 1)),
        "slot_h": np.arange(EP, dtype=np.float32).reshape(P, T),
    }
    nc = _bacc.Bacc("TRN2", target_bir_lowering=False, num_devices=1)
    aps = {n: nc.dram_tensor(n, a.shape, mybir.dt.from_np(a.dtype), kind="ExternalInput").ap() for n, a in arrays.items()}
    out = nc.dram_tensor("out", (N, D), F32, kind="ExternalOutput").ap()
    with nc.allow_non_contiguous_dma(reason="rows of edges and nodes"):
        bass_gnn_resnorm(nc, **aps, out=out)
    r = _run(nc, [arrays], core_ids=[0])
    return r.results[0]["out"]
```

```python
from contextlib import ExitStack

import numpy as np
import concourse.bass as bass
from concourse import mybir

F32 = mybir.dt.float32
BF16 = mybir.dt.bfloat16
I32 = mybir.dt.int32
ALU = mybir.AluOpType
ACT = mybir.ActivationFunctionType

N, D, E, EC, DM = 100000, 32, 25000, 16, 56
P = 128
Q = 4
J = -(-E // (P * Q))
T = Q * J
QE = J * P
EP = T * P
JC = 7
EI = J // JC
CW = JC * P
UC = JC * Q
NP = 125
NR = N // NP
NG = 8
NI = NR // (NG * Q)
NH = NG // 2 * NP
NC = NG * Q
TW = 36
RW = 20
HT = 14
PI = T // (2 * HT)
LOW, HIGH = 256, 392
BT = 14
STEPS = 4
SPLIT = (9, 8, 8)
FAR = 1.0e6
BIG = 1.5e38
EPS = 1e-5

IH, HH, WB = 0, 3, 6
L0S, L0D, L0E, L0V = WB + EC + 1, WB + EC + 3, WB + EC + 5, WB + EC + 7
IDENT, CENTRE, ONES = range(WB + EC + 9, WB + EC + 12)
NW = ONES + 1
B_R, B_Z, B_IN, B_HN, B_RH, B_ZH, B_1A, B_1B, B_2, B_EPS = range(10)
NB = 10


class Signal:

    def __init__(self, sem, base):
        self.sem, self.base = sem, base

    def at(self, n):
        return n + self.base


def bass_gnn_resnorm(nc, x, src_pu, dst_pu, ea_pu, ea_t, weights, biases, sel_h, triu_h, iota_h, slot_h, out):
    ctx = ExitStack()
    with ctx:
        def sb(name, shape, dt=F32):
            return ctx.enter_context(nc.sbuf_tensor(name, shape, dt))

        def dram(name, shape, dt=F32):
            return nc.dram_tensor(name, shape, dt, kind="Internal").ap()

        signals = {}

        def sig(name):
            if name not in signals:
                signals[name] = Signal(ctx.enter_context(nc.semaphore(name)), 0 if name.startswith("d_") else 2)
            return signals[name]

        l0_src_rows = dram("l0_src_rows", (P, T, D))
        l0_dst_rows = dram("l0_dst_rows", (P, T, D))
        edges0 = dram("edges0", (P, T, RW))
        edges1 = dram("edges1", (EP, RW))
        edges2 = dram("edges2", (EP, RW))
        x1_rows = dram("x1_rows", (P, T, TW))
        table = dram("table", (N, TW))
        table_words = table.rearrange("n (w o) -> (n w) o", o=1)
        src_rows = dram("src_rows", (P, T, D))
        dst_rows = dram("dst_rows", (P, T, D))
        alone_rows = [dram(f"alone_rows{t}", (P, T, D)) for t in range(STEPS - 1)]
        nbr_rows = dram("nbr_rows", (P, T, D))
        state = dram("state", (EP, D))
        state_rows = state.rearrange("(p u) d -> p u d", p=P)
        final_rows = dram("final_rows", (P, T, D))

        w = sb("w", [P, NW * P])
        bias = sb("bias", [P, NB])
        sel = sb("sel", [P, EC * P], BF16)
        triu = sb("triu", [P, P], BF16)
        iota = sb("iota", [P, HIGH])
        slots = sb("slots", [P, T])

        def W(n, k=P):
            return w[0:k, n * P:(n + 1) * P]

        def B(n):
            return bias[:, n:n + 1]

        arr_s = sb("arr_s", [P, QE])
        arr_d = sb("arr_d", [P, QE])
        arr_m = sb("arr_m", [P, QE + 1])
        same = sb("same", [P, QE], BF16)
        prefix = sb("prefix", [P, QE], BF16)
        ea_hm = sb("ea_hm", [P, QE], BF16)
        ea_lo = sb("ea_lo", [Q * EC, QE], BF16)

        src_i = sb("src_i", [P, T], I32)
        dst_i = sb("dst_i", [P, T], I32)
        key_f = sb("key_f", [P, T])
        src_f = sb("src_f", [P, T])
        dst_f = sb("dst_f", [P, T])
        digit = sb("digit", [P, T])
        rank = sb("rank", [P, T])
        rank_t = sb("rank_t", [P, BT])
        tmp_i = sb("tmp_i", [P, T], I32)
        tmp_f = sb("tmp_f", [P, T])
        idx_a = sb("idx_a", [P, T], I32)
        idx_b = sb("idx_b", [P, T], I32)
        idx_c = sb("idx_c", [P, T], I32)
        slot_f = sb("slot_f", [P, T])
        last_f = sb("last_f", [P, T])

        ring = sb("ring", [P, 2, HT * TW])
        ring_i = sb("ring_i", [P, 2, HT], I32)

        rows = sb("rows", [P, NC * TW])
        rows_b = sb("rows_b", [P, CW])
        rows_o = sb("rows_o", [P, NC * TW])
        ca = sb("ca", [P, NC * D])
        cb = sb("cb", [P, NC * D])
        cc = sb("cc", [P, NC * D])
        cd = sb("cd", [P, NC * D])
        ce = sb("ce", [P, NC * D])
        cf = sb("cf", [P, NC * D])
        cg = sb("cg", [P, NC * D])
        col = sb("col", [P, 8])
        stat = sb("stat", [P, 3, NC])
        oh = sb("oh", [P, 2, HIGH], BF16)
        cum = sb("cum", [P, 2, HIGH])

        PA, PB, PC, PD = (ctx.enter_context(nc.psum_tensor(f"p{n}", [P, 1024], F32)) for n in "abcd")

        def halves(ps, buf, dense):
            if dense:
                return [(ps[:, 512 * h:512 * h + NH], buf[:, NH * h:NH * h + NH]) for h in range(2)]
            return [(ps[:, 0:512], buf[:, 0:512]), (ps[:, 512:CW], buf[:, 512:CW])]

        def pv(ps, dense):
            return ps[:, :].rearrange("p (h c) -> p h c", h=2)[:, :, 0:NH] if dense else ps[:, 0:CW]

        def bv(buf, dense):
            return buf[:, 0:2 * NH].rearrange("p (h c) -> p h c", h=2) if dense else buf[:, 0:CW]

        def rows_view(buf, width, dense):
            return buf[0:NP, 0:NC * width].rearrange("p (n w) -> p n w", w=width) if dense \
                else buf[:, 0:UC * width].rearrange("p (n w) -> p n w", w=width)

        def advance(name, n):
            sig(name).base += n

        class RingPass:

            def __init__(self, idx, table_ap, width, last, scatter=False, load_from=None, store=None, stored=0):
                self.idx, self.table_ap, self.width, self.last, self.scatter = idx, table_ap, width, last, scatter
                self.load_from, self.store, self.n_stored = load_from, store, stored
                self.n_loaded = 16 if load_from is None else 32
                self.base = {n: sig(n).base for h in range(2) for n in (f"d_loaded{h}", f"d_done{h}", f"d_stored{h}")}
                for h in range(2):
                    advance(f"d_loaded{h}", PI * self.n_loaded)
                    advance(f"d_done{h}", PI * 16 * HT)
                    advance(f"d_stored{h}", PI * 16 * stored)

            def pool(self, pool):
                width = self.width
                with pool.Fori(0, PI) as i:
                    for h in range(2):
                        pool.wait_ge(sig(f"d_loaded{h}").sem, (i + 1) * self.n_loaded + self.base[f"d_loaded{h}"])
                        pool.sem_inc(sig("turns").sem, 1)
                        for k in range(HT):
                            view = ring[:, h, k * width:(k + 1) * width]
                            at = bass.IndirectOffsetOnAxis(ap=ring_i[:, h, k:k + 1], axis=0)
                            ends = (self.table_ap, at, view, None) if self.scatter else (view, None, self.table_ap, at)
                            pool.indirect_dma_start(*ends, bounds_check=self.last, oob_is_err=False)\
                                .then_inc(sig(f"d_done{h}").sem, 16)

            def sp(self, sp):
                def fill(h, u):
                    sp.dma_start(ring_i[:, h, :], self.idx[:, bass.ds(u, HT)]).then_inc(sig(f"d_loaded{h}").sem, 16)
                    if self.load_from is not None:
                        sp.dma_start(ring[:, h, 0:HT * self.width].rearrange("p (t w) -> p t w", w=self.width),
                                     self.load_from[:, bass.ds(u, HT), :]).then_inc(sig(f"d_loaded{h}").sem, 16)

                def turn(i, h):
                    sp.wait_ge(sig(f"d_done{h}").sem, (i + 1) * (16 * HT) + self.base[f"d_done{h}"])
                    if self.store is not None:
                        self.store(sp, h, (i * 2 + h) * HT, sig(f"d_stored{h}").sem)
                        sp.wait_ge(sig(f"d_stored{h}").sem, (i + 1) * (16 * self.n_stored) + self.base[f"d_stored{h}"])

                for h in range(2):
                    fill(h, h * HT)
                with sp.Fori(0, PI - 1) as i:
                    for h in range(2):
                        turn(i, h)
                        fill(h, (i * 2 + 2 + h) * HT)
                for h in range(2):
                    turn(PI - 1, h)

        def back(store_ap, width=D):
            def store(sp, h, u, sem):
                sp.dma_start(store_ap[:, bass.ds(u, HT), :],
                             ring[:, h, 0:HT * width].rearrange("p (t w) -> p t w", w=width)[:, :, 0:D]).then_inc(sem, 16)
            return store

        def back_with_slot(store_ap):
            def store(sp, h, u, sem):
                g = ring[:, h, :].rearrange("p (t w) -> p t w", w=TW)
                sp.dma_start(store_ap[:, bass.ds(u, HT), :], g[:, :, 0:D]).then_inc(sem, 16)
                sp.dma_start(slot_f[:, bass.ds(u, HT)], g[:, :, D]).then_inc(sem, 16)
            return store

        def to_columns(pe, ps, buf, dense, width=D):
            if dense:
                v = buf[0:NP, 0:NC * width].rearrange("p (g r w) -> p g r w", r=Q, w=width)
                for g in range(NG):
                    o = 512 * (g // (NG // 2)) + NP * (g % (NG // 2))
                    ins = pe.transpose(ps[:, o:o + NP], v[:, g, :, 0:D], W(IDENT)[0:NP, 0:NP])
            else:
                for j in range(JC):
                    ins = pe.transpose(ps[:, j * P:(j + 1) * P], buf[:, j * P:(j + 1) * P], W(IDENT))
            return ins

        def to_rows(pe, ps, buf, dense, centred=False):
            n, width = (NG, NP) if dense else (JC, P)
            for g in range(n):
                o, cols_g = ps[0:width, g * P:(g + 1) * P], buf[:, g * width:(g + 1) * width]
                ins = pe.matmul(o, cols_g, W(CENTRE), start=True, stop=True) if centred else pe.transpose(o, cols_g, W(IDENT))
            return ins

        def ln_views(width, dense):
            p, n = (NP, NC) if dense else (P, UC)
            view = lambda buf: buf[0:p, 0:n * D].rearrange("p (n d) -> p n d", d=D)
            return p, n, view(PC), view(cc), rows_view(rows_o, width, dense)[:, :, 0:D]

        def ln_act(act, i, dense):
            p, n, centred, squares, _ = ln_views(D, dense)
            act.wait_ge(sig("out_rows").sem, sig("out_rows").at(i + 1))
            act.activation(squares, centred, ACT.Square).then_inc(sig("ln_squared").sem, 1)
            act.wait_ge(sig("ln_sum").sem, sig("ln_sum").at(i + 1))
            act.activation(stat[0:p, 1, 0:n], stat[0:p, 0, 0:n], ACT.Sqrt, bias=bias[0:p, B_EPS:B_EPS + 1], scale=1.0 / D)\
               .then_inc(sig("ln_dev").sem, 1)

        def ln_dve(dve, i, width, dense):
            p, n, centred, squares, target = ln_views(width, dense)
            dve.wait_ge(sig("ln_squared").sem, sig("ln_squared").at(i + 1))
            dve.tensor_reduce(stat[0:p, 0, 0:n], squares, mybir.AxisListType.X, ALU.add).then_inc(sig("ln_sum").sem, 1)
            dve.wait_ge(sig("ln_dev").sem, sig("ln_dev").at(i + 1))
            dve.reciprocal(stat[0:p, 2, 0:n], stat[0:p, 1, 0:n]).then_inc(sig("ln_inv").sem, 1)
            dve.wait_ge(sig("ln_inv").sem, sig("ln_inv").at(i + 1))
            dve.wait_ge(sig("stored").sem, sig("stored").at(i))
            dve.tensor_tensor(target, centred, stat[0:p, 2, 0:n].unsqueeze(2).to_broadcast([p, n, D]), ALU.mult)\
               .then_inc(sig("rows_ready").sem, 1)

        def ln_advance(n):
            for name in ("ln_squared", "ln_sum", "ln_dev", "ln_inv"):
                advance(name, n)

        def half_of(buf, half, dense):
            if dense:
                return buf[:, NH * half:NH * half + NH]
            return (buf[:, 0:512], buf[:, 512:CW])[half]

        def bank(ps, half, dense):
            return ps[:, 512 * half:512 * half + (NH if dense else (512, CW - 512)[half])]

        def gru_pe(pe, n, h, agg, dense, state_ready):
            for half in range(2):
                state_ready(half)
                gates = [(PA, IH, HH), (PB, IH + 1, HH + 1), (PC, None, HH + 2)]
                if agg is not None:
                    gates.append((PD, IH + 2, None))
                for ps, wi, wh in gates:
                    parts = [(W(wh), h(half))] if wh is not None else []
                    if wi is not None and agg is not None:
                        parts.append((W(wi), agg(half)))
                    for m, (l, r) in enumerate(parts):
                        ins = pe.matmul(bank(ps, half, dense), l, r, start=(m == 0), stop=(m == len(parts) - 1))
                ins.then_inc(sig("gates").sem, 1)

        def gru_act(act, n, dense):
            for half in range(2):
                t = n * 2 + half
                act.wait_ge(sig("gates").sem, sig("gates").at(t + 1))
                act.activation(half_of(ca, half, dense), bank(PA, half, dense), ACT.Sigmoid, bias=B(B_R))\
                   .then_inc(sig("gate_r").sem, 1)
                act.activation(half_of(cb, half, dense), bank(PB, half, dense), ACT.Sigmoid, bias=B(B_Z))\
                   .then_inc(sig("gate_z").sem, 1)
            for half in range(2):
                t = n * 2 + half
                act.wait_ge(sig("cand").sem, sig("cand").at(t + 1))
                act.activation(half_of(cd, half, dense), half_of(cc, half, dense), ACT.Tanh, bias=B(B_IN))\
                   .then_inc(sig("gate_n").sem, 1)

        def gru_dve(dve, n, h, has_agg, dense):
            for half in range(2):
                t = n * 2 + half
                dve.wait_ge(sig("gate_r").sem, sig("gate_r").at(t + 1))
                first = half_of(ce if has_agg else cc, half, dense)
                ins = dve.scalar_tensor_tensor(first, bank(PC, half, dense), B(B_HN), half_of(ca, half, dense),
                                               ALU.add, ALU.mult)
                if has_agg:
                    ins.then_inc(sig("cand_h").sem, 1)
                    dve.wait_ge(sig("cand_h").sem, sig("cand_h").at(t + 1))
                    ins = dve.tensor_tensor(half_of(cc, half, dense), first, bank(PD, half, dense), ALU.add)
                ins.then_inc(sig("cand").sem, 1)
            for half in range(2):
                t = n * 2 + half
                r, z, cand_n = (half_of(buf, half, dense) for buf in (ca, cb, cd))
                dve.wait_ge(sig("gate_n").sem, sig("gate_n").at(t + 1))
                dve.wait_ge(sig("gate_z").sem, sig("gate_z").at(t + 1))
                dve.tensor_tensor(r, h(half), cand_n, ALU.subtract).then_inc(sig("h_minus_n").sem, 1)
                dve.wait_ge(sig("h_minus_n").sem, sig("h_minus_n").at(t + 1))
                dve.tensor_tensor(z, z, r, ALU.mult).then_inc(sig("z_part").sem, 1)
                dve.wait_ge(sig("z_part").sem, sig("z_part").at(t + 1))
                dve.tensor_tensor(half_of(cf, half, dense), cand_n, z, ALU.add).then_inc(sig("h_new").sem, 1)

        def gru_advance(n, has_agg):
            for name in ("gates", "gate_r", "gate_z", "cand", "gate_n", "h_minus_n", "z_part", "h_new"):
                advance(name, 2 * n)
            if has_agg:
                advance("cand_h", 2 * n)

        def waited(eng):
            eng.sem_inc(sig("turns").sem, 1)

        link_count = [0]

        def link(eng, ins):
            ins.then_inc(sig("dve_link").sem, 1)
            link_count[0] += 1
            eng.wait_ge(sig("dve_link").sem, sig("dve_link").base + link_count[0])

        def by_tile(a):
            return a[:, :].rearrange("p (j c) -> p c j", c=Q)

        def rank_pe(pe, buckets):
            with pe.Fori(0, T // 2) as i:
                for k in range(2):
                    pe.wait_ge(sig("hot").sem, sig("hot").at(i * 2 + k + 1))
                    pe.matmul(PD[:, 0:buckets], ones_b[:, :], oh[:, k, 0:buckets], start=False, stop=False,
                              skip_group_check=True).then_inc(sig("counted").sem, 1)
            with pe.Fori(0, T // BT) as i:
                for k in range(BT):
                    ps = (PA, PB)[k % 2][:, 0:buckets]
                    pe.wait_ge(sig("hot").sem, sig("hot").at(i * BT + k + 1 + T))
                    pe.wait_ge(sig("cum").sem, sig("cum").at(i * BT + k + 1))
                    pe.wait_ge(sig("placed").sem, sig("placed").at(i * BT + (k - 1 if k else 0)))
                    pe.matmul(ps, triu[:, :], oh[:, k % 2, 0:buckets], start=True, stop=False)
                    pe.matmul(ps, W(ONES), cum[:, k % 2, 0:buckets], start=False, stop=True).then_inc(sig("before").sem, 1)

        def rank_dve(dve, buckets):
            link(dve, dve.memset(PD[:, 0:buckets], 0.0))
            link(dve, dve.memset(cum[:, 0, 0:buckets], 0.0))
            with dve.Fori(0, T // 2) as i:
                for k in range(2):
                    t = i * 2 + k
                    dve.wait_ge(sig("counted").sem, sig("counted").at(i * 2 + (k - 1)))
                    dve.tensor_scalar(oh[:, k, 0:buckets], iota[:, 0:buckets], digit[:, bass.ds(t, 1)], None,
                                      ALU.is_equal).then_inc(sig("hot").sem, 1)
            dve.wait_ge(sig("counted").sem, sig("counted").at(T))
            link(dve, dve.tensor_copy(ca[:, 0:buckets], PD[:, 0:buckets]))
            link(dve, dve.memset(cb[:, 0:buckets], 0.0))
            link(dve, dve.tensor_tensor_scan(cc[:, 0:buckets], ca[:, 0:buckets], cb[:, 0:buckets], 0.0, ALU.add, ALU.add))
            dve.tensor_tensor(cum[0:1, 0, 0:buckets], cc[0:1, 0:buckets], ca[0:1, 0:buckets],
                              ALU.subtract).then_inc(sig("cum").sem, 1)
            with dve.Fori(0, T // BT) as i:
                for k in range(BT + 1):
                    t = i * BT + k
                    if 2 <= k < BT:
                        dve.wait_ge(sig("placed").sem, sig("placed").at(t - 1))
                    if k < BT:
                        dve.tensor_scalar(oh[:, k % 2, 0:buckets], iota[:, 0:buckets], digit[:, bass.ds(t, 1)], None,
                                          ALU.is_equal).then_inc(sig("hot").sem, 1)
                    if k:
                        ps = (PA, PB)[(k - 1) % 2][:, 0:buckets]
                        dve.wait_ge(sig("before").sem, sig("before").at(t))
                        dve.tensor_tensor_reduce(ps, ps, oh[:, (k - 1) % 2, 0:buckets], 1.0, 0.0, ALU.mult, ALU.add,
                                                 rank_t[:, k - 1:k]).then_inc(sig("placed").sem, 1)
                    if k < BT:
                        dve.wait_ge(sig("hot").sem, sig("hot").at(t + 1 + T))
                        dve.wait_ge(sig("cum").sem, sig("cum").at(t + 1))
                        dve.tensor_tensor(cum[:, (k + 1) % 2, 0:buckets], cum[:, k % 2, 0:buckets],
                                          oh[:, k % 2, 0:buckets], ALU.add).then_inc(sig("cum").sem, 1)
                dve.wait_ge(sig("placed").sem, sig("placed").at((i + 1) * BT))
                waited(dve)
                dve.tensor_copy(rank[:, bass.ds(i * BT, BT)], rank_t[:, :]).then_inc(sig("ranked").sem, 1)
                dve.wait_ge(sig("ranked").sem, sig("ranked").at(i + 1))

        def rank_advance():
            advance("hot", 2 * T)
            advance("counted", T)
            advance("cum", T + 1)
            advance("before", T)
            advance("placed", T)
            advance("ranked", T // BT)

        def rank_to_row(dve, idx):
            link(dve, dve.tensor_copy(tmp_i[:, :], rank[:, :]))
            link(dve, dve.tensor_scalar(src_i[:, :], tmp_i[:, :], 7, None, ALU.arith_shift_right))
            link(dve, dve.tensor_copy(tmp_f[:, :], src_i[:, :]))
            link(dve, dve.scalar_tensor_tensor(key_f[:, :], tmp_f[:, :], -128.0, rank[:, :], ALU.mult, ALU.add))
            link(dve, dve.tensor_scalar(key_f[:, :], key_f[:, :], float(T), None, ALU.mult))
            link(dve, dve.scalar_tensor_tensor(key_f[:, :], tmp_f[:, :], float(Q), key_f[:, :], ALU.mult, ALU.add))
            for c in range(1, Q):
                link(dve, dve.tensor_scalar(rank[:, :], tmp_f[:, :], float(c * J), -float(Q * J - 1), ALU.is_ge, ALU.mult))
                link(dve, dve.tensor_tensor(key_f[:, :], key_f[:, :], rank[:, :], ALU.add))
            link(dve, dve.tensor_copy(idx[:, :].rearrange("p (j c) -> p c j", c=Q),
                                      key_f[:, :].rearrange("p (c j) -> p c j", c=Q)))

        ones_b = ctx.enter_context(nc.sbuf_tensor("ones_b", [P, P], BF16))

        def masks_pe(pe):
            with pe.Fori(0, EI) as i:
                pe.wait_ge(sig("m_rows").sem, sig("m_rows").at(i + 1))
                to_columns(pe, PA, cf, False).then_inc(sig("m_cols").sem, 1)
            with pe.Fori(0, EI) as i:
                pe.wait_ge(sig("m_last").sem, sig("m_last").at(i + 1))
                to_rows(pe, PA, ce, False).then_inc(sig("m_back").sem, 1)

        def masks_dve(dve):
            kt = arr_m
            with dve.Fori(0, EI) as i:
                dve.wait_ge(sig("m_cols").sem, sig("m_cols").at(i))
                dve.tensor_copy(ca[:, 0:UC], key_f[:, bass.ds(i * UC, UC)]).then_inc(sig("m_keys").sem, 1)
                dve.wait_ge(sig("m_keys").sem, sig("m_keys").at(i + 1))
                dve.tensor_copy(cf[:, 0:CW].rearrange("p (u f) -> p u f", f=D),
                                ca[:, 0:UC].unsqueeze(2).to_broadcast([P, UC, D])).then_inc(sig("m_rows").sem, 1)
                dve.wait_ge(sig("m_cols").sem, sig("m_cols").at(i + 1))
                waited(dve)
                dve.tensor_copy(kt[:, bass.ds(i * CW, CW)], PA[:, 0:CW]).then_inc(sig("m_kt").sem, 1)
            dve.wait_ge(sig("m_kt").sem, sig("m_kt").at(EI))
            link(dve, dve.memset(col[:, :], -1.0))
            for c in range(1, Q):
                link(dve, dve.tensor_copy(col[D * c:D * c + D, 0:1], kt[D * (c - 1):D * c, QE - 1:QE]))
            link(dve, dve.tensor_tensor(same[:, 1:QE], kt[:, 1:QE], kt[:, 0:QE - 1], ALU.is_equal))
            link(dve, dve.tensor_tensor(same[:, 0:1], kt[:, 0:1], col[:, 0:1], ALU.is_equal))
            link(dve, dve.tensor_tensor_scan(prefix[:, :], same[:, :], same[:, :], 1.0, ALU.mult, ALU.mult))
            link(dve, dve.memset(col[:, 1:2], 0.0))
            for c in range(1, Q):
                link(dve, dve.tensor_copy(col[D * (c - 1):D * c, 1:2], same[D * c:D * c + D, 0:1]))
            link(dve, dve.scalar_tensor_tensor(kt[:, 0:QE - 1], same[:, 1:QE], FAR, kt[:, 0:QE - 1], ALU.mult, ALU.add))
            link(dve, dve.scalar_tensor_tensor(kt[:, QE - 1:QE], col[:, 1:2], FAR, kt[:, QE - 1:QE], ALU.mult, ALU.add))
            link(dve, dve.memset(same[:, 0:1], 0.0))
            with dve.Fori(0, EI) as i:
                dve.wait_ge(sig("m_back").sem, sig("m_back").at(i))
                waited(dve)
                dve.tensor_copy(ce[:, 0:CW], kt[:, bass.ds(i * CW, CW)]).then_inc(sig("m_last").sem, 1)
                dve.wait_ge(sig("m_back").sem, sig("m_back").at(i + 1))
                waited(dve)
                dve.tensor_copy(last_f[:, bass.ds(i * UC, UC)],
                                PA[:, 0:CW].rearrange("p (u f) -> p u f", f=D)[:, :, 0]).then_inc(sig("m_lf").sem, 1)
            dve.wait_ge(sig("m_lf").sem, sig("m_lf").at(EI))

        def masks_advance():
            for name in ("m_rows", "m_cols", "m_last", "m_back", "m_keys", "m_kt", "m_lf"):
                advance(name, EI)

        def carry_over(dve, a, op_fix, neutral, mask):
            last = slice(QE - 1, QE)
            link(dve, dve.memset(col[:, 2:3], neutral))
            link(dve, dve.tensor_copy(col[:, 3:4], a[:, last]))
            link(dve, dve.tensor_copy(col[:, 4:5], mask[:, last]))
            for c in range(1, Q):
                q, b = slice(D * c, D * c + D), slice(D * (c - 1), D * c)
                link(dve, dve.tensor_copy(col[q, 2:3], col[b, 3:4]))
                link(dve, dve.scalar_tensor_tensor(col[q, 3:4], col[q, 4:5], col[q, 2:3], a[q, last], op_fix[0], op_fix[1]))
            link(dve, dve.scalar_tensor_tensor(a[:, 0:QE], mask[:, 0:QE], col[:, 2:3], a[:, 0:QE], op_fix[0], op_fix[1]))

        COMPUTE = """turns ln_squared ln_sum ln_dev ln_inv gates gate_r gate_z cand_h cand gate_n
            h_minus_n z_part h_new dve_link hot cum counted before placed m_rows m_cols m_last m_back m_keys m_kt m_lf
            edge_rows in_cols y_ready out_rows rows_ready stored x_cols x1_max l0_cols l0_s l0_d l0_h l0_y l0_hl l0_v
            l0_yv l0_done ea_rows ea_cols split hd_ready sel_cols z_ready z_used msg_saved 
            h_saved packed ranked""".split()

        for name in COMPUTE:
            sig(name)
        with nc.Block() as block:
            @block.sync
            def _(sp):
                for name in COMPUTE:
                    sp.sem_inc(signals[name].sem, 2)

        with nc.Block() as block:
            @block.sync
            def _(sp):
                for dst, source in ((w, weights), (bias, biases), (sel, sel_h), (triu, triu_h), (iota, iota_h),
                                    (slots, slot_h), (src_i, src_pu), (dst_i, dst_pu)):
                    sp.dma_start(dst[:, :], source).then_inc(sig("d_const").sem, 16)
                sp.dma_start(arr_s[:, 0:T * EC], ea_pu.rearrange("p t k -> p (t k)")).then_inc(sig("d_const").sem, 16)
                sp.wait_ge(sig("edge_rows").sem, sig("edge_rows").at(1))
                sp.dma_start(edges0, arr_d[:, 0:T * RW].rearrange("p (t w) -> p t w", w=RW)).then_inc(sig("d_out").sem, 16)
                sp.wait_ge(sig("d_out").sem, 16)

            @block.vector
            def _(dve):
                dve.wait_ge(sig("d_const").sem, 9 * 16)
                er = arr_d[:, 0:T * RW].rearrange("p (t w) -> p t w", w=RW)
                link(dve, dve.memset(arr_d[:, 0:T * RW], 0.0))
                link(dve, dve.memset(ones_b[:, :], 1.0))
                link(dve, dve.tensor_copy(src_f[:, :], src_i[:, :]))
                link(dve, dve.tensor_copy(dst_f[:, :], dst_i[:, :]))
                link(dve, dve.tensor_copy(er[:, :, 0], src_f[:, :]))
                link(dve, dve.tensor_copy(er[:, :, 1], dst_f[:, :]))
                link(dve, dve.tensor_copy(er[:, :, 2:2 + EC], arr_s[:, 0:T * EC].rearrange("p (t k) -> p t k", k=EC)))
                dve.sem_inc(sig("edge_rows").sem, 1)
                link(dve, dve.tensor_scalar(tmp_f[:, :], src_f[:, :], float(N - 1), None, ALU.min))
                link(dve, dve.tensor_copy(idx_a[:, :], tmp_f[:, :]))
                link(dve, dve.tensor_scalar(tmp_f[:, :], dst_f[:, :], float(N - 1), None, ALU.min))
                link(dve, dve.tensor_copy(idx_b[:, :], tmp_f[:, :]))
                link(dve, dve.tensor_scalar(tmp_i[:, :], src_i[:, :], LOW - 1, None, ALU.bitwise_and))
                link(dve, dve.tensor_copy(digit[:, :].rearrange("p (c j) -> p c j", c=Q), by_tile(tmp_i)))
                link(dve, dve.tensor_tensor(bias[:, B_R:B_R + 2], bias[:, B_R:B_R + 2], bias[:, B_RH:B_RH + 2], ALU.add))
                link(dve, dve.memset(rows_o[:, :], FAR))

        advance("d_const", 9 * 16)
        advance("d_out", 16)
        advance("edge_rows", 1)

        def cols(a, i, width=CW):
            return a[:, bass.ds(i * width, width)]

        def stream_sp(sp, n, load, store, n_out=1):
            def put(i):
                sp.wait_ge(sig("rows_ready").sem, sig("rows_ready").at(i + 1))
                store(sp, i).then_inc(sig("d_out").sem, 16)
                sp.wait_ge(sig("d_out").sem, sig("d_out").at((i + 1) * 16))
                sp.sem_inc(sig("stored").sem, 1)

            if load is not None:
                load(sp, 0).then_inc(sig("d_in").sem, 16)
            with sp.Fori(0, n - 1) as i:
                if load is not None:
                    sp.wait_ge(sig("in_cols").sem, sig("in_cols").at(i + 1))
                    load(sp, i + 1).then_inc(sig("d_in").sem, 16)
                if store is not None:
                    put(i)
            if store is not None:
                put(n - 1)

        def stream_advance(n, load, store):
            if load:
                advance("d_in", 16 * n)
                advance("in_cols", n)
            if store:
                advance("d_out", 16 * n)
                advance("stored", n)
                advance("rows_ready", n)
                advance("out_rows", n)

        def x_nodes(ap, i):
            return ap.rearrange("(p n) d -> p n d", p=NP)[:, bass.ds(i * NC, NC), :]

        def rows_out(act, i, ps, width, dense):
            act.wait_ge(sig("out_rows").sem, sig("out_rows").at(i + 1))
            act.wait_ge(sig("stored").sem, sig("stored").at(i))
            source = ps[0:NP, 0:NG * P] if dense else ps[:, 0:CW]
            act.activation(rows_view(rows_o, width, dense)[:, :, 0:D], source.rearrange("p (n w) -> p n w", w=D),
                           ACT.Copy).then_inc(sig("rows_ready").sem, 1)

        def chunks(eng, n, body):
            with eng.Fori(0, n - 1) as i:
                body(i, True)
            body(n - 1, False)

        def act_store(act, i, target, source):
            act.wait_ge(sig("rows_ready").sem, sig("rows_ready").at(i + 1))
            act.dma_start(target, source).then_inc(sig("d_out").sem, 16)
            act.wait_ge(sig("d_out").sem, sig("d_out").at((i + 1) * 16))
            act.sem_inc(sig("stored").sem, 1)

        def edge_rows_of(ap, i):
            return ap[:, bass.ds(i * UC, UC), :]

        g_src = RingPass(idx_a, x, D, N - 1, store=back(l0_src_rows), stored=1)
        g_dst = RingPass(idx_b, x, D, N - 1, store=back(l0_dst_rows), stored=1)
        with nc.Block() as block:
            @block.gpsimd
            def _(pool):
                g_src.pool(pool)
                g_dst.pool(pool)

            @block.sync
            def _(sp):
                g_src.sp(sp)
                g_dst.sp(sp)

            @block.tensor
            def _(pe):
                rank_pe(pe, LOW)
                masks_pe(pe)
                with pe.Fori(0, NI) as i:
                    pe.wait_ge(sig("y_ready").sem, sig("y_ready").at(i + 1))
                    to_columns(pe, PA, cf, True).then_inc(sig("in_cols").sem, 1)
                    pe.wait_ge(sig("x_cols").sem, sig("x_cols").at(i + 1))
                    pe.wait_ge(sig("rows_ready").sem, sig("rows_ready").at(i))
                    to_rows(pe, PC, cg, True, centred=True).then_inc(sig("out_rows").sem, 1)

            @block.scalar
            def _(act):
                def load(i):
                    act.dma_start(rows_view(rows, D, True), x_nodes(x, i)).then_inc(sig("d_in").sem, 16)

                def body(i, more):
                    act.wait_ge(sig("in_cols").sem, sig("in_cols").at(i + 1))
                    if more:
                        load(i + 1)
                    act.activation(bv(cg, True), pv(PA, True), ACT.Copy).then_inc(sig("x_cols").sem, 1)
                    ln_act(act, i, True)
                    act_store(act, i, x_nodes(table, i), rows_view(rows_o, TW, True))
                load(0)
                chunks(act, NI, body)

            @block.vector
            def _(dve):
                rank_dve(dve, LOW)
                rank_to_row(dve, idx_c)
                link(dve, dve.tensor_copy(key_f[:, :], dst_f[:, :]))
                masks_dve(dve)
                link(dve, dve.tensor_scalar(same[:, :], same[:, :], -1.0, BIG, ALU.add, ALU.mult))
                link(dve, dve.tensor_scalar(prefix[:, :], prefix[:, :], -1.0, BIG, ALU.add, ALU.mult))
                link(dve, dve.memset(rows_o[:, :], FAR))
                with dve.Fori(0, NI) as i:
                    dve.wait_ge(sig("d_in").sem, sig("d_in").at((i + 1) * 16))
                    dve.wait_ge(sig("in_cols").sem, sig("in_cols").at(i))
                    dve.scalar_tensor_tensor(cf[0:NP, 0:NC * D], rows[0:NP, 0:NC * D], 0.0, rows[0:NP, 0:NC * D],
                                             ALU.max, ALU.add).then_inc(sig("y_ready").sem, 1)
                    ln_dve(dve, i, TW, True)
        rank_advance()
        masks_advance()
        stream_advance(NI, True, True)
        advance("x_cols", NI)
        advance("y_ready", NI)
        ln_advance(NI)

        sort_low = RingPass(idx_c, edges1, RW, EP - 1, scatter=True, load_from=edges0)

        def maximum_x1(dve):
            link(dve, dve.tensor_tensor_scan(arr_m[:, 0:QE], same[:, :], arr_m[:, 0:QE], -BIG, ALU.add, ALU.max))
            carry_over(dve, arr_m, (ALU.add, ALU.max), -BIG, prefix)

        with nc.Block() as block:
            @block.gpsimd
            def _(pool):
                sort_low.pool(pool)

            @block.sync
            def _(sp):
                sort_low.sp(sp)

            @block.scalar
            def _(act):
                def load(i):
                    act.dma_start(rows[:, 0:CW].rearrange("p (u d) -> p u d", d=D),
                                  l0_src_rows[:, bass.ds(i * UC, UC), :]).then_inc(sig("d_l0").sem, 16)
                    act.dma_start(rows_b[:, 0:CW].rearrange("p (u d) -> p u d", d=D),
                                  l0_dst_rows[:, bass.ds(i * UC, UC), :]).then_inc(sig("d_l0").sem, 16)
                    act.dma_start(ce[0:Q * EC, 0:CW], ea_t[:, bass.ds(i * CW, CW)]).then_inc(sig("d_l0").sem, 16)
                with act.Fori(0, EI) as i:
                    act.wait_ge(sig("l0_h").sem, sig("l0_h").at(i))
                    load(i)
                    act.wait_ge(sig("l0_cols").sem, sig("l0_cols").at(i + 1))
                    act.activation(ca[:, 0:CW], PA[:, 0:CW], ACT.Copy).then_inc(sig("l0_s").sem, 1)
                    act.wait_ge(sig("l0_h").sem, sig("l0_h").at(i + 1))
                    act.activation(cc[:, 0:CW], PC[:, 0:CW], ACT.Identity, bias=B(B_1A))
                    act.activation(cd[:, 0:CW], PD[:, 0:CW], ACT.Identity, bias=B(B_1B)).then_inc(sig("l0_y").sem, 1)
                    act.wait_ge(sig("l0_v").sem, sig("l0_v").at(i + 1))
                    act.activation(cg[:, 0:CW], PA[:, 0:CW], ACT.Identity, bias=B(B_2)).then_inc(sig("l0_yv").sem, 1)
                with act.Fori(0, EI) as i:
                    ln_act(act, i, False)
                    act_store(act, i, edge_rows_of(x1_rows, i), rows_view(rows_o, TW, False))

            @block.tensor
            def _(pe):
                with pe.Fori(0, EI) as i:
                    pe.wait_ge(sig("d_l0").sem, sig("d_l0").at((i + 1) * 48))
                    to_columns(pe, PA, rows, False)
                    to_columns(pe, PB, rows_b, False).then_inc(sig("l0_cols").sem, 1)
                    pe.wait_ge(sig("l0_s").sem, sig("l0_s").at(i + 1))
                    pe.wait_ge(sig("l0_d").sem, sig("l0_d").at(i + 1))
                    for pair, ps in enumerate((PC, PD)):
                        for half in range(2):
                            o, xs = halves(ps, ca, False)[half]
                            xd, ea = halves(ps, cb, False)[half][1], halves(ps, ce, False)[half][1]
                            pe.matmul(o, W(L0S + pair), xs, start=True, stop=False)
                            pe.matmul(o, W(L0D + pair), xd, start=False, stop=False)
                            ins = pe.matmul(o, W(L0E + pair, Q * EC), ea[0:Q * EC, :], start=False, stop=True)
                    ins.then_inc(sig("l0_h").sem, 1)
                    pe.wait_ge(sig("l0_hl").sem, sig("l0_hl").at(i + 1))
                    for half in range(2):
                        o, ha = halves(PA, rows_o, False)[half]
                        pe.matmul(o, W(L0V), ha, start=True, stop=False)
                        ins = pe.matmul(o, W(L0V + 1), halves(PA, cf, False)[half][1], start=False, stop=True)
                    ins.then_inc(sig("l0_v").sem, 1)
                    pe.wait_ge(sig("l0_yv").sem, sig("l0_yv").at(i + 1))
                with pe.Fori(0, EI) as i:
                    pe.wait_ge(sig("y_ready").sem, sig("y_ready").at(i + 1))
                    pe.wait_ge(sig("rows_ready").sem, sig("rows_ready").at(i))
                    to_rows(pe, PC, cf, False, centred=True).then_inc(sig("out_rows").sem, 1)

            @block.vector
            def _(dve):
                with dve.Fori(0, EI) as i:
                    dve.wait_ge(sig("l0_cols").sem, sig("l0_cols").at(i + 1))
                    dve.tensor_copy(cb[:, 0:CW], PB[:, 0:CW]).then_inc(sig("l0_d").sem, 1)
                    dve.tensor_copy(cols(arr_d, i), PB[:, 0:CW])
                    dve.wait_ge(sig("l0_y").sem, sig("l0_y").at(i + 1))
                    dve.scalar_tensor_tensor(rows_o[:, 0:CW], cc[:, 0:CW], 0.01, cc[:, 0:CW], ALU.mult, ALU.max)
                    dve.scalar_tensor_tensor(cf[:, 0:CW], cd[:, 0:CW], 0.01, cd[:, 0:CW], ALU.mult, ALU.max)\
                       .then_inc(sig("l0_hl").sem, 1)
                    dve.wait_ge(sig("l0_yv").sem, sig("l0_yv").at(i + 1))
                    dve.scalar_tensor_tensor(cols(arr_m, i), cg[:, 0:CW], 0.01, cg[:, 0:CW], ALU.mult, ALU.max)\
                       .then_inc(sig("l0_done").sem, 1)
                dve.wait_ge(sig("l0_done").sem, sig("l0_done").at(EI))
                link(dve, dve.memset(rows_o[:, :], FAR))
                maximum_x1(dve)
                with dve.Fori(0, EI) as i:
                    dve.tensor_tensor(cb[:, 0:CW], cols(arr_m, i), cols(arr_d, i), ALU.max).then_inc(sig("x1_max").sem, 1)
                    dve.wait_ge(sig("x1_max").sem, sig("x1_max").at(i + 1))
                    dve.tensor_tensor(cf[:, 0:CW], cb[:, 0:CW], cols(arr_d, i), ALU.add).then_inc(sig("y_ready").sem, 1)
                    ln_dve(dve, i, TW, False)
                link(dve, dve.tensor_copy(idx_a[:, :], last_f[:, :]))
        advance("d_l0", 48 * EI)
        for name in ("l0_cols", "l0_s", "l0_d", "l0_h", "l0_y", "l0_hl", "l0_v", "l0_yv", "l0_done", "x1_max", "y_ready"):
            advance(name, EI)
        stream_advance(EI, False, True)
        ln_advance(EI)

        put_x1 = RingPass(idx_a, table, TW, N - 1, scatter=True, load_from=x1_rows)
        with nc.Block() as block:
            @block.gpsimd
            def _(pool):
                put_x1.pool(pool)

            @block.sync
            def _(sp):
                put_x1.sp(sp)

            @block.scalar
            def _(act):
                act.dma_start(arr_s[:, 0:T * RW], edges1.rearrange("(p u) w -> p (u w)", p=P)).then_inc(sig("d_const").sem, 16)

            @block.tensor
            def _(pe):
                rank_pe(pe, HIGH)

            @block.vector
            def _(dve):
                dve.wait_ge(sig("d_const").sem, sig("d_const").at(16))
                link(dve, dve.tensor_copy(src_i[:, :], arr_s[:, 0:T * RW].rearrange("p (t w) -> p t w", w=RW)[:, :, 0]))
                link(dve, dve.tensor_scalar(tmp_i[:, :], src_i[:, :], LOW.bit_length() - 1, None, ALU.arith_shift_right))
                link(dve, dve.tensor_copy(digit[:, :].rearrange("p (c j) -> p c j", c=Q), by_tile(tmp_i)))
                rank_dve(dve, HIGH)
                rank_to_row(dve, idx_c)
        advance("d_const", 16)
        rank_advance()

        def dense_pe(pe, first, n):
            with pe.Fori(0, n) as i:
                pe.wait_ge(sig("packed").sem, sig("packed").at(i + 1))
                to_columns(pe, PA, cf, True).then_inc(sig("in_cols").sem, 1)
                for t in range(STEPS):
                    def state_ready(half):
                        if t:
                            m = (i * STEPS + t - 1) * 2 + half
                            pe.wait_ge(sig("h_new").sem, sig("h_new").at(m + 1))
                        elif half == 0:
                            pe.wait_ge(sig("x_cols").sem, sig("x_cols").at(i + 1))
                            pe.wait_ge(sig("rows_ready").sem, sig("rows_ready").at(i))
                    gru_pe(pe, i * STEPS + t, lambda half: half_of(cf if t else cg, half, True), None, True, state_ready)
                pe.wait_ge(sig("y_ready").sem, sig("y_ready").at(i + 1))
                to_rows(pe, PC, cb, True, centred=True).then_inc(sig("out_rows").sem, 1)

        def dense_act(act, first, n):
            def load(i):
                act.dma_start(rows_view(rows, TW, True), x_nodes(table, i + first)).then_inc(sig("d_in").sem, 16)

            def body(i, more):
                act.wait_ge(sig("d_in").sem, sig("d_in").at((i + 1) * 16))
                act.activation(rows_view(cf, D, True), rows_view(rows, TW, True)[:, :, 0:D], ACT.Copy)\
                   .then_inc(sig("packed").sem, 1)
                if more:
                    act.wait_ge(sig("packed").sem, sig("packed").at(i + 1))
                    load(i + 1)
                act.wait_ge(sig("in_cols").sem, sig("in_cols").at(i + 1))
                act.activation(bv(cg, True), pv(PA, True), ACT.Copy).then_inc(sig("x_cols").sem, 1)
                for t in range(STEPS):
                    gru_act(act, i * STEPS + t, True)
                ln_act(act, i, True)
                act_store(act, i, x_nodes(out, i + first), rows_view(rows_o, D, True))
            load(0)
            chunks(act, n, body)

        def dense_dve(dve, first, n):
            with dve.Fori(0, n) as i:
                for t in range(STEPS):
                    gru_dve(dve, i * STEPS + t, lambda half: half_of(cf if t else cg, half, True), False, True)
                dve.wait_ge(sig("h_new").sem, sig("h_new").at(i * (2 * STEPS) + 2 * STEPS))
                dve.tensor_tensor(bv(cb, True), bv(cf, True), bv(cg, True), ALU.add).then_inc(sig("y_ready").sem, 1)
                ln_dve(dve, i, D, True)

        def dense_advance(n):
            stream_advance(n, True, True)
            for name in ("x_cols", "packed", "y_ready"):
                advance(name, n)
            gru_advance(n * STEPS, False)
            ln_advance(n)

        def beside_dense(ring_pass, first, n):
            with nc.Block() as block:
                @block.gpsimd
                def _(pool):
                    ring_pass.pool(pool)

                @block.sync
                def _(sp):
                    ring_pass.sp(sp)

                @block.tensor
                def _(pe):
                    dense_pe(pe, first, n)

                @block.scalar
                def _(act):
                    dense_act(act, first, n)

                @block.vector
                def _(dve):
                    dense_dve(dve, first, n)
            dense_advance(n)

        sort_high = RingPass(idx_c, edges2, RW, EP - 1, scatter=True, load_from=edges1.rearrange("(p u) w -> p u w", p=P))
        beside_dense(sort_high, 0, SPLIT[0])

        sorted_rows = arr_s[:, 0:T * RW].rearrange("p (t w) -> p t w", w=RW)
        with nc.Block() as block:
            @block.sync
            def _(sp):
                sp.dma_start(arr_s[:, 0:T * RW], edges2.rearrange("(p u) w -> p (u w)", p=P)).then_inc(sig("d_const").sem, 16)

            @block.tensor
            def _(pe):
                masks_pe(pe)

            @block.vector
            def _(dve):
                dve.wait_ge(sig("d_const").sem, sig("d_const").at(16))
                link(dve, dve.tensor_copy(key_f[:, :], sorted_rows[:, :, 0]))
                link(dve, dve.tensor_copy(dst_f[:, :], sorted_rows[:, :, 1]))
                link(dve, dve.tensor_scalar(tmp_f[:, :], key_f[:, :], float(N - 1), None, ALU.min))
                link(dve, dve.tensor_copy(idx_a[:, :], tmp_f[:, :]))
                link(dve, dve.tensor_scalar(tmp_f[:, :], dst_f[:, :], float(N - 1), None, ALU.min))
                link(dve, dve.tensor_copy(idx_b[:, :], tmp_f[:, :]))
                masks_dve(dve)
                link(dve, dve.tensor_copy(idx_c[:, :], last_f[:, :]))
                link(dve, dve.tensor_scalar(tmp_f[:, :], last_f[:, :], float(TW), float(D), ALU.mult, ALU.add))
                link(dve, dve.tensor_copy(tmp_i[:, :], tmp_f[:, :]))
        advance("d_const", 16)
        masks_advance()

        put_slots = RingPass(tmp_i, table_words, 1, N * TW - 1, scatter=True, load_from=slots[:, :].unsqueeze(2))
        with nc.Block() as block:
            @block.gpsimd
            def _(pool):
                put_slots.pool(pool)

            @block.sync
            def _(sp):
                put_slots.sp(sp)

            @block.tensor
            def _(pe):
                with pe.Fori(0, EI) as i:
                    pe.wait_ge(sig("ea_rows").sem, sig("ea_rows").at(i + 1))
                    waited(pe)
                    for j in range(JC):
                        ins = pe.transpose(PA[0:Q * EC, j * P:(j + 1) * P], ca[:, j * Q * EC:(j + 1) * Q * EC], W(IDENT))
                    ins.then_inc(sig("ea_cols").sem, 1)

            @block.vector
            def _(dve):
                half = slice(0, Q * EC)
                with dve.Fori(0, EI) as i:
                    dve.wait_ge(sig("ea_cols").sem, sig("ea_cols").at(i))
                    waited(dve)
                    dve.tensor_copy(ca[:, 0:UC * EC].rearrange("p (u k) -> p u k", k=EC),
                                    sorted_rows[:, bass.ds(i * UC, UC), 2:2 + EC]).then_inc(sig("ea_rows").sem, 1)
                    dve.wait_ge(sig("ea_cols").sem, sig("ea_cols").at(i + 1))
                    n = 6
                    dve.tensor_copy(ea_hm[half, bass.ds(i * CW, CW)], PA[half, 0:CW]).then_inc(sig("split").sem, 1)
                    dve.wait_ge(sig("split").sem, sig("split").at(i * n + 1))
                    dve.tensor_tensor(cb[half, 0:CW], PA[half, 0:CW], ea_hm[half, bass.ds(i * CW, CW)],
                                      ALU.subtract).then_inc(sig("split").sem, 1)
                    dve.wait_ge(sig("split").sem, sig("split").at(i * n + 2))
                    waited(dve)
                    dve.tensor_copy(ea_lo[:, bass.ds(i * CW, CW)], cb[half, 0:CW]).then_inc(sig("split").sem, 1)
                    dve.wait_ge(sig("split").sem, sig("split").at(i * n + 3))
                    dve.tensor_tensor(cc[half, 0:CW], cb[half, 0:CW], ea_lo[:, bass.ds(i * CW, CW)],
                                      ALU.subtract).then_inc(sig("split").sem, 1)
                    dve.tensor_copy(ea_hm[Q * EC:P, bass.ds(i * CW, CW)], ea_lo[:, bass.ds(i * CW, CW)])\
                       .then_inc(sig("split").sem, 1)
                    dve.wait_ge(sig("split").sem, sig("split").at(i * n + 5))
                    waited(dve)
                    dve.tensor_copy(ea_lo[:, bass.ds(i * CW, CW)], cc[half, 0:CW]).then_inc(sig("split").sem, 1)
        advance("ea_rows", EI)
        advance("ea_cols", EI)
        advance("split", 6 * EI)

        g_nbr = RingPass(idx_b, table, TW, N - 1, store=back_with_slot(dst_rows), stored=2)
        beside_dense(g_nbr, SPLIT[0], SPLIT[1])
        g_own = RingPass(idx_a, table, TW, N - 1, store=back(src_rows, TW), stored=1)
        beside_dense(g_own, SPLIT[0] + SPLIT[1], SPLIT[2])

        def messages_act(act, neighbours, gathered):
            def load(i):
                gathered(i)
                act.dma_start(rows_view(rows, D, False), edge_rows_of(neighbours, i)).then_inc(sig("d_in").sem, 16)

            def body(i, more):
                act.wait_ge(sig("in_cols").sem, sig("in_cols").at(i + 1))
                act.wait_ge(sig("z_used").sem, sig("z_used").at(i * EC))
                act.activation(cg[:, 0:CW], PA[:, 0:CW], ACT.Copy).then_inc(sig("hd_ready").sem, 1)
                if more:
                    load(i + 1)
            load(0)
            chunks(act, EI, body)

        def messages_pe(pe):
            def attributes(i, k):
                ps = (PB, PC)[k % 2]
                for a, b in ((0, 512), (512, CW)):
                    pe.matmul(ps[:, a:b], sel[:, k * P:(k + 1) * P], ea_hm[:, bass.ds(i * CW + a, b - a)],
                              start=True, stop=False)
                    ins = pe.matmul(ps[:, a:b], sel[0:Q * EC, k * P:(k + 1) * P],
                                    ea_lo[:, bass.ds(i * CW + a, b - a)], start=False, stop=True)
                ins.then_inc(sig("sel_cols").sem, 1)

            with pe.Fori(0, EI) as i:
                attributes(i, 0)
                attributes(i, 1)
                pe.wait_ge(sig("d_in").sem, sig("d_in").at((i + 1) * 16))
                to_columns(pe, PA, rows, False).then_inc(sig("in_cols").sem, 1)
                pe.wait_ge(sig("hd_ready").sem, sig("hd_ready").at(i + 1))
                pe.wait_ge(sig("msg_saved").sem, sig("msg_saved").at(i))
                for o, h in halves(PD, cg, False):
                    pe.matmul(o, W(WB + EC), h, start=True, stop=False)
                for k in range(EC):
                    pe.wait_ge(sig("z_ready").sem, sig("z_ready").at(i * EC + k + 1))
                    if k + 2 < EC:
                        attributes(i, k + 2)
                    for o, z in halves(PD, (ca, cb)[k % 2], False):
                        ins = pe.matmul(o, W(WB + k), z, start=False, stop=(k == EC - 1))
                    ins.then_inc(sig("z_used").sem, 1)

        def messages_dve(dve):
            with dve.Fori(0, EI) as i:
                dve.wait_ge(sig("hd_ready").sem, sig("hd_ready").at(i + 1))
                for k in range(EC):
                    dve.wait_ge(sig("sel_cols").sem, sig("sel_cols").at(i * EC + k + 1))
                    dve.wait_ge(sig("z_used").sem, sig("z_used").at(i * EC + k - 1))
                    dve.tensor_tensor((ca, cb)[k % 2][:, 0:CW], (PB, PC)[k % 2][:, 0:CW], cg[:, 0:CW],
                                      ALU.mult).then_inc(sig("z_ready").sem, 1)
                dve.wait_ge(sig("z_used").sem, sig("z_used").at((i + 1) * EC))
                waited(dve)
                dve.tensor_copy(cols(arr_m, i), PD[:, 0:CW]).then_inc(sig("msg_saved").sem, 1)
            dve.wait_ge(sig("msg_saved").sem, sig("msg_saved").at(EI))
            link(dve, dve.tensor_tensor_scan(arr_m[:, 0:QE], same[:, :], arr_m[:, 0:QE], 0.0, ALU.mult, ALU.add))
            carry_over(dve, arr_m, (ALU.mult, ALU.add), 0.0, prefix)

        def messages_advance():
            stream_advance(EI, True, False)
            for name, n in (("hd_ready", 1), ("sel_cols", EC), ("z_ready", EC), ("z_used", EC), ("msg_saved", 1)):
                advance(name, n * EI)

        with nc.Block() as block:
            @block.tensor
            def _(pe):
                with pe.Fori(0, EI) as i:
                    pe.wait_ge(sig("d_in").sem, sig("d_in").at((i + 1) * 16))
                    to_columns(pe, PA, rows, False).then_inc(sig("in_cols").sem, 1)
                    for t in range(STEPS - 1):
                        def state_ready(half):
                            if t:
                                m = (i * (STEPS - 1) + t - 1) * 2 + half
                                pe.wait_ge(sig("h_new").sem, sig("h_new").at(m + 1))
                            elif half == 0:
                                pe.wait_ge(sig("x_cols").sem, sig("x_cols").at(i + 1))
                        gru_pe(pe, i * (STEPS - 1) + t, lambda half: half_of(cf if t else cg, half, False), None, False,
                               state_ready)
                        pe.wait_ge(sig("h_new").sem, sig("h_new").at((i * (STEPS - 1) + t) * 2 + 2))
                        pe.wait_ge(sig("rows_ready").sem, sig("rows_ready").at(i * (STEPS - 1) + t))
                        to_rows(pe, PD, cf, False).then_inc(sig("out_rows").sem, 1)

            @block.scalar
            def _(act):
                def load(i):
                    act.dma_start(rows_view(rows, D, False), edge_rows_of(dst_rows, i)).then_inc(sig("d_in").sem, 16)

                def body(i, more):
                    act.wait_ge(sig("in_cols").sem, sig("in_cols").at(i + 1))
                    if more:
                        load(i + 1)
                    act.activation(cg[:, 0:CW], PA[:, 0:CW], ACT.Copy).then_inc(sig("x_cols").sem, 1)
                    for t in range(STEPS - 1):
                        m = i * (STEPS - 1) + t
                        gru_act(act, m, False)
                        rows_out(act, m, PD, D, False)
                        act_store(act, m, edge_rows_of(alone_rows[t], i), rows_view(rows_o, D, False))
                load(0)
                chunks(act, EI, body)

            @block.vector
            def _(dve):
                link(dve, dve.tensor_copy(idx_b[:, :], slot_f[:, :]))
                with dve.Fori(0, EI) as i:
                    for t in range(STEPS - 1):
                        dve.wait_ge(sig("out_rows").sem, sig("out_rows").at(i * (STEPS - 1) + t))
                        gru_dve(dve, i * (STEPS - 1) + t, lambda half: half_of(cf if t else cg, half, False), False, False)
        stream_advance(EI, True, False)
        stream_advance(EI * (STEPS - 1), False, True)
        advance("x_cols", EI)
        gru_advance(EI * (STEPS - 1), False)

        for step in range(STEPS):
            final = step == STEPS - 1
            g_state = RingPass(idx_b, state, D, EP - 1, load_from=alone_rows[step - 1], store=back(nbr_rows), stored=1) \
                if step else None
            with nc.Block() as block:
                if step:
                    @block.gpsimd
                    def _(pool):
                        g_state.pool(pool)

                    @block.sync
                    def _(sp):
                        g_state.sp(sp)

                @block.scalar
                def _(act):
                    def gathered(i):
                        if step:
                            for h in range(2):
                                act.wait_ge(sig(f"d_stored{h}").sem, (i + 1) * 16 + g_state.base[f"d_stored{h}"])
                    messages_act(act, nbr_rows if step else dst_rows, gathered)

                @block.tensor
                def _(pe):
                    messages_pe(pe)

                @block.vector
                def _(dve):
                    messages_dve(dve)
            messages_advance()

            if step == 0:
                with nc.Block() as block:
                    @block.sync
                    def _(sp):
                        stream_sp(sp, EI, lambda sp, i: sp.dma_start(rows_view(rows, D, False), edge_rows_of(src_rows, i)), None)

                    @block.tensor
                    def _(pe):
                        with pe.Fori(0, EI) as i:
                            pe.wait_ge(sig("d_in").sem, sig("d_in").at((i + 1) * 16))
                            pe.wait_ge(sig("x_cols").sem, sig("x_cols").at(i))
                            to_columns(pe, PA, rows, False).then_inc(sig("in_cols").sem, 1)

                    @block.vector
                    def _(dve):
                        with dve.Fori(0, EI) as i:
                            dve.wait_ge(sig("in_cols").sem, sig("in_cols").at(i + 1))
                            waited(dve)
                            dve.tensor_copy(cols(arr_s, i), PA[:, 0:CW]).then_inc(sig("x_cols").sem, 1)
                stream_advance(EI, True, False)
                advance("x_cols", EI)

            with nc.Block() as block:
                @block.sync
                def _(sp):
                    stream_sp(sp, EI, (lambda sp, i: sp.dma_start(rows_view(rows, D, False), edge_rows_of(src_rows, i)))
                              if final else None,
                              lambda sp, i: sp.dma_start(edge_rows_of(final_rows if final else state_rows, i),
                                                         rows_view(rows_o, D, False)))

                @block.scalar
                def _(act):
                    with act.Fori(0, EI) as i:
                        gru_act(act, i, False)
                        if final:
                            ln_act(act, i, False)
                        else:
                            act.wait_ge(sig("h_new").sem, sig("h_new").at(i * 2 + 2))
                            waited(act)
                            act.activation(cols(arr_s, i), cf[:, 0:CW], ACT.Copy).then_inc(sig("h_saved").sem, 1)
                            rows_out(act, i, PC, D, False)

                @block.tensor
                def _(pe):
                    with pe.Fori(0, EI) as i:
                        def half_cols(a):
                            return lambda half: a[:, bass.ds(i * CW + 512 * half, (512, CW - 512)[half])]
                        pe.wait_ge(sig("rows_ready").sem, sig("rows_ready").at(i))
                        gru_pe(pe, i, half_cols(arr_s), half_cols(arr_m), False, lambda half: None)
                        pe.wait_ge(sig("h_new").sem, sig("h_new").at(i * 2 + 2))
                        if final:
                            pe.wait_ge(sig("d_in").sem, sig("d_in").at((i + 1) * 16))
                            to_columns(pe, PB, rows, False).then_inc(sig("in_cols").sem, 1)
                            pe.wait_ge(sig("y_ready").sem, sig("y_ready").at(i + 1))
                        to_rows(pe, PC, cb if final else cf, False, centred=final).then_inc(sig("out_rows").sem, 1)

                @block.vector
                def _(dve):
                    with dve.Fori(0, EI) as i:
                        dve.wait_ge(sig("out_rows").sem, sig("out_rows").at(i))
                        if not final:
                            dve.wait_ge(sig("h_saved").sem, sig("h_saved").at(i))
                        gru_dve(dve, i, lambda half: arr_s[:, bass.ds(i * CW + 512 * half, (512, CW - 512)[half])],
                                True, False)
                        if final:
                            dve.wait_ge(sig("h_new").sem, sig("h_new").at(i * 2 + 2))
                            dve.wait_ge(sig("in_cols").sem, sig("in_cols").at(i + 1))
                            dve.tensor_tensor(cb[:, 0:CW], cf[:, 0:CW], PB[:, 0:CW], ALU.add).then_inc(sig("y_ready").sem, 1)
                            ln_dve(dve, i, D, False)
            stream_advance(EI, final, True)
            gru_advance(EI, True)
            if final:
                advance("y_ready", EI)
                ln_advance(EI)
            else:
                advance("h_saved", EI)

        put_out = RingPass(idx_c, out, D, N - 1, scatter=True, load_from=final_rows)
        with nc.Block() as block:
            @block.gpsimd
            def _(pool):
                put_out.pool(pool)

            @block.sync
            def _(sp):
                put_out.sp(sp)


def kernel(**inputs):
    import concourse.bacc as _bacc
    import ml_dtypes
    from concourse.bass_utils import run_bass_kernel_spmd as _run

    def get(name):
        return np.asarray(inputs[name])

    def by_slot(a, fill):
        full = np.full((EP,) + a.shape[1:], fill, a.dtype)
        full[:E] = a
        full = full.reshape((Q, J, P) + a.shape[1:])
        return np.ascontiguousarray(np.moveaxis(full, 2, 0).swapaxes(1, 2)).reshape((P, T) + a.shape[1:])

    ea = get("edge_attr_16")
    ea_t = np.zeros((EP, EC), np.float32)
    ea_t[:E] = ea
    ea_t = np.ascontiguousarray(ea_t.reshape(Q, QE, EC).transpose(0, 2, 1)).reshape(Q * EC, QE)

    w = np.zeros((P, NW, P), np.float32)
    w_ih, w_hh = get("L1_gnn_W_ih"), get("L1_gnn_W_hh")
    w_bond, b_bond = get("L1_gnn_W_bond").reshape(EC, D, D), get("L1_gnn_b_bond").reshape(D, D)
    w1, w2 = get("L0_gnn_W1"), get("L0_gnn_W2")
    for c in range(Q):
        q = slice(c * D, c * D + D)
        for g in range(3):
            w[q, IH + g, q] = w_ih[g * D:(g + 1) * D].T
            w[q, HH + g, q] = w_hh[g * D:(g + 1) * D].T
        for k in range(EC):
            w[q, WB + k, q] = w_bond[k].T
        w[q, WB + EC, q] = b_bond.T
        pair, m = c // 2, slice((c % 2) * DM, (c % 2) * DM + DM)
        w[q, L0S + pair, m] = w1[0:D]
        w[q, L0D + pair, m] = w1[D:2 * D]
        w[c * EC:(c + 1) * EC, L0E + pair, m] = w1[2 * D:]
        w[m, L0V + pair, q] = w2
    w[:, IDENT] = np.eye(P)
    block_mean = np.kron(np.eye(Q), np.ones((D, D))) / D
    w[:, CENTRE] = np.eye(P) - block_mean
    w[:, ONES] = 1.0

    bias = np.zeros((P, NB), np.float32)
    b_ih, b_hh = get("L1_gnn_b_ih"), get("L1_gnn_b_hh")
    b1, b2 = get("L0_gnn_b1"), get("L0_gnn_b2")
    for c in range(Q):
        q = slice(c * D, c * D + D)
        bias[q, B_R], bias[q, B_Z], bias[q, B_IN] = b_ih[:D], b_ih[D:2 * D], b_ih[2 * D:]
        bias[q, B_RH], bias[q, B_ZH], bias[q, B_HN] = b_hh[:D], b_hh[D:2 * D], b_hh[2 * D:]
        bias[q, B_2] = b2
    for m in range(2):
        bias[m * DM:(m + 1) * DM, B_1A] = b1
        bias[m * DM:(m + 1) * DM, B_1B] = b1
    bias[:, B_EPS] = EPS

    sel = np.zeros((2, Q, EC, EC, Q, D), np.float32)
    for k in range(EC):
        for c in range(Q):
            sel[:, c, k, k, c, :] = 1.0
    arrays = {
        "x": np.ascontiguousarray(get("x")),
        "src_pu": by_slot(get("src"), N),
        "dst_pu": by_slot(get("dst"), N),
        "ea_pu": by_slot(ea, 0),
        "ea_t": ea_t,
        "weights": w.reshape(P, NW * P),
        "biases": bias,
        "sel_h": sel.reshape(P, EC * P).astype(ml_dtypes.bfloat16),
        "triu_h": np.triu(np.ones((P, P), np.float32), 1).astype(ml_dtypes.bfloat16),
        "iota_h": np.tile(np.arange(HIGH, dtype=np.float32), (P, 1)),
        "slot_h": np.arange(EP, dtype=np.float32).reshape(P, T),
    }
    nc = _bacc.Bacc("TRN2", target_bir_lowering=False, num_devices=1)
    aps = {n: nc.dram_tensor(n, a.shape, mybir.dt.from_np(a.dtype), kind="ExternalInput").ap() for n, a in arrays.items()}
    out = nc.dram_tensor("out", (N, D), F32, kind="ExternalOutput").ap()
    with nc.allow_non_contiguous_dma(reason="rows of edges and nodes"):
        bass_gnn_resnorm(nc, **aps, out=out)
    r = _run(nc, [arrays], core_ids=[0])
    return r.results[0]["out"]
```

```python
from contextlib import ExitStack

import numpy as np
import concourse.bass as bass
from concourse import mybir

F32 = mybir.dt.float32
BF16 = mybir.dt.bfloat16
I32 = mybir.dt.int32
ALU = mybir.AluOpType
ACT = mybir.ActivationFunctionType

N, D, E, EC, DM = 100000, 32, 25000, 16, 56
P = 128
Q = 4
J = -(-E // (P * Q))
T = Q * J
QE = J * P
EP = T * P
JC = 7
EI = J // JC
CW = JC * P
UC = JC * Q
NP = 125
NR = N // NP
NG = 8
NI = NR // (NG * Q)
NH = NG // 2 * NP
NC = NG * Q
TW = 36
RW = 20
HT = 14
PI = T // (2 * HT)
LOW, HIGH = 256, 400
DIGITS = 16
PARTS = 3
BT = 14
RING = 7
STEPS = 4
SPLIT = (8, 3, 7, 7)
FAR = 1.0e6
BIG = 1.5e38
EPS = 1e-5

IH, HH, BOND, BOND_B, REPEAT = 0, 3, 6, 7, 8
L0S, L0D, L0E, L0V = (REPEAT + Q + 2 * m for m in range(4))
IDENT, CENTRE, ONES = range(REPEAT + Q + 8, REPEAT + Q + 11)
NW = ONES + 1
B_R, B_Z, B_IN, B_HN, B_RH, B_ZH, B_1A, B_1B, B_2, B_EPS = range(10)
NB = 10


class Signal:

    def __init__(self, sem, base):
        self.sem, self.base = sem, base

    def at(self, n):
        return n + self.base


def bass_gnn_resnorm(nc, x, src_pu, dst_pu, ea_pu, ea_t, weights, biases, sel_h, triu_h, tril_h, iota_h, slot_h, out):
    ctx = ExitStack()
    with ctx:
        def sb(name, shape, dt=F32):
            return ctx.enter_context(nc.sbuf_tensor(name, shape, dt))

        def dram(name, shape, dt=F32):
            return nc.dram_tensor(name, shape, dt, kind="Internal").ap()

        signals = {}

        def sig(name):
            if name not in signals:
                signals[name] = Signal(ctx.enter_context(nc.semaphore(name)), 0 if name.startswith("d_") else 2)
            return signals[name]

        l0_src_rows = dram("l0_src_rows", (P, T, D))
        l0_dst_rows = dram("l0_dst_rows", (P, T, D))
        edges0 = dram("edges0", (P, T, RW))
        edges1 = dram("edges1", (EP, RW))
        edges2 = dram("edges2", (EP, RW))
        x1_rows = dram("x1_rows", (P, T, TW))
        table = dram("table", (N, TW))
        table_words = table.rearrange("n (w o) -> (n w) o", o=1)
        src_rows = dram("src_rows", (P, T, D))
        dst_rows = dram("dst_rows", (P, T, D))
        alone_rows = [dram(f"alone_rows{t}", (P, T, D)) for t in range(STEPS - 1)]
        nbr_rows = dram("nbr_rows", (P, T, D))
        state = dram("state", (EP, D))
        state_rows = state.rearrange("(p u) d -> p u d", p=P)
        final_rows = dram("final_rows", (P, T, D))

        w = sb("w", [P, NW * P])
        bias = sb("bias", [P, NB])
        sel = sb("sel", [PARTS * 2 * EC, 2 * EC // Q * P], BF16)
        triu = sb("triu", [P, P], BF16)
        tril = sb("tril", [P, P], BF16)
        iota = sb("iota", [P, HIGH])
        slots = sb("slots", [P, T])

        def W(n, k=P):
            return w[0:k, n * P:(n + 1) * P]

        def B(n):
            return bias[:, n:n + 1]

        arr_s = sb("arr_s", [P, QE])
        arr_d = sb("arr_d", [P, QE])
        arr_m = sb("arr_m", [P, QE + 1])
        same = sb("same", [P, QE], BF16)
        prefix = sb("prefix", [P, QE], BF16)
        ea_pair = [sb(f"ea_pair{n}", [PARTS * 2 * EC, QE], BF16) for n in range(Q // 2)]

        src_i = sb("src_i", [P, T], I32)
        dst_i = sb("dst_i", [P, T], I32)
        key_f = sb("key_f", [P, T])
        src_f = sb("src_f", [P, T])
        dst_f = sb("dst_f", [P, T])
        digit = sb("digit", [P, T])
        rank = sb("rank", [P, T])
        rank_t = sb("rank_t", [P, BT])
        tmp_i = sb("tmp_i", [P, T], I32)
        tmp_f = sb("tmp_f", [P, T])
        idx_a = sb("idx_a", [P, T], I32)
        idx_b = sb("idx_b", [P, T], I32)
        idx_c = sb("idx_c", [P, T], I32)
        slot_f = sb("slot_f", [P, T])
        last_f = sb("last_f", [P, T])

        ring = sb("ring", [P, 2, HT * TW])
        ring_i = sb("ring_i", [P, 2, HT], I32)

        rows = sb("rows", [P, NC * TW])
        rows_b = sb("rows_b", [P, CW])
        rows_o = sb("rows_o", [P, NC * TW])
        ca = sb("ca", [P, NC * D])
        cb = sb("cb", [P, NC * D])
        cc = sb("cc", [P, NC * D])
        cd = sb("cd", [P, NC * D])
        ce = sb("ce", [P, NC * D])
        cf = sb("cf", [P, NC * D])
        cg = sb("cg", [P, NC * D])
        col = sb("col", [P, 8])
        stat = sb("stat", [P, 3, NC])
        oh = arr_d[:, 0:RING * HIGH // 2].bitcast(BF16).rearrange("p (r b) -> p r b", b=HIGH)
        cum = arr_d[:, RING * HIGH:RING * HIGH + HIGH]
        oh_minor = arr_d[:, 0:T * DIGITS // 2].bitcast(BF16)
        oh_major = arr_d[:, (RING + 1) * HIGH:(RING + 1) * HIGH + T * (HIGH // DIGITS) // 2].bitcast(BF16)

        PA, PB, PC, PD = (ctx.enter_context(nc.psum_tensor(f"p{n}", [P, 1024], F32)) for n in "abcd")

        def halves(ps, buf, dense):
            if dense:
                return [(ps[:, 512 * h:512 * h + NH], buf[:, NH * h:NH * h + NH]) for h in range(2)]
            return [(ps[:, 0:512], buf[:, 0:512]), (ps[:, 512:CW], buf[:, 512:CW])]

        def pv(ps, dense):
            return ps[:, :].rearrange("p (h c) -> p h c", h=2)[:, :, 0:NH] if dense else ps[:, 0:CW]

        def bv(buf, dense):
            return buf[:, 0:2 * NH].rearrange("p (h c) -> p h c", h=2) if dense else buf[:, 0:CW]

        def rows_view(buf, width, dense):
            return buf[0:NP, 0:NC * width].rearrange("p (n w) -> p n w", w=width) if dense \
                else buf[:, 0:UC * width].rearrange("p (n w) -> p n w", w=width)

        def advance(name, n):
            sig(name).base += n

        class RingPass:

            def __init__(self, idx, table_ap, width, last, scatter=False, load_from=None, store=None, stored=0,
                         rows_there=lambda sp, turn: None):
                self.rows_there = rows_there
                self.idx, self.table_ap, self.width, self.last, self.scatter = idx, table_ap, width, last, scatter
                self.load_from, self.store, self.n_stored = load_from, store, stored
                self.n_loaded = 16 if load_from is None else 32
                self.base = {n: sig(n).base for h in range(2) for n in (f"d_loaded{h}", f"d_done{h}", f"d_stored{h}")}
                for h in range(2):
                    advance(f"d_loaded{h}", PI * self.n_loaded)
                    advance(f"d_done{h}", PI * 16 * HT)
                    advance(f"d_stored{h}", PI * 16 * stored)

            def pool(self, pool):
                width = self.width
                with pool.Fori(0, PI) as i:
                    for h in range(2):
                        pool.wait_ge(sig(f"d_loaded{h}").sem, (i + 1) * self.n_loaded + self.base[f"d_loaded{h}"])
                        pool.sem_inc(sig("turns").sem, 1)
                        for k in range(HT):
                            view = ring[:, h, k * width:(k + 1) * width]
                            at = bass.IndirectOffsetOnAxis(ap=ring_i[:, h, k:k + 1], axis=0)
                            ends = (self.table_ap, at, view, None) if self.scatter else (view, None, self.table_ap, at)
                            pool.indirect_dma_start(*ends, bounds_check=self.last, oob_is_err=False)\
                                .then_inc(sig(f"d_done{h}").sem, 16)

            def sp(self, sp):
                def fill(h, u):
                    sp.dma_start(ring_i[:, h, :], self.idx[:, bass.ds(u, HT)]).then_inc(sig(f"d_loaded{h}").sem, 16)
                    if self.load_from is not None:
                        sp.dma_start(ring[:, h, 0:HT * self.width].rearrange("p (t w) -> p t w", w=self.width),
                                     self.load_from[:, bass.ds(u, HT), :]).then_inc(sig(f"d_loaded{h}").sem, 16)

                def turn(i, h):
                    sp.wait_ge(sig(f"d_done{h}").sem, (i + 1) * (16 * HT) + self.base[f"d_done{h}"])
                    if self.store is not None:
                        self.store(sp, h, (i * 2 + h) * HT, sig(f"d_stored{h}").sem)
                        sp.wait_ge(sig(f"d_stored{h}").sem, (i + 1) * (16 * self.n_stored) + self.base[f"d_stored{h}"])

                self.rows_there(sp, 0)
                for h in range(2):
                    fill(h, h * HT)
                with sp.Fori(0, PI - 1) as i:
                    for h in range(2):
                        turn(i, h)
                        if h == 0:
                            self.rows_there(sp, i + 1)
                        fill(h, (i * 2 + 2 + h) * HT)
                for h in range(2):
                    turn(PI - 1, h)

        def back(store_ap, width=D):
            def store(sp, h, u, sem):
                sp.dma_start(store_ap[:, bass.ds(u, HT), :],
                             ring[:, h, 0:HT * width].rearrange("p (t w) -> p t w", w=width)[:, :, 0:D]).then_inc(sem, 16)
            return store

        def back_with_slot(store_ap):
            def store(sp, h, u, sem):
                g = ring[:, h, :].rearrange("p (t w) -> p t w", w=TW)
                sp.dma_start(store_ap[:, bass.ds(u, HT), :], g[:, :, 0:D]).then_inc(sem, 16)
                sp.dma_start(slot_f[:, bass.ds(u, HT)], g[:, :, D]).then_inc(sem, 16)
            return store

        def to_columns(pe, ps, buf, dense, width=D):
            if dense:
                v = buf[0:NP, 0:NC * width].rearrange("p (g r w) -> p g r w", r=Q, w=width)
                for g in range(NG):
                    o = 512 * (g // (NG // 2)) + NP * (g % (NG // 2))
                    ins = pe.transpose(ps[:, o:o + NP], v[:, g, :, 0:D], W(IDENT)[0:NP, 0:NP])
            else:
                for j in range(JC):
                    ins = pe.transpose(ps[:, j * P:(j + 1) * P], buf[:, j * P:(j + 1) * P], W(IDENT))
            return ins

        def to_rows(pe, ps, buf, dense, centred=False):
            n, width = (NG, NP) if dense else (JC, P)
            for g in range(n):
                o, cols_g = ps[0:width, g * P:(g + 1) * P], buf[:, g * width:(g + 1) * width]
                ins = pe.matmul(o, cols_g, W(CENTRE), start=True, stop=True) if centred else pe.transpose(o, cols_g, W(IDENT))
            return ins

        def ln_views(ps, sq, width, dense):
            p, n = (NP, NC) if dense else (P, UC)
            view = lambda buf: buf[0:p, 0:n * D].rearrange("p (n d) -> p n d", d=D)
            return p, n, view(ps), view(sq), rows_view(rows_o, width, dense)[:, :, 0:D]

        def ln_square(act, i, dense, ps, sq):
            p, n, centred, squares, _ = ln_views(ps, sq, D, dense)
            act.wait_ge(sig("out_rows").sem, sig("out_rows").at(i + 1))
            act.activation(squares, centred, ACT.Square).then_inc(sig("ln_squared").sem, 1)

        def ln_deviation(act, i, dense):
            p, n = (NP, NC) if dense else (P, UC)
            act.wait_ge(sig("ln_sum").sem, sig("ln_sum").at(i + 1))
            act.activation(stat[0:p, 1, 0:n], stat[0:p, 0, 0:n], ACT.Sqrt, bias=bias[0:p, B_EPS:B_EPS + 1], scale=1.0 / D)\
               .then_inc(sig("ln_dev").sem, 1)

        def ln_sums(dve, i, dense, ps, sq):
            p, n, centred, squares, _ = ln_views(ps, sq, D, dense)
            dve.wait_ge(sig("ln_squared").sem, sig("ln_squared").at(i + 1))
            dve.tensor_reduce(stat[0:p, 0, 0:n], squares, mybir.AxisListType.X, ALU.add).then_inc(sig("ln_sum").sem, 1)

        def ln_scale(dve, i, width, dense, ps, sq, direct=False):
            p, n, centred, squares, target = ln_views(ps, sq, width, dense)
            dve.wait_ge(sig("ln_dev").sem, sig("ln_dev").at(i + 1))
            dve.reciprocal(stat[0:p, 2, 0:n], stat[0:p, 1, 0:n]).then_inc(sig("ln_inv").sem, 1)
            dve.wait_ge(sig("ln_inv").sem, sig("ln_inv").at(i + 1))
            if direct:
                dve.wait_ge(sig("d_out").sem, sig("d_out").at(i * 16))
            else:
                dve.wait_ge(sig("stored").sem, sig("stored").at(i))
            dve.tensor_tensor(target, centred, stat[0:p, 2, 0:n].unsqueeze(2).to_broadcast([p, n, D]), ALU.mult)\
               .then_inc(sig("rows_ready").sem, 1)

        def ln_dve(dve, i, width, dense):
            ln_sums(dve, i, dense, PC, cc)
            ln_scale(dve, i, width, dense, PC, cc)

        def ln_advance(n):
            for name in ("ln_squared", "ln_sum", "ln_dev", "ln_inv"):
                advance(name, n)

        def half_of(buf, half, dense):
            if dense:
                return buf[:, NH * half:NH * half + NH]
            return (buf[:, 0:512], buf[:, 512:CW])[half]

        def bank(ps, half, dense):
            return ps[:, 512 * half:512 * half + (NH if dense else (512, CW - 512)[half])]

        def gru_pe(pe, n, h, agg, dense, state_ready, before_n=lambda half: None):
            for half in range(2):
                state_ready(half)
                gates = [(PA, IH, HH, "pre_r"), (PB, IH + 1, HH + 1, "pre_z"), (PC, None, HH + 2, "pre_n")]
                if agg is not None:
                    gates.insert(2, (PD, IH + 2, None, None))
                for ps, wi, wh, ready in gates:
                    if ps is gates[2][0]:
                        before_n(half)
                    parts = [(W(wh), h(half))] if wh is not None else []
                    if wi is not None and agg is not None:
                        parts.append((W(wi), agg(half)))
                    for m, (l, r) in enumerate(parts):
                        ins = pe.matmul(bank(ps, half, dense), l, r, start=(m == 0), stop=(m == len(parts) - 1))
                    if ready:
                        ins.then_inc(sig(ready).sem, 1)

        def gru_act(act, n, dense, between=lambda: None, before_tanh=lambda half: None):
            for half in range(2):
                t = n * 2 + half
                act.wait_ge(sig("pre_r").sem, sig("pre_r").at(t + 1))
                act.activation(half_of(ca, half, dense), bank(PA, half, dense), ACT.Sigmoid, bias=B(B_R))\
                   .then_inc(sig("gate_r").sem, 1)
                act.wait_ge(sig("pre_z").sem, sig("pre_z").at(t + 1))
                act.activation(half_of(cb, half, dense), bank(PB, half, dense), ACT.Sigmoid, bias=B(B_Z))\
                   .then_inc(sig("gate_z").sem, 1)
                before_tanh(half)
                act.wait_ge(sig("cand").sem, sig("cand").at(t + 1))
                act.activation(half_of(cd, half, dense), half_of(cc, half, dense), ACT.Tanh, bias=B(B_IN))\
                   .then_inc(sig("gate_n").sem, 1)
                if half == 0:
                    between()

        def gru_dve(dve, n, h, has_agg, dense, between=lambda: None, new=None):
            new = cf if new is None else new
            for half in range(2):
                t = n * 2 + half
                dve.wait_ge(sig("pre_n").sem, sig("pre_n").at(t + 1))
                dve.wait_ge(sig("gate_r").sem, sig("gate_r").at(t + 1))
                first = half_of(ce if has_agg else cc, half, dense)
                ins = dve.scalar_tensor_tensor(first, bank(PC, half, dense), B(B_HN), half_of(ca, half, dense),
                                               ALU.add, ALU.mult)
                if has_agg:
                    ins.then_inc(sig("cand_h").sem, 1)
                    dve.wait_ge(sig("cand_h").sem, sig("cand_h").at(t + 1))
                    ins = dve.tensor_tensor(half_of(cc, half, dense), first, bank(PD, half, dense), ALU.add)
                ins.then_inc(sig("cand").sem, 1)
                if half == 0:
                    between()
                r, z, cand_n = (half_of(buf, half, dense) for buf in (ca, cb, cd))
                dve.wait_ge(sig("gate_z").sem, sig("gate_z").at(t + 1))
                dve.wait_ge(sig("cand").sem, sig("cand").at(t + 1))
                dve.tensor_tensor(r, z, h(half), ALU.mult).then_inc(sig("z_h").sem, 1)
                dve.wait_ge(sig("z_h").sem, sig("z_h").at(t + 1))
                dve.wait_ge(sig("gate_n").sem, sig("gate_n").at(t + 1))
                dve.scalar_tensor_tensor(z, z, 1.0, cand_n, ALU.subtract, ALU.mult).then_inc(sig("n_part").sem, 1)
                dve.wait_ge(sig("n_part").sem, sig("n_part").at(t + 1))
                dve.tensor_tensor(half_of(new, half, dense), r, z, ALU.subtract).then_inc(sig("h_new").sem, 1)

        def gru_advance(n, has_agg):
            for name in ("pre_r", "pre_z", "pre_n", "gate_r", "gate_z", "cand", "gate_n", "z_h", "n_part", "h_new"):
                advance(name, 2 * n)
            if has_agg:
                advance("cand_h", 2 * n)

        def waited(eng):
            eng.sem_inc(sig("turns").sem, 1)

        link_count = [0]

        def link(eng, ins):
            ins.then_inc(sig("dve_link").sem, 1)
            link_count[0] += 1
            eng.wait_ge(sig("dve_link").sem, sig("dve_link").base + link_count[0])

        def by_tile(a):
            return a[:, :].rearrange("p (j c) -> p c j", c=Q)

        def rank_pe(pe, buckets):
            n = buckets // DIGITS
            pe.wait_ge(sig("hot").sem, sig("hot").at(1))
            with pe.Fori(0, T // BT) as i:
                for k in range(BT):
                    ins = pe.matmul(PD[0:n, 0:DIGITS], oh_major[:, bass.ds((i * BT + k) * n, n)],
                                    oh_minor[:, bass.ds((i * BT + k) * DIGITS, DIGITS)], start=False, stop=False,
                                    skip_group_check=True)
                ins.then_inc(sig("counted").sem, 1)
            pe.wait_ge(sig("row_totals").sem, sig("row_totals").at(1))
            pe.matmul(PC[0:n, 0:1], cd[0:n, 0:n], cc[0:n, DIGITS - 1:DIGITS], start=True, stop=True)\
              .then_inc(sig("rows_before").sem, 1)
            pe.wait_ge(sig("based").sem, sig("based").at(1))
            for ps in (PA, PB):
                pe.matmul(ps[:, 0:buckets], W(ONES), cum[:, 0:buckets], start=True, stop=False, skip_group_check=True)
            with pe.Fori(0, T // BT) as i:
                for k in range(BT):
                    def hot(m):
                        return oh[:, m % RING, 0:buckets]
                    ps = (PA, PB)[k % 2][:, 0:buckets]
                    pe.wait_ge(sig("hot").sem, sig("hot").at(i * BT + k + 2))
                    pe.wait_ge(sig("placed").sem, sig("placed").at(i * BT + k - 1))
                    pe.matmul(ps, tril[:, :], hot(k - 2), start=False, stop=False, skip_group_check=True)
                    pe.matmul(ps, ones_b[:, :], hot(k - 1), start=False, stop=False, skip_group_check=True)
                    pe.matmul(ps, triu[:, :], hot(k), start=False, stop=False, skip_group_check=True)\
                      .then_inc(sig("before").sem, 1)

        def rank_dve(dve, buckets):
            n = buckets // DIGITS
            link(dve, dve.memset(PD[:, 0:DIGITS], 0.0))
            link(dve, dve.memset(cum[:, 0:buckets], 0.0))
            link(dve, dve.tensor_copy(tmp_i[:, :], digit[:, :]))
            link(dve, dve.tensor_scalar(src_i[:, :], tmp_i[:, :], 4, None, ALU.arith_shift_right))
            link(dve, dve.tensor_copy(tmp_f[:, :], src_i[:, :]))
            link(dve, dve.scalar_tensor_tensor(key_f[:, :], tmp_f[:, :], -float(DIGITS), digit[:, :], ALU.mult, ALU.add))
            for one_hot, value, m in ((oh_major, tmp_f, n), (oh_minor, key_f, DIGITS)):
                link(dve, dve.tensor_tensor(one_hot[:, 0:T * m].rearrange("p (t m) -> p t m", m=m),
                                            value[:, :].unsqueeze(2).to_broadcast([P, T, m]),
                                            iota[:, 0:m].unsqueeze(1).to_broadcast([P, T, m]), ALU.is_equal))
            dve.sem_inc(sig("hot").sem, 1)
            link(dve, dve.tensor_copy(cd[0:n, 0:n], triu[0:n, 0:n]))
            link(dve, dve.memset(cb[0:n, 0:DIGITS], 0.0))
            dve.wait_ge(sig("counted").sem, sig("counted").at(T // BT))
            link(dve, dve.tensor_copy(ca[0:n, 0:DIGITS], PD[0:n, 0:DIGITS]))
            link(dve, dve.tensor_tensor_scan(cc[0:n, 0:DIGITS], ca[0:n, 0:DIGITS], cb[0:n, 0:DIGITS], 0.0, ALU.add, ALU.add))
            dve.sem_inc(sig("row_totals").sem, 1)
            dve.wait_ge(sig("rows_before").sem, sig("rows_before").at(1))
            link(dve, dve.tensor_copy(col[0:n, 0:1], PC[0:n, 0:1]))
            link(dve, dve.scalar_tensor_tensor(ce[0:n, 0:DIGITS], cc[0:n, 0:DIGITS], col[0:n, 0:1], ca[0:n, 0:DIGITS],
                                               ALU.add, ALU.subtract))
            dve.tensor_tensor(cum[0:n, 0:buckets].rearrange("p (r m) -> p r m", m=DIGITS),
                              ce[0:n, 0:DIGITS].unsqueeze(1).to_broadcast([n, n, DIGITS]),
                              W(IDENT)[0:n, 0:n].unsqueeze(2).to_broadcast([n, n, DIGITS]),
                              ALU.mult).then_inc(sig("based").sem, 1)
            link(dve, dve.memset(oh[:, :, 0:buckets], 0.0))
            with dve.Fori(0, T // BT) as i:
                for k in range(BT + 2):
                    if k < BT:
                        dve.tensor_scalar(oh[:, k % RING, 0:buckets], iota[:, 0:buckets],
                                          digit[:, bass.ds(i * BT + k, 1)], None, ALU.is_equal).then_inc(sig("hot").sem, 1)
                    if k >= 2:
                        m, t = (k - 2) % 2, i * BT + (k - 2)
                        dve.wait_ge(sig("hot").sem, sig("hot").at(t + 2))
                        dve.wait_ge(sig("placed").sem, sig("placed").at(t - 1))
                        dve.wait_ge(sig("before").sem, sig("before").at(t + 1))
                        dve.tensor_tensor_reduce((ca, cb)[m][:, 0:buckets], (PA, PB)[m][:, 0:buckets],
                                                 oh[:, (k - 2) % RING, 0:buckets], 1.0, 0.0, ALU.mult, ALU.add,
                                                 rank_t[:, k - 2:k - 1]).then_inc(sig("placed").sem, 1)
                dve.wait_ge(sig("placed").sem, sig("placed").at((i + 1) * BT))
                waited(dve)
                dve.tensor_copy(rank[:, bass.ds(i * BT, BT)], rank_t[:, :]).then_inc(sig("ranked").sem, 1)
                dve.wait_ge(sig("ranked").sem, sig("ranked").at(i + 1))

        def rank_advance():
            advance("hot", T + 1)
            advance("counted", T // BT)
            advance("row_totals", 1)
            advance("rows_before", 1)
            advance("based", 1)
            advance("before", T)
            advance("placed", T)
            advance("ranked", T // BT)

        def rank_to_row(dve, idx):
            link(dve, dve.tensor_copy(tmp_i[:, :], rank[:, :]))
            link(dve, dve.tensor_scalar(src_i[:, :], tmp_i[:, :], 7, None, ALU.arith_shift_right))
            link(dve, dve.tensor_copy(tmp_f[:, :], src_i[:, :]))
            link(dve, dve.scalar_tensor_tensor(key_f[:, :], tmp_f[:, :], -128.0, rank[:, :], ALU.mult, ALU.add))
            link(dve, dve.tensor_scalar(key_f[:, :], key_f[:, :], float(T), None, ALU.mult))
            link(dve, dve.scalar_tensor_tensor(key_f[:, :], tmp_f[:, :], float(Q), key_f[:, :], ALU.mult, ALU.add))
            for c in range(1, Q):
                link(dve, dve.tensor_scalar(rank[:, :], tmp_f[:, :], float(c * J), -float(Q * J - 1), ALU.is_ge, ALU.mult))
                link(dve, dve.tensor_tensor(key_f[:, :], key_f[:, :], rank[:, :], ALU.add))
            link(dve, dve.tensor_copy(idx[:, :].rearrange("p (j c) -> p c j", c=Q),
                                      key_f[:, :].rearrange("p (c j) -> p c j", c=Q)))

        ones_b = ctx.enter_context(nc.sbuf_tensor("ones_b", [P, P], BF16))

        def masks_pe(pe):
            with pe.Fori(0, EI) as i:
                pe.wait_ge(sig("m_rows").sem, sig("m_rows").at(i + 1))
                to_columns(pe, PA, cf, False).then_inc(sig("m_cols").sem, 1)
            with pe.Fori(0, EI) as i:
                pe.wait_ge(sig("m_last").sem, sig("m_last").at(i + 1))
                to_rows(pe, PA, ce, False).then_inc(sig("m_back").sem, 1)

        def masks_dve(dve):
            kt = arr_m
            with dve.Fori(0, EI) as i:
                dve.wait_ge(sig("m_cols").sem, sig("m_cols").at(i))
                dve.tensor_copy(ca[:, 0:UC], key_f[:, bass.ds(i * UC, UC)]).then_inc(sig("m_keys").sem, 1)
                dve.wait_ge(sig("m_keys").sem, sig("m_keys").at(i + 1))
                dve.tensor_copy(cf[:, 0:CW].rearrange("p (u f) -> p u f", f=D),
                                ca[:, 0:UC].unsqueeze(2).to_broadcast([P, UC, D])).then_inc(sig("m_rows").sem, 1)
                dve.wait_ge(sig("m_cols").sem, sig("m_cols").at(i + 1))
                waited(dve)
                dve.tensor_copy(kt[:, bass.ds(i * CW, CW)], PA[:, 0:CW]).then_inc(sig("m_kt").sem, 1)
            dve.wait_ge(sig("m_kt").sem, sig("m_kt").at(EI))
            link(dve, dve.memset(col[:, :], -1.0))
            for c in range(1, Q):
                link(dve, dve.tensor_copy(col[D * c:D * c + D, 0:1], kt[D * (c - 1):D * c, QE - 1:QE]))
            link(dve, dve.tensor_tensor(same[:, 1:QE], kt[:, 1:QE], kt[:, 0:QE - 1], ALU.is_equal))
            link(dve, dve.tensor_tensor(same[:, 0:1], kt[:, 0:1], col[:, 0:1], ALU.is_equal))
            link(dve, dve.tensor_tensor_scan(prefix[:, :], same[:, :], same[:, :], 1.0, ALU.mult, ALU.mult))
            link(dve, dve.memset(col[:, 1:2], 0.0))
            for c in range(1, Q):
                link(dve, dve.tensor_copy(col[D * (c - 1):D * c, 1:2], same[D * c:D * c + D, 0:1]))
            link(dve, dve.scalar_tensor_tensor(kt[:, 0:QE - 1], same[:, 1:QE], FAR, kt[:, 0:QE - 1], ALU.mult, ALU.add))
            link(dve, dve.scalar_tensor_tensor(kt[:, QE - 1:QE], col[:, 1:2], FAR, kt[:, QE - 1:QE], ALU.mult, ALU.add))
            link(dve, dve.memset(same[:, 0:1], 0.0))
            with dve.Fori(0, EI) as i:
                dve.wait_ge(sig("m_back").sem, sig("m_back").at(i))
                waited(dve)
                dve.tensor_copy(ce[:, 0:CW], kt[:, bass.ds(i * CW, CW)]).then_inc(sig("m_last").sem, 1)
                dve.wait_ge(sig("m_back").sem, sig("m_back").at(i + 1))
                waited(dve)
                dve.tensor_copy(last_f[:, bass.ds(i * UC, UC)],
                                PA[:, 0:CW].rearrange("p (u f) -> p u f", f=D)[:, :, 0]).then_inc(sig("m_lf").sem, 1)
            dve.wait_ge(sig("m_lf").sem, sig("m_lf").at(EI))

        def masks_advance():
            for name in ("m_rows", "m_cols", "m_last", "m_back", "m_keys", "m_kt", "m_lf"):
                advance(name, EI)

        def carry_over(dve, a, op_fix, neutral, mask):
            last = slice(QE - 1, QE)
            link(dve, dve.memset(col[:, 2:3], neutral))
            link(dve, dve.tensor_copy(col[:, 3:4], a[:, last]))
            link(dve, dve.tensor_copy(col[:, 4:5], mask[:, last]))
            for c in range(1, Q):
                q, b = slice(D * c, D * c + D), slice(D * (c - 1), D * c)
                link(dve, dve.tensor_copy(col[q, 2:3], col[b, 3:4]))
                link(dve, dve.scalar_tensor_tensor(col[q, 3:4], col[q, 4:5], col[q, 2:3], a[q, last], op_fix[0], op_fix[1]))
            link(dve, dve.scalar_tensor_tensor(a[:, 0:QE], mask[:, 0:QE], col[:, 2:3], a[:, 0:QE], op_fix[0], op_fix[1]))

        COMPUTE = """turns ln_squared ln_sum ln_dev ln_inv pre_r pre_z pre_n gate_r gate_z cand_h cand gate_n
            z_h n_part h_new dve_link hot based counted row_totals rows_before before placed m_rows m_cols m_last m_back m_keys
            m_kt m_lf
            edge_rows in_cols y_ready out_rows rows_ready stored x_cols x1_max l0_cols l0_s l0_d l0_h l0_y l0_hl l0_v
            l0_yv l0_done ea_rows ea_cols split hd_ready own_cols sel_cols z_ready z_used msg_saved repeat_cols repeated
            h_saved packed ranked x_kept""".split()

        for name in COMPUTE:
            sig(name)
        with nc.Block() as block:
            @block.sync
            def _(sp):
                for name in COMPUTE:
                    sp.sem_inc(signals[name].sem, 2)

        with nc.Block() as block:
            @block.sync
            def _(sp):
                for dst, source in ((w, weights), (bias, biases), (sel, sel_h), (triu, triu_h), (tril, tril_h), (iota, iota_h),
                                    (slots, slot_h), (src_i, src_pu), (dst_i, dst_pu)):
                    sp.dma_start(dst[:, :], source).then_inc(sig("d_const").sem, 16)
                sp.dma_start(arr_s[:, 0:T * EC], ea_pu.rearrange("p t k -> p (t k)")).then_inc(sig("d_const").sem, 16)
                sp.wait_ge(sig("edge_rows").sem, sig("edge_rows").at(1))
                sp.dma_start(edges0, arr_d[:, 0:T * RW].rearrange("p (t w) -> p t w", w=RW)).then_inc(sig("d_out").sem, 16)
                sp.wait_ge(sig("d_out").sem, 16)

            @block.vector
            def _(dve):
                dve.wait_ge(sig("d_const").sem, 10 * 16)
                er = arr_d[:, 0:T * RW].rearrange("p (t w) -> p t w", w=RW)
                link(dve, dve.memset(arr_d[:, 0:T * RW], 0.0))
                link(dve, dve.memset(ones_b[:, :], 1.0))
                link(dve, dve.tensor_copy(src_f[:, :], src_i[:, :]))
                link(dve, dve.tensor_copy(dst_f[:, :], dst_i[:, :]))
                link(dve, dve.tensor_copy(er[:, :, 0], src_f[:, :]))
                link(dve, dve.tensor_copy(er[:, :, 1], dst_f[:, :]))
                link(dve, dve.tensor_copy(er[:, :, 2:2 + EC], arr_s[:, 0:T * EC].rearrange("p (t k) -> p t k", k=EC)))
                dve.sem_inc(sig("edge_rows").sem, 1)
                link(dve, dve.tensor_scalar(tmp_f[:, :], src_f[:, :], float(N - 1), None, ALU.min))
                link(dve, dve.tensor_copy(idx_a[:, :], tmp_f[:, :]))
                link(dve, dve.tensor_scalar(tmp_f[:, :], dst_f[:, :], float(N - 1), None, ALU.min))
                link(dve, dve.tensor_copy(idx_b[:, :], tmp_f[:, :]))
                link(dve, dve.tensor_scalar(tmp_i[:, :], src_i[:, :], LOW - 1, None, ALU.bitwise_and))
                link(dve, dve.tensor_copy(digit[:, :].rearrange("p (c j) -> p c j", c=Q), by_tile(tmp_i)))
                link(dve, dve.tensor_tensor(bias[:, B_R:B_R + 2], bias[:, B_R:B_R + 2], bias[:, B_RH:B_RH + 2], ALU.add))
                link(dve, dve.memset(rows_o[:, :], FAR))

        advance("d_const", 10 * 16)
        advance("d_out", 16)
        advance("edge_rows", 1)

        def cols(a, i, width=CW):
            return a[:, bass.ds(i * width, width)]

        def stream_sp(sp, n, load, store, n_out=1):
            def put(i):
                sp.wait_ge(sig("rows_ready").sem, sig("rows_ready").at(i + 1))
                store(sp, i).then_inc(sig("d_out").sem, 16)
                sp.wait_ge(sig("d_out").sem, sig("d_out").at((i + 1) * 16))
                sp.sem_inc(sig("stored").sem, 1)

            if load is not None:
                load(sp, 0).then_inc(sig("d_in").sem, 16)
            with sp.Fori(0, n - 1) as i:
                if load is not None:
                    sp.wait_ge(sig("in_cols").sem, sig("in_cols").at(i + 1))
                    load(sp, i + 1).then_inc(sig("d_in").sem, 16)
                if store is not None:
                    put(i)
            if store is not None:
                put(n - 1)

        def stream_advance(n, load, store):
            if load:
                advance("d_in", 16 * n)
                advance("in_cols", n)
            if store:
                advance("d_out", 16 * n)
                advance("stored", n)
                advance("rows_ready", n)
                advance("out_rows", n)

        def x_nodes(ap, i):
            return ap.rearrange("(p n) d -> p n d", p=NP)[:, bass.ds(i * NC, NC), :]

        def rows_out(act, i, ps, width, dense):
            act.wait_ge(sig("out_rows").sem, sig("out_rows").at(i + 1))
            act.wait_ge(sig("stored").sem, sig("stored").at(i))
            source = ps[0:NP, 0:NG * P] if dense else ps[:, 0:CW]
            act.activation(rows_view(rows_o, width, dense)[:, :, 0:D], source.rearrange("p (n w) -> p n w", w=D),
                           ACT.Copy).then_inc(sig("rows_ready").sem, 1)

        def chunks(eng, n, body):
            with eng.Fori(0, n - 1) as i:
                body(i, True)
            body(n - 1, False)

        def put(act, i, target, source):
            act.wait_ge(sig("rows_ready").sem, sig("rows_ready").at(i + 1))
            act.dma_start(target, source).then_inc(sig("d_out").sem, 16)

        def put_done(act, i):
            act.wait_ge(sig("d_out").sem, sig("d_out").at((i + 1) * 16))
            act.sem_inc(sig("stored").sem, 1)

        def act_store(act, i, target, source):
            put(act, i, target, source)
            put_done(act, i)

        def edge_rows_of(ap, i):
            return ap[:, bass.ds(i * UC, UC), :]

        g_src = RingPass(idx_a, x, D, N - 1, store=back(l0_src_rows), stored=1)
        g_dst = RingPass(idx_b, x, D, N - 1, store=back(l0_dst_rows), stored=1)
        with nc.Block() as block:
            @block.gpsimd
            def _(pool):
                g_src.pool(pool)
                g_dst.pool(pool)

            @block.sync
            def _(sp):
                g_src.sp(sp)
                g_dst.sp(sp)

            @block.tensor
            def _(pe):
                rank_pe(pe, LOW)
                masks_pe(pe)
                def columns(i):
                    pe.wait_ge(sig("y_ready").sem, sig("y_ready").at(i + 1))
                    to_columns(pe, PA, cf, True).then_inc(sig("in_cols").sem, 1)

                def body(i, more):
                    pe.wait_ge(sig("x_cols").sem, sig("x_cols").at(i + 1))
                    pe.wait_ge(sig("rows_ready").sem, sig("rows_ready").at(i))
                    to_rows(pe, PC, cg, True, centred=True).then_inc(sig("out_rows").sem, 1)
                    if more:
                        columns(i + 1)
                columns(0)
                chunks(pe, NI, body)

            @block.scalar
            def _(act):
                def load(i):
                    act.dma_start(rows_view(rows, D, True), x_nodes(x, i)).then_inc(sig("d_in").sem, 16)

                def columns(i, more):
                    act.wait_ge(sig("in_cols").sem, sig("in_cols").at(i + 1))
                    if more:
                        load(i + 1)
                    act.activation(bv(cg, True), pv(PA, True), ACT.Copy).then_inc(sig("x_cols").sem, 1)

                def body(i, before, more, more2):
                    ln_square(act, i, True, PC, cc)
                    if before:
                        put_done(act, i - 1)
                    if more:
                        columns(i + 1, more2)
                    ln_deviation(act, i, True)
                    put(act, i, x_nodes(table, i), rows_view(rows_o, TW, True))
                load(0)
                columns(0, True)
                body(0, False, True, True)
                with act.Fori(1, NI - 2) as i:
                    body(i, True, True, True)
                body(NI - 2, True, True, False)
                body(NI - 1, True, False, False)
                put_done(act, NI - 1)

            @block.vector
            def _(dve):
                rank_dve(dve, LOW)
                rank_to_row(dve, idx_c)
                link(dve, dve.tensor_copy(key_f[:, :], dst_f[:, :]))
                masks_dve(dve)
                link(dve, dve.tensor_scalar(same[:, :], same[:, :], -1.0, BIG, ALU.add, ALU.mult))
                link(dve, dve.tensor_scalar(prefix[:, :], prefix[:, :], -1.0, BIG, ALU.add, ALU.mult))
                link(dve, dve.memset(rows_o[:, :], FAR))
                def sums(i):
                    dve.wait_ge(sig("d_in").sem, sig("d_in").at((i + 1) * 16))
                    dve.wait_ge(sig("in_cols").sem, sig("in_cols").at(i))
                    dve.scalar_tensor_tensor(cf[0:NP, 0:NC * D], rows[0:NP, 0:NC * D], 0.0, rows[0:NP, 0:NC * D],
                                             ALU.max, ALU.add).then_inc(sig("y_ready").sem, 1)

                def body(i, more):
                    if more:
                        sums(i + 1)
                    ln_dve(dve, i, TW, True)
                sums(0)
                chunks(dve, NI, body)
        rank_advance()
        masks_advance()
        stream_advance(NI, True, True)
        advance("x_cols", NI)
        advance("y_ready", NI)
        ln_advance(NI)

        sort_low = RingPass(idx_c, edges1, RW, EP - 1, scatter=True, load_from=edges0)

        def maximum_x1(dve):
            link(dve, dve.tensor_tensor_scan(arr_m[:, 0:QE], same[:, :], arr_m[:, 0:QE], -BIG, ALU.add, ALU.max))
            carry_over(dve, arr_m, (ALU.add, ALU.max), -BIG, prefix)

        with nc.Block() as block:
            @block.gpsimd
            def _(pool):
                sort_low.pool(pool)

            @block.sync
            def _(sp):
                sort_low.sp(sp)

            @block.scalar
            def _(act):
                def load_rows(i):
                    act.dma_start(rows[:, 0:CW].rearrange("p (u d) -> p u d", d=D),
                                  l0_src_rows[:, bass.ds(i * UC, UC), :]).then_inc(sig("d_l0").sem, 16)
                    act.dma_start(rows_b[:, 0:CW].rearrange("p (u d) -> p u d", d=D),
                                  l0_dst_rows[:, bass.ds(i * UC, UC), :]).then_inc(sig("d_l0").sem, 16)

                def load_attributes(i):
                    act.dma_start(ce[0:Q * EC, 0:CW], ea_t[:, bass.ds(i * CW, CW)]).then_inc(sig("d_l0").sem, 16)

                def layer0(i, more):
                    act.wait_ge(sig("l0_cols").sem, sig("l0_cols").at(i + 1))
                    if more:
                        load_rows(i + 1)
                    act.activation(ca[:, 0:CW], PA[:, 0:CW], ACT.Copy).then_inc(sig("l0_s").sem, 1)
                    act.wait_ge(sig("l0_h").sem, sig("l0_h").at(i + 1))
                    if more:
                        load_attributes(i + 1)
                    act.activation(cc[:, 0:CW], PC[:, 0:CW], ACT.Identity, bias=B(B_1A))
                    act.activation(cd[:, 0:CW], PD[:, 0:CW], ACT.Identity, bias=B(B_1B)).then_inc(sig("l0_y").sem, 1)
                    act.wait_ge(sig("l0_v").sem, sig("l0_v").at(i + 1))
                    act.activation(cg[:, 0:CW], PA[:, 0:CW], ACT.Identity, bias=B(B_2)).then_inc(sig("l0_yv").sem, 1)
                load_rows(0)
                load_attributes(0)
                chunks(act, EI, layer0)

                def store_x1(i, before):
                    ln_square(act, i, False, PC, cc)
                    if before:
                        put_done(act, i - 1)
                    ln_deviation(act, i, False)
                    put(act, i, edge_rows_of(x1_rows, i), rows_view(rows_o, TW, False))
                store_x1(0, False)
                with act.Fori(1, EI) as i:
                    store_x1(i, True)
                put_done(act, EI - 1)

            @block.tensor
            def _(pe):
                with pe.Fori(0, EI) as i:
                    pe.wait_ge(sig("d_l0").sem, sig("d_l0").at((i + 1) * 48))
                    to_columns(pe, PA, rows, False)
                    to_columns(pe, PB, rows_b, False).then_inc(sig("l0_cols").sem, 1)
                    pe.wait_ge(sig("l0_s").sem, sig("l0_s").at(i + 1))
                    pe.wait_ge(sig("l0_d").sem, sig("l0_d").at(i + 1))
                    for pair, ps in enumerate((PC, PD)):
                        for half in range(2):
                            o, xs = halves(ps, ca, False)[half]
                            xd, ea = halves(ps, cb, False)[half][1], halves(ps, ce, False)[half][1]
                            pe.matmul(o, W(L0S + pair), xs, start=True, stop=False)
                            pe.matmul(o, W(L0D + pair), xd, start=False, stop=False)
                            ins = pe.matmul(o, W(L0E + pair, Q * EC), ea[0:Q * EC, :], start=False, stop=True)
                    ins.then_inc(sig("l0_h").sem, 1)
                    pe.wait_ge(sig("l0_hl").sem, sig("l0_hl").at(i + 1))
                    for half in range(2):
                        o, ha = halves(PA, rows_o, False)[half]
                        pe.matmul(o, W(L0V), ha, start=True, stop=False)
                        ins = pe.matmul(o, W(L0V + 1), halves(PA, cf, False)[half][1], start=False, stop=True)
                    ins.then_inc(sig("l0_v").sem, 1)
                    pe.wait_ge(sig("l0_yv").sem, sig("l0_yv").at(i + 1))
                with pe.Fori(0, EI) as i:
                    pe.wait_ge(sig("y_ready").sem, sig("y_ready").at(i + 1))
                    pe.wait_ge(sig("rows_ready").sem, sig("rows_ready").at(i))
                    to_rows(pe, PC, cf, False, centred=True).then_inc(sig("out_rows").sem, 1)

            @block.vector
            def _(dve):
                with dve.Fori(0, EI) as i:
                    dve.wait_ge(sig("l0_cols").sem, sig("l0_cols").at(i + 1))
                    dve.tensor_copy(cb[:, 0:CW], PB[:, 0:CW]).then_inc(sig("l0_d").sem, 1)
                    dve.tensor_copy(cols(arr_d, i), PB[:, 0:CW])
                    dve.wait_ge(sig("l0_y").sem, sig("l0_y").at(i + 1))
                    dve.scalar_tensor_tensor(rows_o[:, 0:CW], cc[:, 0:CW], 0.01, cc[:, 0:CW], ALU.mult, ALU.max)
                    dve.scalar_tensor_tensor(cf[:, 0:CW], cd[:, 0:CW], 0.01, cd[:, 0:CW], ALU.mult, ALU.max)\
                       .then_inc(sig("l0_hl").sem, 1)
                    dve.wait_ge(sig("l0_yv").sem, sig("l0_yv").at(i + 1))
                    dve.scalar_tensor_tensor(cols(arr_m, i), cg[:, 0:CW], 0.01, cg[:, 0:CW], ALU.mult, ALU.max)\
                       .then_inc(sig("l0_done").sem, 1)
                dve.wait_ge(sig("l0_done").sem, sig("l0_done").at(EI))
                link(dve, dve.memset(rows_o[:, :], FAR))
                maximum_x1(dve)
                with dve.Fori(0, EI) as i:
                    dve.tensor_tensor(cb[:, 0:CW], cols(arr_m, i), cols(arr_d, i), ALU.max).then_inc(sig("x1_max").sem, 1)
                    dve.wait_ge(sig("x1_max").sem, sig("x1_max").at(i + 1))
                    dve.tensor_tensor(cf[:, 0:CW], cb[:, 0:CW], cols(arr_d, i), ALU.add).then_inc(sig("y_ready").sem, 1)
                    ln_dve(dve, i, TW, False)
                link(dve, dve.tensor_copy(idx_a[:, :], last_f[:, :]))
        advance("d_l0", 48 * EI)
        for name in ("l0_cols", "l0_s", "l0_d", "l0_h", "l0_y", "l0_hl", "l0_v", "l0_yv", "l0_done", "x1_max", "y_ready"):
            advance(name, EI)
        stream_advance(EI, False, True)
        ln_advance(EI)

        put_x1 = RingPass(idx_a, table, TW, N - 1, scatter=True, load_from=x1_rows)
        with nc.Block() as block:
            @block.gpsimd
            def _(pool):
                put_x1.pool(pool)

            @block.sync
            def _(sp):
                put_x1.sp(sp)

            @block.scalar
            def _(act):
                act.dma_start(arr_s[:, 0:T * RW], edges1.rearrange("(p u) w -> p (u w)", p=P)).then_inc(sig("d_const").sem, 16)

            @block.tensor
            def _(pe):
                rank_pe(pe, HIGH)

            @block.vector
            def _(dve):
                dve.wait_ge(sig("d_const").sem, sig("d_const").at(16))
                link(dve, dve.tensor_copy(src_i[:, :], arr_s[:, 0:T * RW].rearrange("p (t w) -> p t w", w=RW)[:, :, 0]))
                link(dve, dve.tensor_scalar(tmp_i[:, :], src_i[:, :], LOW.bit_length() - 1, None, ALU.arith_shift_right))
                link(dve, dve.tensor_copy(digit[:, :].rearrange("p (c j) -> p c j", c=Q), by_tile(tmp_i)))
                rank_dve(dve, HIGH)
                rank_to_row(dve, idx_c)
        advance("d_const", 16)
        rank_advance()

        x_next, squared, summed, packed_rows = (arr_d[:, NC * D * m:NC * D * (m + 1)] for m in range(4))

        def with_neighbours(eng, n, body):
            body(0, False, True)
            if n > 2:
                with eng.Fori(1, n - 1) as i:
                    body(i, True, True)
            body(n - 1, True, False)

        def dense_pe(pe, first, n):
            def columns(i):
                pe.wait_ge(sig("packed").sem, sig("packed").at(i + 1))
                pe.wait_ge(sig("rows_ready").sem, sig("rows_ready").at(i - 1))
                to_columns(pe, PD, packed_rows, True).then_inc(sig("in_cols").sem, 1)

            def centred_rows(i):
                pe.wait_ge(sig("y_ready").sem, sig("y_ready").at(i + 1))
                to_rows(pe, PD, summed, True, centred=True).then_inc(sig("out_rows").sem, 1)

            def body(i, before, after):
                for t in range(STEPS):
                    def state_ready(half):
                        if t:
                            m = (i * STEPS + t - 1) * 2 + half
                            pe.wait_ge(sig("h_new").sem, sig("h_new").at(m + 1))
                        elif half == 0:
                            pe.wait_ge(sig("x_cols").sem, sig("x_cols").at(i + 1))
                            pe.wait_ge(sig("h_new").sem, sig("h_new").at(i * (2 * STEPS)))
                    gru_pe(pe, i * STEPS + t, lambda half: half_of(cf if t else x_next, half, True), None, True,
                           state_ready)
                    if t == 0 and before:
                        centred_rows(i - 1)
                    if t == 2 and after:
                        columns(i + 1)
            pe.wait_ge(sig("packed").sem, sig("packed").at(1))
            to_columns(pe, PD, packed_rows, True).then_inc(sig("in_cols").sem, 1)
            with_neighbours(pe, n, body)
            centred_rows(n - 1)

        def dense_act(act, first, n, width=TW):
            def load(i):
                act.dma_start(rows_view(rows, width, True), x_nodes(table, i + first)[:, :, 0:width])\
                   .then_inc(sig("d_in").sem, 16)

            def load_next(i):
                act.wait_ge(sig("packed").sem, sig("packed").at(i))
                load(i)

            def pack(i):
                act.wait_ge(sig("d_in").sem, sig("d_in").at((i + 1) * 16))
                act.wait_ge(sig("in_cols").sem, sig("in_cols").at(i))
                act.activation(rows_view(packed_rows, D, True), rows_view(rows, width, True)[:, :, 0:D], ACT.Copy)\
                   .then_inc(sig("packed").sem, 1)

            def columns(i):
                act.wait_ge(sig("in_cols").sem, sig("in_cols").at(i + 1))
                act.wait_ge(sig("x_kept").sem, sig("x_kept").at(i))
                act.activation(bv(x_next, True), pv(PD, True), ACT.Copy).then_inc(sig("x_cols").sem, 1)

            def keep(i):
                act.wait_ge(sig("x_cols").sem, sig("x_cols").at(i + 1))
                act.wait_ge(sig("y_ready").sem, sig("y_ready").at(i))
                act.activation(bv(cg, True), bv(x_next, True), ACT.Copy).then_inc(sig("x_kept").sem, 1)

            def body(i, before, after):
                gru_act(act, i * STEPS, True, lambda: keep(i))
                if before:
                    ln_square(act, i - 1, True, PD, squared)
                gru_act(act, i * STEPS + 1, True)
                if before:
                    ln_deviation(act, i - 1, True)
                if after:
                    pack(i + 1)
                gru_act(act, i * STEPS + 2, True)
                if before:
                    put(act, i - 1, x_nodes(out, i - 1 + first), rows_view(rows_o, D, True))
                gru_act(act, i * STEPS + 3, True, lambda: columns(i + 1) if after else None)
                if before:
                    put_done(act, i - 1)

            def loading(i, before, after):
                body(i, before, after)
                load_next(i + 2)

            load(0)
            pack(0)
            load_next(1)
            columns(0)
            if n > 2:
                loading(0, False, True)
                if n > 3:
                    with act.Fori(1, n - 2) as i:
                        loading(i, True, True)
                body(n - 2, True, True)
            else:
                body(0, False, True)
            body(n - 1, True, False)
            ln_square(act, n - 1, True, PD, squared)
            ln_deviation(act, n - 1, True)
            act_store(act, n - 1, x_nodes(out, n - 1 + first), rows_view(rows_o, D, True))

        def dense_dve(dve, first, n):
            def body(i, before, after):
                for t in range(STEPS):
                    gru_dve(dve, i * STEPS + t, lambda half: half_of(cf if t else x_next, half, True), False, True)
                    if t == 0 and before:
                        ln_sums(dve, i - 1, True, PD, squared)
                    if t == 1 and before:
                        ln_scale(dve, i - 1, D, True, PD, squared)
                dve.wait_ge(sig("h_new").sem, sig("h_new").at(i * (2 * STEPS) + 2 * STEPS))
                dve.wait_ge(sig("x_kept").sem, sig("x_kept").at(i + 1))
                dve.wait_ge(sig("out_rows").sem, sig("out_rows").at(i))
                dve.tensor_tensor(bv(summed, True), bv(cf, True), bv(cg, True), ALU.add).then_inc(sig("y_ready").sem, 1)
            with_neighbours(dve, n, body)
            ln_sums(dve, n - 1, True, PD, squared)
            ln_scale(dve, n - 1, D, True, PD, squared)

        def dense_advance(n):
            stream_advance(n, True, True)
            for name in ("x_cols", "x_kept", "packed", "y_ready"):
                advance(name, n)
            gru_advance(n * STEPS, False)
            ln_advance(n)

        def beside_dense(ring_pass, first, n):
            with nc.Block() as block:
                @block.gpsimd
                def _(pool):
                    ring_pass.pool(pool)

                @block.sync
                def _(sp):
                    ring_pass.sp(sp)

                @block.tensor
                def _(pe):
                    dense_pe(pe, first, n)

                @block.scalar
                def _(act):
                    dense_act(act, first, n)

                @block.vector
                def _(dve):
                    dense_dve(dve, first, n)
            dense_advance(n)

        sort_high = RingPass(idx_c, edges2, RW, EP - 1, scatter=True, load_from=edges1.rearrange("(p u) w -> p u w", p=P))
        beside_dense(sort_high, 0, SPLIT[0])

        sorted_rows = arr_s[:, 0:T * RW].rearrange("p (t w) -> p t w", w=RW)
        with nc.Block() as block:
            @block.sync
            def _(sp):
                sp.dma_start(arr_s[:, 0:T * RW], edges2.rearrange("(p u) w -> p (u w)", p=P)).then_inc(sig("d_const").sem, 16)

            @block.tensor
            def _(pe):
                masks_pe(pe)

            @block.vector
            def _(dve):
                dve.wait_ge(sig("d_const").sem, sig("d_const").at(16))
                link(dve, dve.tensor_copy(key_f[:, :], sorted_rows[:, :, 0]))
                link(dve, dve.tensor_copy(dst_f[:, :], sorted_rows[:, :, 1]))
                link(dve, dve.tensor_scalar(tmp_f[:, :], key_f[:, :], float(N - 1), None, ALU.min))
                link(dve, dve.tensor_copy(idx_a[:, :], tmp_f[:, :]))
                link(dve, dve.tensor_scalar(tmp_f[:, :], dst_f[:, :], float(N - 1), None, ALU.min))
                link(dve, dve.tensor_copy(idx_b[:, :], tmp_f[:, :]))
                masks_dve(dve)
                link(dve, dve.tensor_copy(idx_c[:, :], last_f[:, :]))
                link(dve, dve.tensor_scalar(tmp_f[:, :], last_f[:, :], float(TW), float(D), ALU.mult, ALU.add))
                link(dve, dve.tensor_copy(tmp_i[:, :], tmp_f[:, :]))
        advance("d_const", 16)
        masks_advance()

        put_slots = RingPass(tmp_i, table_words, 1, N * TW - 1, scatter=True, load_from=slots[:, :].unsqueeze(2))
        with nc.Block() as block:
            @block.gpsimd
            def _(pool):
                put_slots.pool(pool)

            @block.sync
            def _(sp):
                put_slots.sp(sp)

            @block.tensor
            def _(pe):
                with pe.Fori(0, EI) as i:
                    pe.wait_ge(sig("ea_rows").sem, sig("ea_rows").at(i + 1))
                    waited(pe)
                    for j in range(JC):
                        ins = pe.transpose(PA[0:Q * EC, j * P:(j + 1) * P], ca[:, j * Q * EC:(j + 1) * Q * EC], W(IDENT))
                    ins.then_inc(sig("ea_cols").sem, 1)
                pe.wait_ge(sig("split").sem, sig("split").at((5 + PARTS * Q // 2) * EI))
                dense_pe(pe, SPLIT[0], SPLIT[1])

            @block.scalar
            def _(act):
                act.wait_ge(sig("split").sem, sig("split").at((5 + PARTS * Q // 2) * EI))
                dense_act(act, SPLIT[0], SPLIT[1], D)

            @block.vector
            def _(dve):
                half = slice(0, Q * EC)
                parts = [buf[half, 0:CW // 2].bitcast(BF16) for buf in (cd, ce, cf)]
                n = 5 + PARTS * Q // 2
                with dve.Fori(0, EI) as i:
                    def step(k, ins):
                        ins.then_inc(sig("split").sem, 1)
                        dve.wait_ge(sig("split").sem, sig("split").at(i * n + (k + 1)))
                    dve.wait_ge(sig("ea_cols").sem, sig("ea_cols").at(i))
                    waited(dve)
                    dve.tensor_copy(ca[:, 0:UC * EC].rearrange("p (u k) -> p u k", k=EC),
                                    sorted_rows[:, bass.ds(i * UC, UC), 2:2 + EC]).then_inc(sig("ea_rows").sem, 1)
                    dve.wait_ge(sig("ea_cols").sem, sig("ea_cols").at(i + 1))
                    step(0, dve.tensor_copy(parts[0], PA[half, 0:CW]))
                    step(1, dve.tensor_tensor(cb[half, 0:CW], PA[half, 0:CW], parts[0], ALU.subtract))
                    step(2, dve.tensor_copy(parts[1], cb[half, 0:CW]))
                    step(3, dve.tensor_tensor(cc[half, 0:CW], cb[half, 0:CW], parts[1], ALU.subtract))
                    step(4, dve.tensor_copy(parts[2], cc[half, 0:CW]))
                    for m, part in enumerate(parts):
                        for pair in range(Q // 2):
                            waited(dve)
                            step(5 + m * 2 + pair, dve.tensor_copy(
                                ea_pair[pair][m * 2 * EC:(m + 1) * 2 * EC, bass.ds(i * CW, CW)],
                                part[pair * 2 * EC:(pair + 1) * 2 * EC, :]))
                dense_dve(dve, SPLIT[0], SPLIT[1])
        advance("ea_rows", EI)
        advance("ea_cols", EI)
        advance("split", (5 + PARTS * Q // 2) * EI)
        dense_advance(SPLIT[1])

        g_nbr = RingPass(idx_b, table, TW, N - 1, store=back_with_slot(dst_rows), stored=2)
        beside_dense(g_nbr, SPLIT[0] + SPLIT[1], SPLIT[2])
        g_own = RingPass(idx_a, table, TW, N - 1, store=back(src_rows, TW), stored=1)
        beside_dense(g_own, SPLIT[0] + SPLIT[1] + SPLIT[2], SPLIT[3])

        KG = P // D
        GROUPS = EC // KG
        SN = GROUPS * Q
        repeated = [arr_d[:, CW * q:CW * (q + 1)] for q in range(Q)]
        products = [arr_d[:, CW * m:CW * (m + 1)] for m in range(Q, JC)] + [buf[:, 0:CW] for buf in (ca, cb, cc, cd, ce)]
        BANKS = ((0, 512), (512, CW))

        def messages_act(act, neighbours, gathered, own):
            def load_own(i):
                act.dma_start(rows_view(rows_b, D, False), edge_rows_of(src_rows, i)).then_inc(sig("d_l0").sem, 16)

            def load(i):
                gathered(i)
                act.dma_start(rows_view(rows, D, False), edge_rows_of(neighbours, i)).then_inc(sig("d_in").sem, 16)

            def save(i):
                act.wait_ge(sig("z_used").sem, sig("z_used").at((i + 1) * GROUPS))
                waited(act)
                act.activation(cols(arr_m, i), PD[:, 0:CW], ACT.Copy).then_inc(sig("msg_saved").sem, 1)

            def body(i, saving, more):
                act.wait_ge(sig("in_cols").sem, sig("in_cols").at(i + 1))
                act.activation(cg[:, 0:CW], PA[:, 0:CW], ACT.Copy).then_inc(sig("hd_ready").sem, 1)
                for q in range(Q):
                    act.wait_ge(sig("z_ready").sem, sig("z_ready").at(i * SN + max(q - Q + 1, -2)))
                    for h, (a, b) in enumerate(BANKS):
                        act.wait_ge(sig("repeat_cols").sem, sig("repeat_cols").at(i * (2 * Q) + (2 * q + h + 1)))
                        act.activation(repeated[q][:, a:b], PA[:, a:b], ACT.Copy).then_inc(sig("repeated").sem, 1)
                if saving:
                    save(i - 1)
                if more:
                    load(i + 1)
                if own:
                    act.wait_ge(sig("own_cols").sem, sig("own_cols").at(i + 1))
                    if more:
                        load_own(i + 1)
                    waited(act)
                    act.activation(cols(arr_s, i), PA[:, 0:CW], ACT.Copy).then_inc(sig("x_cols").sem, 1)
            load(0)
            if own:
                load_own(0)
            with_neighbours(act, EI, body)
            save(EI - 1)

        def messages_pe(pe, own):
            def attributes(i, s):
                ps = (PB, PC)[s % 2]
                m = s // Q * 2 + s % 2
                for a, b in BANKS:
                    ins = pe.matmul(ps[:, a:b], sel[:, m * P:(m + 1) * P],
                                    ea_pair[s % Q // 2][:, bass.ds(i * CW + a, b - a)], start=True, stop=True)
                ins.then_inc(sig("sel_cols").sem, 1)

            def neighbours(i):
                pe.wait_ge(sig("d_in").sem, sig("d_in").at((i + 1) * 16))
                pe.wait_ge(sig("repeated").sem, sig("repeated").at(i * (2 * Q)))
                to_columns(pe, PA, rows, False).then_inc(sig("in_cols").sem, 1)

            def repeat(i, q):
                if q == 0:
                    pe.wait_ge(sig("hd_ready").sem, sig("hd_ready").at(i + 1))
                for h, (a, b) in enumerate(BANKS):
                    pe.wait_ge(sig("repeated").sem, sig("repeated").at(i * (2 * Q) + (2 * q + h - 1)))
                    pe.matmul(PA[:, a:b], W(REPEAT + q), cg[:, a:b], start=True, stop=True)\
                      .then_inc(sig("repeat_cols").sem, 1)

            def group(i, g):
                for a, b in BANKS:
                    for q in range(Q):
                        ins = pe.matmul(PD[q * D:(q + 1) * D, a:b], W(BOND)[:, g * D:(g + 1) * D],
                                        products[g % 2 * Q + q][:, a:b], start=False, stop=(g == GROUPS - 1),
                                        tile_position=(0, q * D), skip_group_check=True)
                ins.then_inc(sig("z_used").sem, 1)

            def body(i, more):
                for s in range(SN):
                    pe.wait_ge(sig("z_ready").sem, sig("z_ready").at(i * SN + s + 1))
                    if s + 2 < SN:
                        attributes(i, s + 2)
                    elif more:
                        attributes(i + 1, s + 2 - SN)
                    if s == Q + 1 and own:
                        pe.wait_ge(sig("repeated").sem, sig("repeated").at((i + 1) * (2 * Q)))
                        pe.wait_ge(sig("d_l0").sem, sig("d_l0").at((i + 1) * 16))
                        to_columns(pe, PA, rows_b, False).then_inc(sig("own_cols").sem, 1)
                    if s == SN - 6 and more:
                        if own:
                            pe.wait_ge(sig("x_cols").sem, sig("x_cols").at(i + 1))
                        neighbours(i + 1)
                    if s == Q - 1:
                        pe.wait_ge(sig("msg_saved").sem, sig("msg_saved").at(i))
                        for a, b in BANKS:
                            pe.matmul(PD[:, a:b], W(BOND_B), cg[:, a:b], start=True, stop=False, skip_group_check=True)
                    if s % Q == Q - 1:
                        group(i, s // Q)
                    if s >= SN - Q and more:
                        repeat(i + 1, s - (SN - Q))
            neighbours(0)
            attributes(0, 0)
            attributes(0, 1)
            for q in range(Q):
                repeat(0, q)
            chunks(pe, EI, body)

        def messages_dve(dve):
            with dve.Fori(0, EI) as i:
                for s in range(SN):
                    g, q = s // Q, s % Q
                    if g == 0:
                        dve.wait_ge(sig("repeated").sem, sig("repeated").at(i * (2 * Q) + (2 * q + 2)))
                    if q == 0:
                        dve.wait_ge(sig("z_used").sem, sig("z_used").at(i * GROUPS + g - 1))
                    dve.wait_ge(sig("sel_cols").sem, sig("sel_cols").at(i * SN + s + 1))
                    dve.tensor_tensor(products[g % 2 * Q + q], (PB, PC)[s % 2][:, 0:CW], repeated[q],
                                      ALU.mult).then_inc(sig("z_ready").sem, 1)
            dve.wait_ge(sig("msg_saved").sem, sig("msg_saved").at(EI))
            link(dve, dve.tensor_tensor_scan(arr_m[:, 0:QE], same[:, :], arr_m[:, 0:QE], 0.0, ALU.mult, ALU.add))
            carry_over(dve, arr_m, (ALU.mult, ALU.add), 0.0, prefix)

        def messages_advance():
            stream_advance(EI, True, False)
            for name, n in (("hd_ready", 1), ("sel_cols", SN), ("z_ready", SN), ("z_used", GROUPS), ("msg_saved", 1),
                            ("repeat_cols", 2 * Q), ("repeated", 2 * Q)):
                advance(name, n * EI)

        alone = (cf, ce, arr_d[:, 0:CW])

        with nc.Block() as block:
            @block.sync
            def _(sp):
                with sp.Fori(0, EI) as i:
                    for t in range(STEPS - 1):
                        m = i * (STEPS - 1) + t
                        put(sp, m, edge_rows_of(alone_rows[t], i), rows_view(rows_o, D, False))
                        put_done(sp, m)

            @block.tensor
            def _(pe):
                def state_rows_of(m, t):
                    pe.wait_ge(sig("h_new").sem, sig("h_new").at(m * 2 + 2))
                    pe.wait_ge(sig("rows_ready").sem, sig("rows_ready").at(m))
                    to_rows(pe, PD, alone[t], False).then_inc(sig("out_rows").sem, 1)

                def body(i, before, after):
                    pe.wait_ge(sig("d_in").sem, sig("d_in").at((i + 1) * 16))
                    pe.wait_ge(sig("h_new").sem, sig("h_new").at(i * 2 * (STEPS - 1)))
                    to_columns(pe, PA, rows, False).then_inc(sig("in_cols").sem, 1)
                    for t in range(STEPS - 1):
                        m = i * (STEPS - 1) + t

                        def state_ready(half):
                            if t:
                                pe.wait_ge(sig("h_new").sem, sig("h_new").at(m * 2 + half - 1))
                            elif half == 0:
                                pe.wait_ge(sig("x_cols").sem, sig("x_cols").at(i + 1))
                        gru_pe(pe, m, lambda half: half_of(alone[t - 1] if t else cg, half, False), None, False,
                               state_ready)
                        if t or before:
                            state_rows_of(m - 1, (t - 1) % (STEPS - 1))
                with_neighbours(pe, EI, body)
                state_rows_of(EI * (STEPS - 1) - 1, STEPS - 2)

            @block.scalar
            def _(act):
                def load(i):
                    act.dma_start(rows_view(rows, D, False), edge_rows_of(dst_rows, i)).then_inc(sig("d_in").sem, 16)

                def body(i, before, more):
                    act.wait_ge(sig("in_cols").sem, sig("in_cols").at(i + 1))
                    if more:
                        load(i + 1)
                    act.activation(cg[:, 0:CW], PA[:, 0:CW], ACT.Copy).then_inc(sig("x_cols").sem, 1)
                    for t in range(STEPS - 1):
                        m = i * (STEPS - 1) + t
                        gru_act(act, m, False)
                        if t or before:
                            rows_out(act, m - 1, PD, D, False)
                load(0)
                with_neighbours(act, EI, body)
                rows_out(act, EI * (STEPS - 1) - 1, PD, D, False)

            @block.vector
            def _(dve):
                link(dve, dve.tensor_copy(idx_b[:, :], slot_f[:, :]))
                with dve.Fori(0, EI) as i:
                    for t in range(STEPS - 1):
                        m = i * (STEPS - 1) + t

                        def state_read():
                            dve.wait_ge(sig("out_rows").sem, sig("out_rows").at(m - 1))
                        gru_dve(dve, m, lambda half: half_of(alone[t - 1] if t else cg, half, False), False, False,
                                state_read, alone[t])
        stream_advance(EI, True, False)
        stream_advance(EI * (STEPS - 1), False, True)
        advance("x_cols", EI)
        gru_advance(EI * (STEPS - 1), False)

        for step in range(STEPS):
            final = step == STEPS - 1
            g_state = RingPass(idx_b, state, D, EP - 1, load_from=alone_rows[step - 1], store=back(nbr_rows), stored=1) \
                if step else None
            with nc.Block() as block:
                if step:
                    @block.gpsimd
                    def _(pool):
                        g_state.pool(pool)

                    @block.sync
                    def _(sp):
                        g_state.sp(sp)

                @block.scalar
                def _(act):
                    def gathered(i):
                        if step:
                            for h in range(2):
                                act.wait_ge(sig(f"d_stored{h}").sem, (i + 1) * 16 + g_state.base[f"d_stored{h}"])
                    messages_act(act, nbr_rows if step else dst_rows, gathered, step == 0)

                @block.tensor
                def _(pe):
                    messages_pe(pe, step == 0)

                @block.vector
                def _(dve):
                    messages_dve(dve)
            messages_advance()

            if step == 0:
                for name, n in (("d_l0", 16), ("own_cols", 1), ("x_cols", 1)):
                    advance(name, n * EI)

            with nc.Block() as block:
                if final:
                    put_out = RingPass(idx_c, out, D, N - 1, scatter=True, load_from=final_rows,
                                       rows_there=lambda sp, turn: sp.wait_ge(sig("d_out").sem,
                                                                              sig("d_out").at((turn + 1) * 16)))

                    @block.gpsimd
                    def _(pool):
                        put_out.pool(pool)

                @block.sync
                def _(sp):
                    if final:
                        put_out.sp(sp)
                    else:
                        stream_sp(sp, EI, None, lambda sp, i: sp.dma_start(edge_rows_of(state_rows, i),
                                                                           rows_view(rows_o, D, False)))

                LAST_BANKS = ((PC[:, 512:1024], 0, 512), (PD[:, 512:CW], 512, CW))
                total, total_squared, centred = (arr_d[:, NC * D * m:NC * D * (m + 1)] for m in range(3))

                def with_before(eng, body):
                    body(0, False)
                    with eng.Fori(1, EI) as i:
                        body(i, True)

                @block.scalar
                def _(act):
                    def save_state(i, half):
                        act.wait_ge(sig("h_new").sem, sig("h_new").at(i * 2 + half + 1))
                        waited(act)
                        act.activation(arr_s[:, bass.ds(i * CW + 512 * half, (512, CW - 512)[half])],
                                       half_of(cf, half, False), ACT.Copy).then_inc(sig("h_saved").sem, 1)

                    def load(i):
                        act.dma_start(rows_view(rows, D, False), edge_rows_of(src_rows, i)).then_inc(sig("d_in").sem, 16)

                    def rows_before(i, more):
                        act.wait_ge(sig("out_rows").sem, sig("out_rows").at(i + 1))
                        if final:
                            if more:
                                load(i + 1)
                            act.wait_ge(sig("rows_ready").sem, sig("rows_ready").at(i))
                            for ps, a, b in LAST_BANKS:
                                ins = act.activation(centred[:, a:b], ps, ACT.Copy)
                            ins.then_inc(sig("x_kept").sem, 1)
                            act.wait_ge(sig("x_kept").sem, sig("x_kept").at(i + 1))
                            act.activation(total_squared[:, 0:CW], centred[:, 0:CW], ACT.Square)\
                               .then_inc(sig("ln_squared").sem, 1)
                        else:
                            act.wait_ge(sig("stored").sem, sig("stored").at(i))
                            for ps, a, b in LAST_BANKS:
                                ins = act.activation(rows_o[:, a:b], ps, ACT.Copy)
                            ins.then_inc(sig("rows_ready").sem, 1)

                    def body(i, before):
                        def before_tanh(half):
                            if half:
                                save_state(i, 0)
                            elif before:
                                save_state(i - 1, 1)
                        gru_act(act, i, False, lambda: rows_before(i - 1, True) if before else None,
                                before_tanh if not final else lambda half: None)
                        if final and before:
                            ln_deviation(act, i - 1, False)
                            put(act, i - 1, edge_rows_of(final_rows, i - 1), rows_view(rows_o, D, False))
                    if final:
                        load(0)
                    with_before(act, body)
                    if not final:
                        save_state(EI - 1, 1)
                    rows_before(EI - 1, False)
                    if final:
                        ln_deviation(act, EI - 1, False)
                        put(act, EI - 1, edge_rows_of(final_rows, EI - 1), rows_view(rows_o, D, False))

                @block.tensor
                def _(pe):
                    def half_cols(a, i):
                        return lambda half: a[:, bass.ds(i * CW + 512 * half, (512, CW - 512)[half])]

                    def rows_before(i):
                        def each(product):
                            for g in range(JC):
                                ins = product((PC, PD)[g // Q][:, 512 + g % Q * P:512 + (g % Q + 1) * P], g * P)
                            return ins
                        pe.wait_ge(sig("h_new").sem, sig("h_new").at(i * 2 + 2))
                        if final:
                            pe.wait_ge(sig("d_in").sem, sig("d_in").at((i + 1) * 16))
                            each(lambda o, c: pe.transpose(o, rows[:, c:c + P], W(IDENT))).then_inc(sig("in_cols").sem, 1)
                            pe.wait_ge(sig("y_ready").sem, sig("y_ready").at(i + 1))
                            each(lambda o, c: pe.matmul(o, total[:, c:c + P], W(CENTRE), start=True, stop=True))\
                                .then_inc(sig("out_rows").sem, 1)
                        else:
                            each(lambda o, c: pe.transpose(o, cf[:, c:c + P], W(IDENT))).then_inc(sig("out_rows").sem, 1)

                    def body(i, before):
                        def banks_free(half):
                            if half == 0:
                                pe.wait_ge(sig("h_new").sem, sig("h_new").at(i * 2 - 1))
                            elif before:
                                rows_before(i - 1)

                        def rows_read(half):
                            if half:
                                name = "x_kept" if final else "rows_ready"
                                pe.wait_ge(sig(name).sem, sig(name).at(i))
                        gru_pe(pe, i, half_cols(arr_s, i), half_cols(arr_m, i), False, banks_free, rows_read)
                    with_before(pe, body)
                    rows_before(EI - 1)

                @block.vector
                def _(dve):
                    def add_x1(i):
                        dve.wait_ge(sig("h_new").sem, sig("h_new").at(i * 2 + 2))
                        dve.wait_ge(sig("in_cols").sem, sig("in_cols").at(i + 1))
                        dve.wait_ge(sig("out_rows").sem, sig("out_rows").at(i))
                        for ps, a, b in LAST_BANKS:
                            ins = dve.tensor_tensor(total[:, a:b], cf[:, a:b], ps, ALU.add)
                        ins.then_inc(sig("y_ready").sem, 1)
                        dve.wait_ge(sig("y_ready").sem, sig("y_ready").at(i + 1))

                    def norm(i):
                        ln_sums(dve, i, False, centred, total_squared)
                        ln_scale(dve, i, D, False, centred, total_squared, direct=True)

                    def body(i, before):
                        def state_read():
                            if final:
                                if before:
                                    add_x1(i - 1)
                            else:
                                dve.wait_ge(sig("out_rows").sem, sig("out_rows").at(i))
                                dve.wait_ge(sig("h_saved").sem, sig("h_saved").at(i * 2))
                        gru_dve(dve, i, lambda half: arr_s[:, bass.ds(i * CW + 512 * half, (512, CW - 512)[half])],
                                True, False, state_read)
                        if final and before:
                            norm(i - 1)
                    with_before(dve, body)
                    if final:
                        add_x1(EI - 1)
                        norm(EI - 1)
            stream_advance(EI, final, True)
            gru_advance(EI, True)
            if final:
                advance("y_ready", EI)
                advance("x_kept", EI)
                ln_advance(EI)
            else:
                advance("h_saved", 2 * EI)


def kernel(**inputs):
    import concourse.bacc as _bacc
    import ml_dtypes
    from concourse.bass_utils import run_bass_kernel_spmd as _run

    def get(name):
        return np.asarray(inputs[name])

    def by_slot(a, fill):
        full = np.full((EP,) + a.shape[1:], fill, a.dtype)
        full[:E] = a
        full = full.reshape((Q, J, P) + a.shape[1:])
        return np.ascontiguousarray(np.moveaxis(full, 2, 0).swapaxes(1, 2)).reshape((P, T) + a.shape[1:])

    ea = get("edge_attr_16")
    ea_t = np.zeros((EP, EC), np.float32)
    ea_t[:E] = ea
    ea_t = np.ascontiguousarray(ea_t.reshape(Q, QE, EC).transpose(0, 2, 1)).reshape(Q * EC, QE)

    w = np.zeros((P, NW, P), np.float32)
    w_ih, w_hh = get("L1_gnn_W_ih"), get("L1_gnn_W_hh")
    w_bond, b_bond = get("L1_gnn_W_bond").reshape(EC, D, D), get("L1_gnn_b_bond").reshape(D, D)
    w1, w2 = get("L0_gnn_W1"), get("L0_gnn_W2")
    for c in range(Q):
        q = slice(c * D, c * D + D)
        for g in range(3):
            w[q, IH + g, q] = w_ih[g * D:(g + 1) * D].T
            w[q, HH + g, q] = w_hh[g * D:(g + 1) * D].T
        for g in range(EC // Q):
            w[q, BOND, g * D:(g + 1) * D] = w_bond[g * Q + c].T
        for c2 in range(P // D):
            w[q, REPEAT + c, c2 * D:(c2 + 1) * D] = np.eye(D)
        w[q, BOND_B, q] = b_bond.T
        pair, m = c // 2, slice((c % 2) * DM, (c % 2) * DM + DM)
        w[q, L0S + pair, m] = w1[0:D]
        w[q, L0D + pair, m] = w1[D:2 * D]
        w[c * EC:(c + 1) * EC, L0E + pair, m] = w1[2 * D:]
        w[m, L0V + pair, q] = w2
    w[:, IDENT] = np.eye(P)
    block_mean = np.kron(np.eye(Q), np.ones((D, D))) / D
    w[:, CENTRE] = np.eye(P) - block_mean
    w[:, ONES] = 1.0

    bias = np.zeros((P, NB), np.float32)
    b_ih, b_hh = get("L1_gnn_b_ih"), get("L1_gnn_b_hh")
    b1, b2 = get("L0_gnn_b1"), get("L0_gnn_b2")
    for c in range(Q):
        q = slice(c * D, c * D + D)
        bias[q, B_R], bias[q, B_Z], bias[q, B_IN] = b_ih[:D], b_ih[D:2 * D], b_ih[2 * D:]
        bias[q, B_RH], bias[q, B_ZH], bias[q, B_HN] = b_hh[:D], b_hh[D:2 * D], b_hh[2 * D:]
        bias[q, B_2] = b2
    for m in range(2):
        bias[m * DM:(m + 1) * DM, B_1A] = b1
        bias[m * DM:(m + 1) * DM, B_1B] = b1
    bias[:, B_EPS] = EPS

    sel = np.zeros((PARTS, 2, EC, EC // Q, 2, Q, D), np.float32)
    for k in range(EC):
        for c in range(2):
            sel[:, c, k, k // Q, c, k % Q, :] = 1.0
    arrays = {
        "x": np.ascontiguousarray(get("x")),
        "src_pu": by_slot(get("src"), N),
        "dst_pu": by_slot(get("dst"), N),
        "ea_pu": by_slot(ea, 0),
        "ea_t": ea_t,
        "weights": w.reshape(P, NW * P),
        "biases": bias,
        "sel_h": sel.reshape(PARTS * 2 * EC, 2 * EC // Q * P).astype(ml_dtypes.bfloat16),
        "triu_h": np.triu(np.ones((P, P), np.float32), 1).astype(ml_dtypes.bfloat16),
        "tril_h": np.tril(np.ones((P, P), np.float32)).astype(ml_dtypes.bfloat16),
        "iota_h": np.tile(np.arange(HIGH, dtype=np.float32), (P, 1)),
        "slot_h": np.arange(EP, dtype=np.float32).reshape(P, T),
    }
    nc = _bacc.Bacc("TRN2", target_bir_lowering=False, num_devices=1)
    aps = {n: nc.dram_tensor(n, a.shape, mybir.dt.from_np(a.dtype), kind="ExternalInput").ap() for n, a in arrays.items()}
    out = nc.dram_tensor("out", (N, D), F32, kind="ExternalOutput").ap()
    with nc.allow_non_contiguous_dma(reason="rows of edges and nodes"):
        bass_gnn_resnorm(nc, **aps, out=out)
    r = _run(nc, [arrays], core_ids=[0])
    return r.results[0]["out"]
```
